# Optimizing a Trainium2 kernel written in Bass

```python
import numpy as np
import jax
import jax.numpy as jnp

def _softmax(x, axis=-1):
    return jax.nn.softmax(x, axis=axis)

def _gelu(x):
    return jax.nn.gelu(x, approximate=True)

def _silu(x):
    return jax.nn.silu(x)

def _sigmoid(x):
    return jax.nn.sigmoid(x)

def _layernorm(x, axis=-1, eps=1e-05):
    m = jnp.mean(x, axis=axis, keepdims=True)
    v = jnp.var(x, axis=axis, keepdims=True)
    return (x - m) / jnp.sqrt(v + eps)

def _scatter_add(tgt, idx, src, axis=0):
    return tgt.at[idx].add(src)

def _segment_sum(src, seg, n):
    return jax.ops.segment_sum(src, seg, n)
kernel_name = 'mk_decoder_preln_d1_seqx_r4_ac3cd5'

def setup_inputs(seed: int=0):
    np.random.seed(seed)
    _w = jnp.asarray

    def _rec_inputs():
        import jax
        import jax.numpy as jnp
        _rk = jax.random.key(seed)
        x = -0.000125 + 0.9999 * jax.random.normal(jax.random.fold_in(_rk, 1), (4, 512, 512), jnp.float32)
        _lenS = 512 - jax.random.randint(jax.random.fold_in(_rk, 7), (4,), 0, max(1, 512 // 4) + 1, jnp.int32)
        _lenS2 = 512 - jax.random.randint(jax.random.fold_in(_rk, 8), (4,), 0, max(1, 512 // 4) + 1, jnp.int32)
        fside_BxS2xS2_0 = -3.05549e-07 + 0.0199987 * jax.random.normal(jax.random.fold_in(_rk, 11), (4, 512, 512), jnp.float32)
        _ctx_1024P = jax.random.normal(jax.random.fold_in(_rk, 12), (4, 16, 256), jnp.float32)
        _ctx_1024c = jax.random.dirichlet(jax.random.fold_in(_rk, 512), 0.3 * jnp.ones((16,), jnp.float32), (4, 512))
        _ctx_1024t = jnp.einsum('bsk,bkd->bsd', _ctx_1024c, _ctx_1024P)
        _ctx_1024t = _ctx_1024t * jax.lax.rsqrt(jnp.mean(jnp.square(_ctx_1024t)) + 1e-12) * 0.953939
        ctx_1024 = 6.82029e-06 + 0.0200006 * (_ctx_1024t + 0.3 * jax.random.normal(jax.random.fold_in(_rk, 612), (4, 512, 256), jnp.float32))
        return (x, fside_BxS2xS2_0, ctx_1024)
    x, fside_BxS2xS2_0, ctx_1024 = _rec_inputs()

    def _L0_attn_setup():
        import jax, jax.numpy as jnp
        import numpy as np
        B_, L_, D_MODEL = (2, 512, 512)
        EXPAND = 2
        D_IN = EXPAND * D_MODEL
        HEADS = 64
        HEAD_DIM = D_IN // HEADS
        STATE = 128
        NGROUPS = 1
        K = 4
        CONV_DIM = D_IN + 2 * NGROUPS * STATE
        PROJ = D_IN + CONV_DIM + HEADS
        CHUNK = 64
        EPS = 1e-05

        def _segsum(x):
            T = x.shape[-1]
            c = jnp.cumsum(x, axis=-1)
            seg = c[..., :, None] - c[..., None, :]
            return jnp.where(jnp.tril(jnp.ones((T, T), bool)), seg, -jnp.inf)

        def _ssd(x, dA, Bm, Cm):
            b, l, h, p = x.shape
            n = Bm.shape[-1]
            c = l // CHUNK
            rep = h // Bm.shape[2]
            Bh = jnp.repeat(Bm, rep, axis=2).reshape(b, c, CHUNK, h, n)
            Ch = jnp.repeat(Cm, rep, axis=2).reshape(b, c, CHUNK, h, n)
            x = x.reshape(b, c, CHUNK, h, p)
            dA = dA.reshape(b, c, CHUNK, h).transpose(0, 3, 1, 2)
            dA_cum = jnp.cumsum(dA, axis=-1)
            Lmat = jnp.exp(_segsum(dA))
            Y_diag = jnp.einsum('bcthn,bcshn,bhcts,bcshp->bcthp', Ch, Bh, Lmat, x)
            decay_states = jnp.exp(dA_cum[..., -1:] - dA_cum)
            states = jnp.einsum('bcshn,bhcs,bcshp->bchpn', Bh, decay_states, x)
            chunk_decay = jnp.exp(_segsum(jnp.pad(dA_cum[..., -1], ((0, 0), (0, 0), (1, 0)))))
            states = jnp.concatenate([jnp.zeros_like(states[:, :1]), states], axis=1)
            prev = jnp.einsum('bhzc,bchpn->bzhpn', chunk_decay, states)[:, :-1]
            Y_off = jnp.einsum('bcthn,bchpn,bhct->bcthp', Ch, prev, jnp.exp(dA_cum))
            return (Y_diag + Y_off).reshape(b, l, h, p)
        key = jax.random.key(seed)
        ks = jax.random.split(key, 4)
        return {'hidden_states': jax.random.normal(ks[0], (B_, L_, D_MODEL), jnp.float32), 'in_proj_w': jax.random.normal(ks[1], (PROJ, D_MODEL), jnp.float32) * 0.02, 'conv_w': jax.random.normal(ks[2], (CONV_DIM, K), jnp.float32) * 0.2, 'conv_b': jnp.zeros((CONV_DIM,), jnp.float32), 'dt_bias': jnp.ones((HEADS,), jnp.float32), 'A_log': jnp.log(jnp.arange(1, HEADS + 1, dtype=jnp.float32)), 'D': jnp.ones((HEADS,), jnp.float32), 'norm_w': jnp.ones((D_IN,), jnp.float32), 'out_proj_w': jax.random.normal(ks[3], (D_MODEL, D_IN), jnp.float32) * 0.02}
    _L0_attn_all = _L0_attn_setup()
    _L0_attn_in = {k: v for k, v in _L0_attn_all.items() if k in ('in_proj_w', 'conv_w', 'conv_b', 'dt_bias', 'A_log', 'D', 'norm_w', 'out_proj_w')}
    del _L0_attn_all

    def _L0_xattn_setup():
        import jax, jax.numpy as jnp
        import numpy as np
        EPS = 1e-06
        QMAX = 127.0

        def _smooth_quant_linear(x, w):
            amax_x = jnp.max(jnp.abs(x), axis=0)
            amax_w = jnp.max(jnp.abs(w), axis=0)
            s = jnp.sqrt(jnp.maximum(amax_x, EPS) / jnp.maximum(amax_w, EPS))
            s = jnp.maximum(s, EPS)
            xs = x / s
            ws = w * s
            x_scale = jnp.maximum(jnp.max(jnp.abs(xs), axis=-1, keepdims=True), EPS) / QMAX
            w_scale = jnp.maximum(jnp.max(jnp.abs(ws), axis=-1, keepdims=True), EPS) / QMAX
            x_q = jnp.clip(jnp.round(xs / x_scale), -QMAX, QMAX)
            w_q = jnp.clip(jnp.round(ws / w_scale), -QMAX, QMAX)
            return x_q @ w_q.T * x_scale * w_scale.T

        def _expert_forward(xe, guw, dw):
            h = _smooth_quant_linear(xe, guw)
            gate, up = jnp.split(h, 2, axis=-1)
            a = jax.nn.silu(gate) * up
            return _smooth_quant_linear(a, dw)
        key = jax.random.key(seed)
        k1, k2, k3 = jax.random.split(key, 3)
        E, T, D, I = (8, 512, 512, 256)
        x = jax.random.normal(k1, (E, T, D), dtype=jnp.float32)
        gate_up_weight = jax.random.normal(k2, (E, 2 * I, D), dtype=jnp.float32) * 0.02
        down_weight = jax.random.normal(k3, (E, D, I), dtype=jnp.float32) * 0.02
        return {'x': x, 'gate_up_weight': gate_up_weight, 'down_weight': down_weight}
    _L0_xattn_all = _L0_xattn_setup()
    _L0_xattn_in = {k: v for k, v in _L0_xattn_all.items() if k in ()}
    del _L0_xattn_all

    def _L0_ffn_setup():
        import jax, jax.numpy as jnp
        import numpy as np
        TOP_P = 0.9
        S, B, H, I, E = (512, 4, 512, 1024, 8)

        def _top_p_weights(probs, top_p):
            order = jnp.argsort(-probs, axis=-1)
            sp = jnp.take_along_axis(probs, order, axis=-1)
            cum = jnp.cumsum(sp, axis=-1)
            exceed = cum > top_p
            first_idx = jnp.argmax(exceed, axis=-1)
            first = jnp.arange(probs.shape[-1])[None, :] == first_idx[:, None]
            keep = ~exceed | first
            kept = jnp.where(keep, sp, 0.0)
            t_idx = jnp.arange(probs.shape[0])[:, None]
            return jnp.zeros_like(probs).at[t_idx, order].set(kept)
        key = jax.random.key(seed)
        ks = jax.random.split(key, 5)
        scale = 0.02
        return {'hidden_states': jax.random.normal(ks[0], (S, B, H), dtype=jnp.float32), 'router_w': jax.random.normal(ks[1], (E, H), dtype=jnp.float32) * scale, 'gate_w': jax.random.normal(ks[2], (E, I, H), dtype=jnp.float32) * scale, 'up_w': jax.random.normal(ks[3], (E, I, H), dtype=jnp.float32) * scale, 'down_w': jax.random.normal(ks[4], (E, H, I), dtype=jnp.float32) * scale}
    _L0_ffn_all = _L0_ffn_setup()
    _L0_ffn_in = {k: v for k, v in _L0_ffn_all.items() if k in ('router_w', 'gate_w', 'up_w', 'down_w')}
    del _L0_ffn_all
    return {'x': x, 'fside_BxS2xS2_0': fside_BxS2xS2_0, 'ctx_1024': ctx_1024, 'L0_attn_in_proj_w': _L0_attn_in['in_proj_w'], 'L0_attn_conv_w': _L0_attn_in['conv_w'], 'L0_attn_conv_b': _L0_attn_in['conv_b'], 'L0_attn_dt_bias': _L0_attn_in['dt_bias'], 'L0_attn_A_log': _L0_attn_in['A_log'], 'L0_attn_D': _L0_attn_in['D'], 'L0_attn_norm_w': _L0_attn_in['norm_w'], 'L0_attn_out_proj_w': _L0_attn_in['out_proj_w'], 'L0_ffn_router_w': _L0_ffn_in['router_w'], 'L0_ffn_gate_w': _L0_ffn_in['gate_w'], 'L0_ffn_up_w': _L0_ffn_in['up_w'], 'L0_ffn_down_w': _L0_ffn_in['down_w']}

def reference(x, fside_BxS2xS2_0, ctx_1024, L0_attn_in_proj_w, L0_attn_conv_w, L0_attn_conv_b, L0_attn_dt_bias, L0_attn_A_log, L0_attn_D, L0_attn_norm_w, L0_attn_out_proj_w, L0_ffn_router_w, L0_ffn_gate_w, L0_ffn_up_w, L0_ffn_down_w):
    import jax
    import jax.numpy as jnp

    def _L0_attn_ref(hidden_states, in_proj_w, conv_w, conv_b, dt_bias, A_log, D, norm_w, out_proj_w):
        import jax, jax.numpy as jnp
        import numpy as np
        B_, L_, D_MODEL = (2, 512, 512)
        EXPAND = 2
        D_IN = EXPAND * D_MODEL
        HEADS = 64
        HEAD_DIM = D_IN // HEADS
        STATE = 128
        NGROUPS = 1
        K = 4
        CONV_DIM = D_IN + 2 * NGROUPS * STATE
        PROJ = D_IN + CONV_DIM + HEADS
        CHUNK = 64
        EPS = 1e-05

        def _segsum(x):
            T = x.shape[-1]
            c = jnp.cumsum(x, axis=-1)
            seg = c[..., :, None] - c[..., None, :]
            return jnp.where(jnp.tril(jnp.ones((T, T), bool)), seg, -jnp.inf)

        def _ssd(x, dA, Bm, Cm):
            b, l, h, p = x.shape
            n = Bm.shape[-1]
            c = l // CHUNK
            rep = h // Bm.shape[2]
            Bh = jnp.repeat(Bm, rep, axis=2).reshape(b, c, CHUNK, h, n)
            Ch = jnp.repeat(Cm, rep, axis=2).reshape(b, c, CHUNK, h, n)
            x = x.reshape(b, c, CHUNK, h, p)
            dA = dA.reshape(b, c, CHUNK, h).transpose(0, 3, 1, 2)
            dA_cum = jnp.cumsum(dA, axis=-1)
            Lmat = jnp.exp(_segsum(dA))
            Y_diag = jnp.einsum('bcthn,bcshn,bhcts,bcshp->bcthp', Ch, Bh, Lmat, x)
            decay_states = jnp.exp(dA_cum[..., -1:] - dA_cum)
            states = jnp.einsum('bcshn,bhcs,bcshp->bchpn', Bh, decay_states, x)
            chunk_decay = jnp.exp(_segsum(jnp.pad(dA_cum[..., -1], ((0, 0), (0, 0), (1, 0)))))
            states = jnp.concatenate([jnp.zeros_like(states[:, :1]), states], axis=1)
            prev = jnp.einsum('bhzc,bchpn->bzhpn', chunk_decay, states)[:, :-1]
            Y_off = jnp.einsum('bcthn,bchpn,bhct->bcthp', Ch, prev, jnp.exp(dA_cum))
            return (Y_diag + Y_off).reshape(b, l, h, p)
        b, l, _ = hidden_states.shape
        proj = hidden_states @ in_proj_w.T
        gate = proj[..., :D_IN]
        xBC = proj[..., D_IN:D_IN + CONV_DIM]
        dt = proj[..., D_IN + CONV_DIM:]
        xp = jnp.pad(xBC, ((0, 0), (K - 1, 0), (0, 0)))
        conv = conv_b + sum((conv_w[:, i] * xp[:, i:i + l, :] for i in range(K)))
        xBC = jax.nn.silu(conv)
        x = xBC[..., :D_IN].reshape(b, l, HEADS, HEAD_DIM)
        Bm = xBC[..., D_IN:D_IN + NGROUPS * STATE].reshape(b, l, NGROUPS, STATE)
        Cm = xBC[..., D_IN + NGROUPS * STATE:].reshape(b, l, NGROUPS, STATE)
        dt = jax.nn.softplus(dt + dt_bias)
        A = -jnp.exp(A_log)
        y = _ssd(x * dt[..., None], dt * A, Bm, Cm)
        y = y + D[None, None, :, None] * x
        y = y.reshape(b, l, D_IN)
        hg = y * jax.nn.silu(gate)
        var = jnp.mean(hg * hg, axis=-1, keepdims=True)
        y = hg * jax.lax.rsqrt(var + EPS) * norm_w
        return y @ out_proj_w.T

    def _L0_xattn_ref(x, gate_up_weight, down_weight):
        import jax, jax.numpy as jnp
        import numpy as np
        EPS = 1e-06
        QMAX = 127.0

        def _smooth_quant_linear(x, w):
            amax_x = jnp.max(jnp.abs(x), axis=0)
            amax_w = jnp.max(jnp.abs(w), axis=0)
            s = jnp.sqrt(jnp.maximum(amax_x, EPS) / jnp.maximum(amax_w, EPS))
            s = jnp.maximum(s, EPS)
            xs = x / s
            ws = w * s
            x_scale = jnp.maximum(jnp.max(jnp.abs(xs), axis=-1, keepdims=True), EPS) / QMAX
            w_scale = jnp.maximum(jnp.max(jnp.abs(ws), axis=-1, keepdims=True), EPS) / QMAX
            x_q = jnp.clip(jnp.round(xs / x_scale), -QMAX, QMAX)
            w_q = jnp.clip(jnp.round(ws / w_scale), -QMAX, QMAX)
            return x_q @ w_q.T * x_scale * w_scale.T

        def _expert_forward(xe, guw, dw):
            h = _smooth_quant_linear(xe, guw)
            gate, up = jnp.split(h, 2, axis=-1)
            a = jax.nn.silu(gate) * up
            return _smooth_quant_linear(a, dw)
        return jax.vmap(_expert_forward)(x, gate_up_weight, down_weight)

    def _L0_ffn_ref(hidden_states, router_w, gate_w, up_w, down_w):
        import jax, jax.numpy as jnp
        import numpy as np
        TOP_P = 0.9
        S, B, H, I, E = (512, 4, 512, 1024, 8)

        def _top_p_weights(probs, top_p):
            order = jnp.argsort(-probs, axis=-1)
            sp = jnp.take_along_axis(probs, order, axis=-1)
            cum = jnp.cumsum(sp, axis=-1)
            exceed = cum > top_p
            first_idx = jnp.argmax(exceed, axis=-1)
            first = jnp.arange(probs.shape[-1])[None, :] == first_idx[:, None]
            keep = ~exceed | first
            kept = jnp.where(keep, sp, 0.0)
            t_idx = jnp.arange(probs.shape[0])[:, None]
            return jnp.zeros_like(probs).at[t_idx, order].set(kept)
        s, b, h = hidden_states.shape
        x = hidden_states.reshape(-1, h)
        probs = jax.nn.softmax(x @ router_w.T, axis=-1)
        w = _top_p_weights(probs, TOP_P)
        out = jnp.zeros_like(x)
        n_exp = router_w.shape[0]
        for e in range(n_exp):
            g = jax.nn.silu(x @ gate_w[e].T)
            u = x @ up_w[e].T
            y = g * u @ down_w[e].T
            out = out + y * w[:, e:e + 1]
        return out.reshape(s, b, h)
    x = x + _L0_attn_ref(_layernorm(x, axis=-1), L0_attn_in_proj_w, L0_attn_conv_w, L0_attn_conv_b, L0_attn_dt_bias, L0_attn_A_log, L0_attn_D, L0_attn_norm_w, L0_attn_out_proj_w)
    x = x + _L0_xattn_ref(_layernorm(x, axis=-1), fside_BxS2xS2_0, ctx_1024)
    x = x + _L0_ffn_ref(_layernorm(x, axis=-1), L0_ffn_router_w, L0_ffn_gate_w, L0_ffn_up_w, L0_ffn_down_w)
    return x

_drawn_inputs = setup_inputs


def setup_inputs(seed=0):
    import zlib

    import numpy as np

    out = dict(_drawn_inputs(seed))
    spreads = {'L0_attn_conv_b': (0.0, 0.1),
     'L0_attn_dt_bias': (1.0, 0.6),
     'L0_attn_D': (1.0, 0.2),
     'L0_attn_norm_w': (1.0, 0.2)}
    factors = {'L0_attn_A_log': 8.0, 'L0_ffn_router_w': 5.159}
    for name, (base, spread) in spreads.items():
        noise = np.random.default_rng([zlib.crc32(name.encode()), seed]).standard_normal(out[name].shape)
        drawn = base * np.exp(spread * noise) if base else spread * noise
        out[name] = jnp.asarray(drawn.astype(out[name].dtype))
    for name, factor in factors.items():
        out[name] = (out[name] * factor).astype(out[name].dtype)
    return out
```

```python
from contextlib import ExitStack

import concourse.bass as bass
from concourse import mybir

F32 = mybir.dt.float32
BF16 = mybir.dt.bfloat16
ALU = mybir.AluOpType
ACT = mybir.ActivationFunctionType
AX = mybir.AxisListType

P = 128
B, L, D = 4, 512, 512
TT = L // P
KD = D // P
DIN, HEADS, HD, N, CHUNK, KC = 1024, 64, 16, 128, 64, 4
CONV = DIN + 2 * N
PROJ = DIN + CONV + HEADS
NCC = CONV // P
NX = DIN // P
DTC = DIN + CONV
UH = 8
UPT = HEADS // UH
U = TT * UPT
IQ = 256
E, I = 8, 1024
EPS = 1e-5
QEPS, QMAX, MAGIC = 1e-6, 127.0, 12582912.0
TOP_P = 0.9
NT = B * TT
PAIR = 2
PIECES = 12
IC = I // P
CONSTS = 22


class Count:

    def __init__(self, ctx, nc, name, per):
        self.sem, self.per = ctx.enter_context(nc.semaphore(name)), per

    def at(self, i, k):
        return i * self.per + (self.per + k)

    def before(self, i, k):
        return i * self.per + k


class Own:

    def __init__(self, count, eng, i):
        self.c, self.eng, self.i, self.n = count, eng, i, 0

    def link(self, ins):
        self.n += 1
        ins.then_inc(self.c.sem, 1)
        self.eng.wait_ge(self.c.sem, self.c.at(self.i, self.n))

    def close(self):
        assert self.n <= self.c.per, self.n
        if self.n < self.c.per:
            self.eng.sem_inc(self.c.sem, self.c.per - self.n)


def decoder_layer(nc, x, guw, guwT, dnw, dnwT, winT, conv_w, conv_b, dt_bias, a_log, d_skip,
                  norm_w, woutT, rwT, gateT, upT, downT, out):
    x2_dram = nc.dram_tensor("x2_dram", [B, P, TT, D], F32, kind="Internal").ap()
    zh_dram = nc.dram_tensor("zh_dram", [B, P, KD, L], BF16, kind="Internal").ap()
    zl_dram = nc.dram_tensor("zl_dram", [B, P, KD, L], BF16, kind="Internal").ap()
    wt_dram = nc.dram_tensor("wt_dram", [B, P, E * TT], F32, kind="Internal").ap()
    first_pass(nc, x, guw, guwT, dnw, dnwT, winT, conv_w, conv_b, dt_bias, a_log, d_skip,
               norm_w, woutT, rwT, x2_dram, zh_dram, zl_dram, wt_dram)
    expert_pass(nc, gateT, upT, downT, x2_dram, zh_dram, zl_dram, wt_dram, out)


def first_pass(nc, x, guw, guwT, dnw, dnwT, winT, conv_w, conv_b, dt_bias, a_log, d_skip,
               norm_w, woutT, rwT, x2_dram, zh_dram, zl_dram, wt_dram):
    with ExitStack() as ctx:
        def sb(name, shape, dt=F32):
            return ctx.enter_context(nc.sbuf_tensor(name, shape, dt))

        def sem(name):
            return ctx.enter_context(nc.semaphore(name))

        counts = []

        def count(name, per):
            counts.append(Count(ctx, nc, name, per))
            return counts[-1]

        ps = ctx.enter_context(nc.psum_tensor("ps", [P, 8, 512], F32))

        win_h = sb("win_h", [P, KD, PROJ], BF16)
        win_l = sb("win_l", [P, KD, PROJ], BF16)
        wout_h = sb("wout_h", [P, NX, D], BF16)
        wout_l = sb("wout_l", [P, NX, D], BF16)
        rw = sb("rw", [P, KD, E])
        cw = sb("cw", [P, NCC, KC])
        cb = sb("cb", [P, NCC])
        dtb_bc = sb("dtb_bc", [P, HEADS])
        alog_bc = sb("alog_bc", [P, HEADS])
        expa_bc = sb("expa_bc", [P, HEADS])
        d_bc = sb("d_bc", [P, HEADS])
        nw = sb("nw", [P, NX])
        ident = sb("ident", [P, P])
        identb = sb("identb", [P, P], BF16)
        later = sb("later", [P, P], BF16)
        upto = sb("upto", [P, CHUNK, UH], BF16)
        incl = sb("incl", [P, P])
        in_a = sb("in_a", [P, P])
        in_b = sb("in_b", [P, P])
        gmask = sb("gmask", [P, CHUNK])
        tie = sb("tie", [P, E, E])
        xc = sb("xc", [P, TT, D])
        zn = sb("zn", [P, TT, D])
        st6 = sb("st6", [P, TT, 6])
        mv = sb("mv", [P, TT, 2])
        ve = sb("ve", [P, TT])
        sd = sb("sd", [P, TT])
        r0 = sb("r0", [P, TT])
        r1 = sb("r1", [P, TT])
        rs = sb("rs", [P, TT])
        ssq = sb("ssq", [P, TT])
        xnh = sb("xnh", [P, KD, L], BF16)
        xnl = sb("xnl", [P, KD, L], BF16)
        xraw = sb("xraw", [P, 2, KC - 1 + L])
        cacc = sb("cacc", [P, 2, L])
        xT = sb("xT", [P, 2, L])
        bT = sb("bT", [P, L])
        cT = sb("cT", [P, L])
        btok = sb("btok", [P, TT, N])
        big = sb("big", [P, 3 * TT * DIN])
        xtok = big[:, 0:TT * DIN].rearrange("p (t c) -> p t c", t=TT)
        xdt = big[:, TT * DIN:2 * TT * DIN].rearrange("p (t c) -> p t c", t=TT)
        gs = big[:, 2 * TT * DIN:3 * TT * DIN].rearrange("p (t c) -> p t c", t=TT)
        dtv = sb("dtv", [P, TT, HEADS])
        dta = sb("dta", [P, TT, HEADS])
        dte = sb("dte", [P, TT, HEADS])
        dt = sb("dt", [P, TT, HEADS])
        da = sb("da", [P, TT, HEADS])
        dah = sb("dah", [P, TT, HEADS], BF16)
        dal = sb("dal", [P, TT, HEADS], BF16)
        ecum = sb("ecum", [P, TT, HEADS])
        cdec = sb("cdec", [P, 2, TT, HEADS])
        gm = sb("gm", [P, TT, CHUNK])
        bh = sb("bh", [P, 2, CHUNK, UH], BF16)
        bl = sb("bl", [P, 2, CHUNK, UH], BF16)
        eu = sb("eu", [P, 2, CHUNK, UH])
        mu = sb("mu", [P, 2, CHUNK, UH])
        e63 = sb("e63", [P, 2, HEADS])
        xdd = sb("xdd", [P, DIN])
        S = sb("S", [P, DIN])
        y = sb("y", [P, DIN])
        junk = sb("junk", [P, DIN], BF16)
        hth = sb("hth", [P, 2, NX, P], BF16)
        htl = sb("htl", [P, 2, NX, P], BF16)
        wnat = big[:, 0:TT * D].rearrange("p (t d) -> p t d", t=TT)
        wTr = big[:, TT * D:2 * TT * D].rearrange("p (t d) -> p t d", t=TT)
        w2nat = big[:, 2 * TT * D:2 * TT * D + TT * IQ].rearrange("p (t d) -> p t d", t=TT)
        w2Tr = big[:, 2 * TT * D + TT * IQ:3 * TT * D].rearrange("p (t d) -> p t d", t=2)
        axm = sb("axm", [P, KD])
        awm = sb("awm", [P, KD])
        ra = sb("ra", [P, KD])
        sm = sb("sm", [P, KD])
        sq0 = sb("sq0", [P, KD])
        sr = sb("sr", [P, KD])
        xsc = sb("xsc", [P, TT])
        wsc = sb("wsc", [P, TT])
        rx = sb("rx", [P, TT])
        rw_ = sb("rw_", [P, TT])
        qx = gs[:, 0, :].bitcast(BF16).rearrange("p (t d) -> p t d", t=TT)
        qw = gs[:, 1, :].bitcast(BF16).rearrange("p (t d) -> p t d", t=TT)
        qxT = gs[:, 2, :].bitcast(BF16).rearrange("p (t d) -> p t d", t=KD)
        qwT = gs[:, 3, :].bitcast(BF16).rearrange("p (t d) -> p t d", t=KD)
        wscb = y[:, 0:D]
        hq = xdd[:, :].rearrange("p (t d) -> p t d", t=2)
        sg = cacc[:, :, 0:IQ]
        av = S[:, :].rearrange("p (t d) -> p t d", t=TT)
        zTf = sb("zTf", [P, 2, KD, P])
        mx = sb("mx", [P, TT])
        lg = sb("lg", [P, TT, E])
        pe_ = sb("pe_", [P, TT, E])
        pr = sb("pr", [P, TT, E])
        gt = sb("gt", [P, TT, E, E])
        eq = sb("eq", [P, TT, E, E])
        sums = sb("sums", [P, TT])
        mass = sb("mass", [P, TT, E])
        keep = sb("keep", [P, TT, E])
        wt = sb("wt", [P, E, TT])

        s_win = sem("s_win")
        s_wsplit = sem("s_wsplit")
        s_wout = sem("s_wout")
        s_wsc = sem("s_wsc")
        s_small = sem("s_small")
        s_const = sem("s_const")
        s_wh = sem("s_wh")
        s_wl = sem("s_wl")
        s_expa = sem("s_expa")
        s_pass = sem("s_pass")
        ldx = count("ldx", 16)
        ldq = count("ldq", 64)
        stz = count("stz", 64)
        own_v = count("own_v", 140)
        own_a = count("own_a", 8)
        own_p = count("own_p", 8)
        var_in = count("var_in", 4)
        std_out = count("std_out", 4)
        znr = count("znr", 12)
        t1 = count("t1", TT)
        t1h = count("t1h", TT)
        t1l = count("t1l", TT)
        pj = count("pj", NCC)
        raw = count("raw", NCC)
        cv = count("cv", NCC)
        act_x = count("act_x", NCC)
        xt = count("xt", NX + 1)
        xta = count("xta", NX + 1)
        xtd = count("xtd", NX)
        dtp = count("dtp", 1)
        v_in = count("v_in", 1)
        sp_out = count("sp_out", 1)
        dar = count("dar", 1)
        cum = count("cum", 1)
        ecd = count("ecd", 1)
        gp = count("gp", 1)
        gmr = count("gmr", 1)
        gate_p = count("gate_p", 2 * TT)
        gate_s = count("gate_s", 2 * TT)
        bhi = count("bhi", U)
        blo = count("blo", U)
        seg = count("seg", U)
        ex = count("ex", U)
        mr = count("mr", U)
        yd = count("yd", U)
        dxr = count("dxr", TT)
        xddr = count("xddr", TT)
        yo = count("yo", 2 * TT)
        sn = count("sn", 2 * TT)
        su = count("su", 2 * TT)
        s0 = count("s0", 1)
        yc = count("yc", TT)
        hgr = count("hgr", TT)
        sqr = count("sqr", TT)
        ht = count("ht", 2 * TT)
        hh = count("hh", 2 * TT)
        hl = count("hl", 2 * TT)
        op = count("op", TT)
        x1r = count("x1r", TT)
        t2 = count("t2", KD + 2)
        t2r = count("t2r", KD + 2)
        rat = count("rat", 2)
        sqt = count("sqt", 2)
        sbr = count("sbr", 2)
        sbp = count("sbp", 2)
        wsr = count("wsr", 2)
        wsp = count("wsp", 2)
        wsb = count("wsb", 2)
        qr = count("qr", 4 * TT)
        qt = count("qt", 4 * TT)
        qc = count("qc", 4 * TT)
        qm = count("qm", 2 * TT)
        hr = count("hr", TT)
        sgr = count("sgr", TT)
        ar = count("ar", TT)
        x2r = count("x2r", TT)
        t3 = count("t3", TT)
        t3f = count("t3f", TT)
        t3h = count("t3h", TT)
        t3l = count("t3l", TT)
        lgp = count("lgp", TT)
        lgi = count("lgi", 1)
        lge = count("lge", 1)
        wtr = count("wtr", 1)

        block = ctx.enter_context(nc.Block())

        @block.sync
        def _(sp):
            sp.dma_start(big[:, 0:KD * PROJ].rearrange("p (k n) -> p k n", k=KD),
                         winT.rearrange("(k p) n -> p k n", p=P)).then_inc(s_win, 16)
            for dst, src in ((rw[:], rwT), (cw[:], conv_w), (cb[:], conv_b), (nw[:], norm_w),
                             (dtb_bc[:], dt_bias.to_broadcast([P, HEADS])),
                             (alog_bc[:], a_log.to_broadcast([P, HEADS])),
                             (d_bc[:], d_skip.to_broadcast([P, HEADS]))):
                sp.dma_start(dst, src).then_inc(s_small, 16)
            sp.wait_ge(s_wl, 1)
            sp.dma_start(big[:, 0:NX * D].rearrange("p (k n) -> p k n", k=NX),
                         woutT.rearrange("(k p) n -> p k n", p=P)).then_inc(s_wout, 16)
            with sp.Fori(0, B) as i:
                sp.wait_ge(stz.sem, stz.before(i, 64))
                sp.sem_inc(s_pass, 1)
                sp.dma_start(xc[:], x[i]).then_inc(ldx.sem, 16)
                sp.wait_ge(hl.sem, hl.at(i, 2 * TT))
                sp.sem_inc(s_pass, 1)
                sp.dma_start(wnat, guw[i]).then_inc(ldq.sem, 16)
                sp.dma_start(wTr, guwT[i]).then_inc(ldq.sem, 16)
                sp.dma_start(w2nat, dnw[i]).then_inc(ldq.sem, 16)
                sp.dma_start(w2Tr, dnwT[i]).then_inc(ldq.sem, 16)
                sp.wait_ge(x2r.sem, x2r.at(i, TT))
                sp.sem_inc(s_pass, 1)
                sp.dma_start(x2_dram[i], xc[:]).then_inc(stz.sem, 16)
                sp.wait_ge(t3l.sem, t3l.at(i, TT))
                sp.sem_inc(s_pass, 1)
                sp.dma_start(zh_dram[i], xnh[:]).then_inc(stz.sem, 16)
                sp.dma_start(zl_dram[i], xnl[:]).then_inc(stz.sem, 16)
                sp.wait_ge(wtr.sem, wtr.at(i, 1))
                sp.sem_inc(s_pass, 1)
                sp.dma_start(wt_dram[i], wt[:].rearrange("p e t -> p (e t)")).then_inc(stz.sem, 16)
            sp.wait_ge(stz.sem, stz.per * (B + 1))

        @block.gpsimd
        def _(pool):
            for c in counts:
                pool.sem_inc(c.sem, c.per)
            done = [0]

            def step(ins):
                done[0] += 1
                ins.then_inc(s_const, 1)
                pool.wait_ge(s_const, done[0])

            def select(view, op, fill, pattern, mult):
                step(nc.gpsimd.affine_select(out=view, in_=view, compare_op=op, fill=fill, base=0,
                                             pattern=pattern, channel_multiplier=mult))

            for t, v in ((ident, 0.0), (identb, 0.0), (later, 0.0), (incl, 0.0),
                         (upto, 1.0), (gmask, 1.0), (tie, 1.0), (in_a, 0.0), (in_b, 0.0)):
                step(nc.gpsimd.memset(t[:], v))
            for t in (ident, identb):
                select(t[:], ALU.not_equal, 1.0, [[-1, P]], 1)
            select(tie[:], ALU.is_gt, 0.0, [[1, E], [-1, E]], 0)
            step(nc.gpsimd.memset(in_a[0:CHUNK, :], 1.0))
            step(nc.gpsimd.memset(in_b[CHUNK:P, :], 1.0))
            for h in (0, CHUNK):
                r = slice(h, h + CHUNK)
                select(later[r, r], ALU.is_ge, 1.0, [[1, CHUNK]], -1)
                select(incl[r, r], ALU.is_gt, 1.0, [[-1, CHUNK]], 1)
                select(upto[r], ALU.is_ge, 0.0, [[1, CHUNK], [0, UH]], -1)
                select(gmask[r], ALU.is_ge, 0.0, [[1, CHUNK]], -1)
            assert done[0] == CONSTS
            pool.wait_ge(s_small, 7 * 16)
            with pool.Fori(0, B) as i:
                own = Own(own_p, pool, i)

                def low(u):
                    tt, q = divmod(u, UPT)
                    if u >= 2:
                        pool.wait_ge(seg.sem, seg.at(i, u - 1))
                    nc.gpsimd.tensor_tensor(
                        bl[:, u % 2], dal[:, tt, q * UH:(q + 1) * UH].unsqueeze(1).to_broadcast([P, CHUNK, UH]),
                        upto[:], ALU.mult).then_inc(blo.sem, 1)

                def skip(tt):
                    v = xtok[:, tt, :].rearrange("p (h d) -> p h d", h=HEADS)
                    nc.gpsimd.tensor_tensor(v, v, d_bc[:].unsqueeze(2).to_broadcast([P, HEADS, HD]),
                                            ALU.mult).then_inc(dxr.sem, 1)

                def to_end(tt):
                    pool.wait_ge(ex.sem, ex.at(i, (tt + 1) * UPT))
                    if tt:
                        pool.wait_ge(sn.sem, sn.at(i, 2 * tt))
                    nc.gpsimd.tensor_tensor(
                        xdd[:].rearrange("p (h d) -> p h d", h=HEADS),
                        xdt[:, tt, :].rearrange("p (h d) -> p h d", h=HEADS),
                        e63[:, tt % 2, :].unsqueeze(2).to_broadcast([P, HEADS, HD]),
                        ALU.mult).then_inc(xddr.sem, 1)

                def gated(tt):
                    pool.wait_ge(yc.sem, yc.at(i, tt + 1))
                    pool.wait_ge(dxr.sem, dxr.at(i, tt + 1))
                    own.link(nc.gpsimd.tensor_tensor(y[:], y[:], xtok[:, tt, :], ALU.add))
                    pool.wait_ge(gate_s.sem, gate_s.at(i, 2 * tt + 2))
                    nc.gpsimd.tensor_tensor(gs[:, tt, :], y[:], gs[:, tt, :], ALU.mult).then_inc(hgr.sem, 1)

                pool.wait_ge(xta.sem, xta.at(i, NX + 1))
                pool.wait_ge(dar.sem, dar.at(i, 1))
                low(0)
                low(1)
                for u in range(U):
                    tt, q = divmod(u, UPT)
                    if u + 2 < U:
                        low(u + 2)
                    if q == 2 and tt:
                        gated(tt - 1)
                    if q == 4:
                        skip(tt)
                    if q == UPT - 1:
                        to_end(tt)
                gated(TT - 1)
                own.close()

        @block.scalar
        def _(act):
            act.wait_ge(s_win, 16)
            nc.scalar.activation(win_h[:].rearrange("p k n -> p (k n)"), big[:, 0:KD * PROJ],
                                 ACT.Copy).then_inc(s_wh, 1)
            act.wait_ge(s_small, 7 * 16)
            nc.scalar.activation(expa_bc[:], alog_bc[:], ACT.Exp).then_inc(s_expa, 1)
            act.wait_ge(s_wsc, NX)
            nc.scalar.activation(wout_h[:].rearrange("p k n -> p (k n)"), big[:, 0:NX * D],
                                 ACT.Copy).then_inc(s_wh, 1)
            with act.Fori(0, B) as i:
                def root(k, n=TT, src=ve, dst=sd):
                    act.wait_ge(var_in.sem, var_in.at(i, k + 1))
                    nc.scalar.activation(dst[:, 0:n], src[:, 0:n], ACT.Sqrt).then_inc(std_out.sem, 1)

                def split_t(ready, hi, tt):
                    act.wait_ge(ready.sem, ready.at(i, tt + 1))
                    nc.scalar.activation(xnh[:, :, tt * P:(tt + 1) * P],
                                         ps[:, tt % 2, :].rearrange("p (k t) -> p k t", k=KD),
                                         ACT.Copy).then_inc(hi.sem, 1)

                root(0)
                for tt in range(TT):
                    split_t(t1, t1h, tt)

                def conv_in(n):
                    cc = (n + NX) if n < 2 else n - 2
                    act.wait_ge(pj.sem, pj.at(i, n + 1))
                    if n >= 2:
                        act.wait_ge(cv.sem, cv.at(i, n - 1))
                        act.wait_ge(act_x.sem, act_x.at(i, n - 1))
                    nc.scalar.activation(xraw[:, n % 2, KC - 1:], ps[:, 2 + n % 2, :], ACT.Copy)
                    nc.scalar.activation(cacc[:, n % 2, :], ps[:, 2 + n % 2, :], ACT.Identity,
                                         bias=cb[:, cc:cc + 1],
                                         scale=cw[:, cc, KC - 1:KC]).then_inc(raw.sem, 1)

                def conv_out(n):
                    act.wait_ge(cv.sem, cv.at(i, n + 1))
                    dst = (bT[:], cT[:])[n] if n < 2 else xT[:, n % 2, :]
                    if n >= 4:
                        act.wait_ge(xt.sem, xt.at(i, n - 2))
                    nc.scalar.activation(dst, cacc[:, n % 2, :], ACT.Silu).then_inc(act_x.sem, 1)

                def back(j):
                    act.wait_ge(xt.sem, xt.at(i, j + 1))
                    src = ps[:, j % 2, :].rearrange("p (t c) -> p t c", t=TT)
                    dst = btok[:] if j == 0 else xtok[:, :, (j - 1) * P:j * P]
                    nc.scalar.activation(dst, src, ACT.Copy).then_inc(xta.sem, 1)

                for n in range(NCC):
                    conv_in(n)
                    if n == 1:
                        act.wait_ge(v_in.sem, v_in.at(i, 1))
                        own = Own(own_a, act, i)
                        own.link(nc.scalar.activation(dte[:], dta[:], ACT.Exp, scale=-1.0))
                        nc.scalar.activation(dte[:], dte[:], ACT.Ln, bias=1.0).then_inc(sp_out.sem, 1)
                        own.close()
                        act.wait_ge(cum.sem, cum.at(i, 1))
                        nc.scalar.activation(ecum[:], ps[:, 5, 0:TT * HEADS].rearrange("p (t h) -> p t h", t=TT),
                                             ACT.Exp)
                        nc.scalar.activation(cdec[:].rearrange("p c t h -> p (c t h)"), ps[:, 6, :],
                                             ACT.Exp).then_inc(ecd.sem, 1)
                    if n >= 1:
                        conv_out(n - 1)
                    if n == 3:
                        back(0)
                    if n >= 4:
                        back(n - 3)
                conv_out(NCC - 1)
                back(NX - 1)
                back(NX)
                for g in range(2 * TT):
                    act.wait_ge(gate_p.sem, gate_p.at(i, g + 1))
                    nc.scalar.activation(gs[:, g // 2, (g % 2) * 512:(g % 2 + 1) * 512], ps[:, 2 + g % 2, :],
                                         ACT.Silu).then_inc(gate_s.sem, 1)

                def square(tt):
                    act.wait_ge(hgr.sem, hgr.at(i, tt + 1))
                    nc.scalar.activation(junk[:], gs[:, tt, :], ACT.Square,
                                         accum_out=ssq[:, tt:tt + 1]).then_inc(sqr.sem, 1)

                for u in range(U):
                    tt, q = divmod(u, UPT)
                    act.wait_ge(seg.sem, seg.at(i, u + 1))
                    if q == 0 and tt >= 2:
                        act.wait_ge(xddr.sem, xddr.at(i, tt - 1))
                    nc.scalar.activation(e63[:, tt % 2, q * UH:(q + 1) * UH],
                                         ps[:, u % 2, (CHUNK - 1) * UH:], ACT.Exp)
                    if u >= 2:
                        act.wait_ge(mr.sem, mr.at(i, u - 1))
                    nc.scalar.activation(eu[:, u % 2].rearrange("p t h -> p (t h)"), ps[:, u % 2, :],
                                         ACT.Exp).then_inc(ex.sem, 1)
                    if q == 5 and tt:
                        square(tt - 1)
                square(TT - 1)
                root(1)
                for g in range(2 * TT):
                    act.wait_ge(ht.sem, ht.at(i, g + 1))
                    if g >= 4:
                        act.wait_ge(op.sem, op.at(i, g // 2 - 1))
                    nc.scalar.activation(hth[:, g // 2 % 2, (g % 2) * 4:(g % 2) * 4 + 4, :],
                                         ps[:, g % 2, :].rearrange("p (k t) -> p k t", k=4),
                                         ACT.Copy).then_inc(hh.sem, 1)
                root(2)
                for lin in range(2):
                    act.wait_ge(rat.sem, rat.at(i, lin + 1))
                    n = KD if lin == 0 else 2
                    nc.scalar.activation(sq0[:, 0:n], ra[:, 0:n], ACT.Sqrt).then_inc(sqt.sem, 1)
                    act.wait_ge(wsp.sem, wsp.at(i, lin + 1))
                    if lin:
                        act.wait_ge(hr.sem, hr.at(i, TT))
                    nc.scalar.activation(wscb, ps[:, 5, :], ACT.Copy).then_inc(wsb.sem, 1)
                    for g in range(2 * TT):
                        act.wait_ge(qt.sem, qt.at(i, 2 * TT * lin + g + 1))
                        if lin and g == 0:
                            act.wait_ge(qm.sem, qm.at(i, TT))
                        dst = (qxT if g % 2 == 0 else qwT)[:, 0:n, (g // 2) * P:(g // 2 + 1) * P]
                        src = ps[:, g % 2, 0:64 * n].bitcast(BF16).rearrange("p (k t) -> p k t", k=n)
                        nc.scalar.activation(dst, src, ACT.Copy).then_inc(qc.sem, 1)
                    if lin == 0:
                        for tt in range(TT):
                            act.wait_ge(hr.sem, hr.at(i, tt + 1))
                            nc.scalar.activation(sg[:, tt % 2, :], hq[:, tt % 2, 0:IQ],
                                                 ACT.Silu).then_inc(sgr.sem, 1)
                root(3)
                for tt in range(TT):
                    act.wait_ge(t3.sem, t3.at(i, tt + 1))
                    if tt >= 2:
                        act.wait_ge(lgp.sem, lgp.at(i, tt - 1))
                    nc.scalar.activation(zTf[:, tt % 2], ps[:, tt % 2, :].rearrange("p (k t) -> p k t", k=KD),
                                         ACT.Copy).then_inc(t3f.sem, 1)
                    split_t(t3, t3h, tt)
                act.wait_ge(lgi.sem, lgi.at(i, 1))
                nc.scalar.activation(pe_[:], lg[:], ACT.Exp).then_inc(lge.sem, 1)

        @block.vector
        def _(dve):
            nc.vector.memset(xraw[:], 0.0).then_inc(s_wsplit, 1)
            dve.wait_ge(s_wh, 1)
            nc.vector.tensor_tensor(win_l[:].rearrange("p k n -> p (k n)"), big[:, 0:KD * PROJ],
                                    win_h[:].rearrange("p k n -> p (k n)"), ALU.subtract).then_inc(s_wl, 1)
            dve.wait_ge(s_small, 7 * 16)
            dve.wait_ge(s_wout, 16)
            for k in range(NX):
                w = big[:, k * D:(k + 1) * D]
                nc.vector.tensor_scalar(w, w, nw[:, k:k + 1], None, ALU.mult).then_inc(s_wsc, 1)
            dve.wait_ge(s_wh, 2)
            nc.vector.tensor_tensor(wout_l[:].rearrange("p k n -> p (k n)"), big[:, 0:NX * D],
                                    wout_h[:].rearrange("p k n -> p (k n)"), ALU.subtract).then_inc(s_wl, 1)
            dve.wait_ge(s_const, CONSTS)
            dve.wait_ge(s_expa, 1)
            with dve.Fori(0, B) as i:
                own = Own(own_v, dve, i)
                link = own.link

                def inv_root(k):
                    nc.vector.tensor_copy(r0[:], ve[:]).then_inc(var_in.sem, 1)
                    dve.wait_ge(std_out.sem, std_out.at(i, k + 1))
                    link(nc.vector.reciprocal(r0[:], sd[:]))
                    link(nc.vector.tensor_tensor(r1[:], r0[:], r0[:], ALU.mult))
                    link(nc.vector.tensor_tensor(r1[:], r1[:], ve[:], ALU.mult))
                    link(nc.vector.tensor_scalar(r1[:], r1[:], -0.5, 1.5, ALU.mult, ALU.add))
                    link(nc.vector.tensor_tensor(rs[:], r1[:], r0[:], ALU.mult))

                def norm(k, turn):
                    for tt in range(TT):
                        ins = nc.vector.bn_stats(st6[:, tt, :], xc[:, tt, :])
                    link(ins)
                    dve.sem_inc(s_pass, 1)
                    for tt in range(TT):
                        ins = nc.vector.bn_aggr(mv[:, tt, :], st6[:, tt, :])
                    link(ins)
                    link(nc.vector.tensor_scalar(ve[:], mv[:, :, 1], EPS, None, ALU.add))
                    inv_root(turn)
                    for tt in range(TT):
                        nc.vector.tensor_scalar(zn[:, tt, :], xc[:, tt, :], mv[:, tt, 0:1], rs[:, tt:tt + 1],
                                                ALU.subtract, ALU.mult).then_inc(znr.sem, 1)

                def low_t(ready, lo, tt):
                    dve.wait_ge(ready.sem, ready.at(i, tt + 1))
                    nc.vector.tensor_tensor(xnl[:, :, tt * P:(tt + 1) * P],
                                            ps[:, tt % 2, :].rearrange("p (k t) -> p k t", k=KD),
                                            xnh[:, :, tt * P:(tt + 1) * P], ALU.subtract).then_inc(lo.sem, 1)

                dve.wait_ge(ldx.sem, ldx.at(i, 16))
                norm(0, 0)
                for tt in range(TT):
                    low_t(t1h, t1l, tt)

                def conv(n):
                    cc = (n + NX) if n < 2 else n - 2
                    dve.wait_ge(raw.sem, raw.at(i, n + 1))
                    for j in range(KC - 1):
                        ins = nc.vector.scalar_tensor_tensor(
                            out=cacc[:, n % 2, :], in0=xraw[:, n % 2, j:j + L], scalar=cw[:, cc, j:j + 1],
                            in1=cacc[:, n % 2, :], op0=ALU.mult, op1=ALU.add)
                        if j < KC - 2:
                            link(ins)
                    ins.then_inc(cv.sem, 1)

                def back(j):
                    dve.wait_ge(xta.sem, xta.at(i, j + 1))
                    h = P // HD
                    for tt in range(TT):
                        ins = nc.vector.tensor_tensor(
                            xdt[:, tt, (j - 1) * P:j * P].rearrange("p (h d) -> p h d", h=h),
                            ps[:, j % 2, tt * P:(tt + 1) * P].rearrange("p (h d) -> p h d", h=h),
                            dt[:, tt, (j - 1) * h:j * h].unsqueeze(2).to_broadcast([P, h, HD]), ALU.mult)
                    ins.then_inc(xtd.sem, 1)

                for n in range(NCC):
                    if n == 1:
                        dve.wait_ge(dtp.sem, dtp.at(i, 1))
                        link(nc.vector.tensor_tensor(dtv[:], ps[:, 4, 0:TT * HEADS].rearrange("p (t h) -> p t h", t=TT),
                                                     dtb_bc[:].unsqueeze(1).to_broadcast([P, TT, HEADS]), ALU.add))
                        nc.vector.scalar_tensor_tensor(out=dta[:], in0=dtv[:], scalar=-1.0, in1=dtv[:],
                                                       op0=ALU.mult, op1=ALU.max).then_inc(v_in.sem, 1)
                        dve.wait_ge(sp_out.sem, sp_out.at(i, 1))
                        link(nc.vector.scalar_tensor_tensor(out=dt[:], in0=dtv[:], scalar=0.0, in1=dte[:],
                                                            op0=ALU.max, op1=ALU.add))
                        link(nc.vector.scalar_tensor_tensor(
                            out=da[:], in0=dt[:], scalar=-1.0,
                            in1=expa_bc[:].unsqueeze(1).to_broadcast([P, TT, HEADS]),
                            op0=ALU.mult, op1=ALU.mult))
                        link(nc.vector.tensor_copy(dah[:], da[:]))
                        nc.vector.tensor_tensor(dal[:], da[:], dah[:], ALU.subtract).then_inc(dar.sem, 1)
                    conv(n)
                    if n == 3:
                        dve.wait_ge(gp.sem, gp.at(i, 1))
                        nc.vector.tensor_tensor(gm[:], ps[:, 7, 0:TT * CHUNK].rearrange("p (t c) -> p t c", t=TT),
                                                gmask[:].unsqueeze(1).to_broadcast([P, TT, CHUNK]),
                                                ALU.mult).then_inc(gmr.sem, 1)
                    if n >= 5:
                        back(n - 4)
                for j in range(NX - 2, NX + 1):
                    back(j)
                nc.vector.memset(S[:], 0.0).then_inc(s0.sem, 1)

                def high(u):
                    tt, q = divmod(u, UPT)
                    if u >= 2:
                        dve.wait_ge(seg.sem, seg.at(i, u - 1))
                    nc.vector.tensor_tensor(
                        bh[:, u % 2], dah[:, tt, q * UH:(q + 1) * UH].unsqueeze(1).to_broadcast([P, CHUNK, UH]),
                        upto[:], ALU.mult).then_inc(bhi.sem, 1)

                def decayed(u):
                    tt = u // UPT
                    dve.wait_ge(ex.sem, ex.at(i, u + 1))
                    if u >= 2:
                        dve.wait_ge(yd.sem, yd.at(i, u - 1))
                    nc.vector.tensor_tensor(mu[:, u % 2], eu[:, u % 2],
                                            gm[:, tt, :].unsqueeze(2).to_broadcast([P, CHUNK, UH]),
                                            ALU.mult).then_inc(mr.sem, 1)

                def heads(ap):
                    return ap.rearrange("p (h d) -> p h d", h=HEADS)

                def states(tt):
                    for c in range(2):
                        dve.wait_ge(yo.sem, yo.at(i, 2 * tt + c + 1))
                        link(nc.vector.tensor_tensor(
                            heads(S[:]), heads(S[:]),
                            cdec[:, c, tt, :].unsqueeze(2).to_broadcast([P, HEADS, HD]), ALU.mult))
                        dve.wait_ge(sn.sem, sn.at(i, 2 * tt + c + 1))
                        nc.vector.tensor_tensor(S[:], S[:], ps[:, 4:6, :].rearrange("p a b -> p (a b)"),
                                                ALU.add).then_inc(su.sem, 1)
                        if c:
                            continue
                    if tt:
                        dve.wait_ge(hgr.sem, hgr.at(i, tt))
                    link(nc.vector.tensor_tensor(
                        heads(y[:]), heads(ps[:, 6:8, :].rearrange("p a b -> p (a b)")),
                        ecum[:, tt, :].unsqueeze(2).to_broadcast([P, HEADS, HD]), ALU.mult))
                    dve.wait_ge(yd.sem, yd.at(i, (tt + 1) * UPT))
                    nc.vector.tensor_tensor(y[:], y[:], ps[:, 2:4, :].rearrange("p a b -> p (a b)"),
                                            ALU.add).then_inc(yc.sem, 1)

                high(0)
                high(1)
                dve.wait_ge(ecd.sem, ecd.at(i, 1))
                for u in range(U):
                    decayed(u)
                    if u + 2 < U:
                        high(u + 2)
                    if u % UPT == UPT - 1:
                        states(u // UPT)
                dve.wait_ge(sqr.sem, sqr.at(i, TT))
                link(nc.vector.tensor_scalar(ve[:], ssq[:], 1.0 / DIN, EPS, ALU.mult, ALU.add))
                inv_root(1)

                def add_x1(tt):
                    dve.wait_ge(op.sem, op.at(i, tt + 1))
                    nc.vector.scalar_tensor_tensor(out=xc[:, tt, :], in0=ps[:, 4 + tt % 2, :],
                                                   scalar=rs[:, tt:tt + 1], in1=xc[:, tt, :],
                                                   op0=ALU.mult, op1=ALU.add).then_inc(x1r.sem, 1)

                for g in range(2 * TT):
                    dve.wait_ge(hh.sem, hh.at(i, g + 1))
                    half = slice((g % 2) * 4, (g % 2) * 4 + 4)
                    nc.vector.tensor_tensor(htl[:, g // 2 % 2, half, :],
                                            ps[:, g % 2, :].rearrange("p (k t) -> p k t", k=4),
                                            hth[:, g // 2 % 2, half, :], ALU.subtract).then_inc(hl.sem, 1)
                    if g % 2 and g >= 3:
                        add_x1(g // 2 - 1)
                add_x1(TT - 1)
                dve.wait_ge(x1r.sem, x1r.at(i, TT))
                norm(1, 2)

                def linear(lin):
                    n = KD if lin == 0 else 2
                    w = D if lin == 0 else IQ
                    src = zn if lin == 0 else av
                    wn, wr = (wnat, wTr) if lin == 0 else (w2nat, w2Tr)
                    for k in range(n):
                        g = k if lin == 0 else KD + k
                        dve.wait_ge(t2.sem, t2.at(i, g + 1))
                        nc.vector.tensor_reduce(axm[:, k:k + 1], ps[:, g % 2, :], AX.X, ALU.max,
                                                apply_absolute_value=True).then_inc(t2r.sem, 1)
                    if lin == 0:
                        dve.wait_ge(ldq.sem, ldq.at(i, 64))
                    link(nc.vector.tensor_reduce(awm[:, 0:n], wr, AX.X, ALU.max, apply_absolute_value=True))
                    link(nc.vector.tensor_scalar(awm[:, 0:n], awm[:, 0:n], QEPS, None, ALU.max))
                    link(nc.vector.reciprocal(ra[:, 0:n], awm[:, 0:n]))
                    nc.vector.scalar_tensor_tensor(out=ra[:, 0:n], in0=axm[:, 0:n], scalar=QEPS, in1=ra[:, 0:n],
                                                   op0=ALU.max, op1=ALU.mult).then_inc(rat.sem, 1)
                    dve.wait_ge(sqt.sem, sqt.at(i, lin + 1))
                    link(nc.vector.reciprocal(sr[:, 0:n], sq0[:, 0:n]))
                    link(nc.vector.tensor_tensor(sr[:, 0:n], sr[:, 0:n], ra[:, 0:n], ALU.mult))
                    link(nc.vector.tensor_tensor(sm[:, 0:n], sr[:, 0:n], sq0[:, 0:n], ALU.add))
                    link(nc.vector.tensor_scalar(sm[:, 0:n], sm[:, 0:n], 0.5, QEPS, ALU.mult, ALU.max))
                    nc.vector.reciprocal(sr[:, 0:n], sm[:, 0:n]).then_inc(sbr.sem, 1)
                    dve.wait_ge(sbp.sem, sbp.at(i, lin + 1))
                    for t in range(TT):
                        nc.vector.tensor_tensor(src[:, t, :], src[:, t, :], ps[:, 3, 0:w], ALU.mult)
                        ins = nc.vector.tensor_tensor(wn[:, t, :], wn[:, t, :], ps[:, 2, 0:w], ALU.mult)
                    link(ins)
                    nc.vector.tensor_reduce(xsc[:], src[:] if lin == 0 else src, AX.X, ALU.max,
                                            apply_absolute_value=True)
                    link(nc.vector.tensor_reduce(wsc[:], wn, AX.X, ALU.max, apply_absolute_value=True))
                    nc.vector.tensor_scalar(xsc[:], xsc[:], QEPS, 1.0 / QMAX, ALU.max, ALU.mult)
                    ins = nc.vector.tensor_scalar(wsc[:], wsc[:], QEPS, 1.0 / QMAX, ALU.max, ALU.mult)
                    ins.then_inc(wsr.sem, 1)
                    dve.wait_ge(wsr.sem, wsr.at(i, lin + 1))
                    nc.vector.reciprocal(rx[:], xsc[:])
                    link(nc.vector.reciprocal(rw_[:], wsc[:]))
                    if lin:
                        dve.wait_ge(qt.sem, qt.at(i, 2 * TT))
                    both = [(v, r, q, t) for t in range(TT) for v, r, q in ((src, rx, qx), (wn, rw_, qw))]
                    for v, r, q, t in both:
                        ins = nc.vector.tensor_scalar(v[:, t, :], v[:, t, :], r[:, t:t + 1], -QMAX,
                                                      ALU.mult, ALU.max)
                    link(ins)
                    for v, r, q, t in both:
                        ins = nc.vector.tensor_scalar(v[:, t, :], v[:, t, :], QMAX, MAGIC, ALU.min, ALU.add)
                    link(ins)
                    for v, r, q, t in both:
                        nc.vector.tensor_scalar(q[:, t, 0:w], v[:, t, :], MAGIC, None,
                                                ALU.subtract).then_inc(qr.sem, 1)
                    dve.wait_ge(wsb.sem, wsb.at(i, lin + 1))
                    for tt in range(TT):
                        dve.wait_ge(qm.sem, qm.at(i, lin * TT + tt + 1))
                        if lin == 0:
                            if tt >= 2:
                                dve.wait_ge(ar.sem, ar.at(i, tt - 1))
                            h = hq[:, tt % 2, :]
                            nc.vector.scalar_tensor_tensor(out=h, in0=ps[:, 6 + tt % 2, :], scalar=xsc[:, tt:tt + 1],
                                                           in1=wscb, op0=ALU.mult, op1=ALU.mult).then_inc(hr.sem, 1)
                            dve.wait_ge(sgr.sem, sgr.at(i, tt + 1))
                            nc.vector.tensor_tensor(av[:, tt, :], sg[:, tt % 2, :], hq[:, tt % 2, IQ:],
                                                    ALU.mult).then_inc(ar.sem, 1)
                        else:
                            h = hq[:, tt % 2, :]
                            link(nc.vector.scalar_tensor_tensor(out=h, in0=ps[:, 6 + tt % 2, :],
                                                                scalar=xsc[:, tt:tt + 1], in1=wscb,
                                                                op0=ALU.mult, op1=ALU.mult))
                            nc.vector.tensor_tensor(xc[:, tt, :], xc[:, tt, :], h, ALU.add).then_inc(x2r.sem, 1)

                linear(0)
                linear(1)
                dve.wait_ge(x2r.sem, x2r.at(i, TT))
                norm(2, 3)
                for tt in range(TT):
                    low_t(t3h, t3l, tt)
                dve.wait_ge(lgp.sem, lgp.at(i, TT))
                link(nc.vector.tensor_copy(lg[:], ps[:, 2, 0:TT * E].rearrange("p (t e) -> p t e", t=TT)))
                link(nc.vector.tensor_reduce(mx[:], lg[:], AX.X, ALU.max))
                ex8 = [P, TT, E]
                nc.vector.tensor_tensor(lg[:], lg[:], mx[:].unsqueeze(2).to_broadcast(ex8),
                                        ALU.subtract).then_inc(lgi.sem, 1)
                dve.wait_ge(lge.sem, lge.at(i, 1))
                link(nc.vector.tensor_reduce(sums[:], pe_[:], AX.X, ALU.add))
                link(nc.vector.reciprocal(sums[:], sums[:]))
                link(nc.vector.tensor_tensor(pr[:], pe_[:], sums[:].unsqueeze(2).to_broadcast(ex8), ALU.mult))
                for tt in range(TT):
                    pj_, pi_ = (pr[:, tt].unsqueeze(1).to_broadcast([P, E, E]),
                                pr[:, tt].unsqueeze(2).to_broadcast([P, E, E]))
                    nc.vector.tensor_tensor(gt[:, tt], pj_, pi_, ALU.is_gt)
                    ins = nc.vector.tensor_tensor(eq[:, tt], pj_, pi_, ALU.is_equal)
                link(ins)
                link(nc.vector.tensor_tensor(eq[:], eq[:], tie[:].unsqueeze(1).to_broadcast([P, TT, E, E]), ALU.mult))
                link(nc.vector.tensor_tensor(gt[:], gt[:], eq[:], ALU.add))
                link(nc.vector.tensor_tensor(gt[:], gt[:], pr[:].unsqueeze(2).to_broadcast([P, TT, E, E]), ALU.mult))
                link(nc.vector.tensor_reduce(mass[:], gt[:], AX.X, ALU.add))
                link(nc.vector.tensor_scalar(keep[:], mass[:], TOP_P, None, ALU.is_le))
                nc.vector.tensor_tensor(wt[:].rearrange("p e t -> p t e"), pr[:], keep[:],
                                        ALU.mult).then_inc(wtr.sem, 1)
                own.close()

        @block.tensor
        def _(pe):
            pe.wait_ge(s_const, CONSTS)
            pe.wait_ge(s_small, 7 * 16)
            pe.wait_ge(s_wl, 2)

            def mm3(dst, wh, wl, mh, ml, k, last):
                nc.tensor.matmul(dst, wh, mh, start=(k == 0), stop=False)
                nc.tensor.matmul(dst, wh, ml, start=False, stop=False)
                return nc.tensor.matmul(dst, wl, mh, start=False, stop=last)

            with pe.Fori(0, B) as i:
                def turn(src, zbase, ready, tt, used):
                    pe.wait_ge(znr.sem, znr.at(i, zbase + tt + 1))
                    if tt >= 2:
                        pe.wait_ge(used.sem, used.at(i, tt - 1))
                    for k in range(KD):
                        ins = nc.tensor.transpose(ps[:, tt % 2, k * P:(k + 1) * P],
                                                  src[:, tt, k * P:(k + 1) * P], ident[:])
                    ins.then_inc(ready.sem, 1)

                for tt in range(TT):
                    turn(zn, 0, t1, tt, t1l)

                def proj(n):
                    c0 = DIN + ((n + NX) if n < 2 else n - 2) * P
                    if n == 0:
                        pe.wait_ge(t1l.sem, t1l.at(i, TT))
                    if n >= 2:
                        pe.wait_ge(raw.sem, raw.at(i, n - 1))
                    for k in range(KD):
                        ins = mm3(ps[:, 2 + n % 2, :], win_h[:, k, c0:c0 + P], win_l[:, k, c0:c0 + P],
                                  xnh[:, k, :], xnl[:, k, :], k, k == KD - 1)
                    ins.then_inc(pj.sem, 1)

                def back(j):
                    n = 0 if j == 0 else j + 1
                    src = bT[:] if j == 0 else xT[:, n % 2, :]
                    pe.wait_ge(act_x.sem, act_x.at(i, n + 1))
                    if j >= 2:
                        if j == 2:
                            pe.wait_ge(xta.sem, xta.at(i, 1))
                        else:
                            pe.wait_ge(xtd.sem, xtd.at(i, j - 2))
                    for tt in range(TT):
                        ins = nc.tensor.transpose(ps[:, j % 2, tt * P:(tt + 1) * P],
                                                  src[:, tt * P:(tt + 1) * P], ident[:])
                    ins.then_inc(xt.sem, 1)

                proj(0)
                for tt in range(TT):
                    for k in range(KD):
                        t = slice(tt * P, (tt + 1) * P)
                        ins = mm3(ps[:, 4, tt * HEADS:(tt + 1) * HEADS], xnh[:, k, t], xnl[:, k, t],
                                  win_h[:, k, DTC:], win_l[:, k, DTC:], k, k == KD - 1)
                ins.then_inc(dtp.sem, 1)
                proj(1)
                pe.wait_ge(dar.sem, dar.at(i, 1))
                dflat = da[:].rearrange("p t h -> p (t h)")
                nc.tensor.matmul(ps[:, 5, 0:TT * HEADS], incl[:], dflat, start=True, stop=True)
                nc.tensor.matmul(ps[:, 6, 0:TT * HEADS], in_a[:], dflat, start=True, stop=True)
                nc.tensor.matmul(ps[:, 6, TT * HEADS:], in_b[:], dflat, start=True,
                                 stop=True).then_inc(cum.sem, 1)
                proj(2)
                back(0)
                proj(3)
                pe.wait_ge(act_x.sem, act_x.at(i, 2))
                for tt in range(TT):
                    for c in range(2):
                        t = slice(tt * P + c * CHUNK, tt * P + (c + 1) * CHUNK)
                        ins = nc.tensor.matmul(ps[c * CHUNK:(c + 1) * CHUNK, 7, tt * CHUNK:(tt + 1) * CHUNK],
                                               bT[:, t], cT[:, t], start=True, stop=True)
                ins.then_inc(gp.sem, 1)
                for n in range(4, NCC):
                    proj(n)
                    back(n - 3)
                back(NX - 1)
                back(NX)
                for g in range(2 * TT):
                    t = slice(g // 2 * P, (g // 2 + 1) * P)
                    c = slice((g % 2) * 512, (g % 2 + 1) * 512)
                    if g < 2:
                        pe.wait_ge(raw.sem, raw.at(i, NCC))
                    else:
                        pe.wait_ge(gate_s.sem, gate_s.at(i, g - 1))
                    for k in range(KD):
                        ins = mm3(ps[:, 2 + g % 2, :], xnh[:, k, t], xnl[:, k, t], win_h[:, k, c],
                                  win_l[:, k, c], k, k == KD - 1)
                    ins.then_inc(gate_p.sem, 1)

                def decay(u):
                    pe.wait_ge(bhi.sem, bhi.at(i, u + 1))
                    pe.wait_ge(blo.sem, blo.at(i, u + 1))
                    if u >= 2:
                        pe.wait_ge(ex.sem, ex.at(i, u - 1))
                    nc.tensor.matmul(ps[:, u % 2, :], later[:], bh[:, u % 2].rearrange("p t h -> p (t h)"),
                                     start=True, stop=False)
                    nc.tensor.matmul(ps[:, u % 2, :], later[:], bl[:, u % 2].rearrange("p t h -> p (t h)"),
                                     start=False, stop=True).then_inc(seg.sem, 1)

                def within(u):
                    tt, q = divmod(u, UPT)
                    pe.wait_ge(mr.sem, mr.at(i, u + 1))
                    if q == 0 and tt:
                        pe.wait_ge(yc.sem, yc.at(i, tt))
                    pe.sem_inc(s_pass, 1)
                    for h in range(UH):
                        col = (q * UH + h) * HD
                        for c in range(2):
                            r = slice(c * CHUNK, (c + 1) * CHUNK)
                            ins = nc.tensor.matmul(ps[r, 2 + col // 512, col % 512:col % 512 + HD],
                                                   mu[r, u % 2, :, h], xdt[r, tt, col:col + HD],
                                                   start=True, stop=True)
                    ins.then_inc(yd.sem, 1)

                def states(tt):
                    for c in range(2):
                        r = slice(c * CHUNK, (c + 1) * CHUNK)
                        t = slice(tt * P + c * CHUNK, tt * P + (c + 1) * CHUNK)
                        if tt == 0 and c == 0:
                            pe.wait_ge(s0.sem, s0.at(i, 1))
                        else:
                            pe.wait_ge(su.sem, su.at(i, 2 * tt + c))
                        if tt and c == 0:
                            pe.wait_ge(yc.sem, yc.at(i, tt))
                        for a in range(2):
                            ins = nc.tensor.matmul(ps[r, 6 + a, :], cT[:, t], S[:, a * 512:(a + 1) * 512],
                                                   start=True, stop=True)
                        ins.then_inc(yo.sem, 1)
                        pe.wait_ge(xddr.sem, xddr.at(i, tt + 1))
                        for a in range(2):
                            ins = nc.tensor.matmul(ps[:, 4 + a, :], btok[r, tt, :], xdd[r, a * 512:(a + 1) * 512],
                                                   start=True, stop=True)
                        ins.then_inc(sn.sem, 1)

                pe.wait_ge(xtd.sem, xtd.at(i, NX))
                pe.wait_ge(gate_s.sem, gate_s.at(i, 2 * TT))
                pe.wait_ge(gmr.sem, gmr.at(i, 1))
                pe.wait_ge(ecd.sem, ecd.at(i, 1))
                decay(0)
                decay(1)
                for u in range(U):
                    within(u)
                    if u + 2 < U:
                        decay(u + 2)
                    if u % UPT == UPT - 1:
                        states(u // UPT)

                def out_proj(tt):
                    pe.wait_ge(hl.sem, hl.at(i, 2 * tt + 2))
                    if tt == 0:
                        pe.wait_ge(su.sem, su.at(i, 2 * TT))
                    if tt >= 2:
                        pe.wait_ge(x1r.sem, x1r.at(i, tt - 1))
                    for k in range(NX):
                        ins = mm3(ps[:, 4 + tt % 2, :], hth[:, tt % 2, k, :], htl[:, tt % 2, k, :],
                                  wout_h[:, k, :], wout_l[:, k, :], k, k == NX - 1)
                    ins.then_inc(op.sem, 1)

                for tt in range(TT):
                    pe.wait_ge(hgr.sem, hgr.at(i, tt + 1))
                    for a in range(2):
                        g = 2 * tt + a
                        if g >= 2:
                            pe.wait_ge(hl.sem, hl.at(i, g - 1))
                        for k in range(4):
                            c = (a * 4 + k) * P
                            ins = nc.tensor.transpose(ps[:, a, k * P:(k + 1) * P], gs[:, tt, c:c + P], ident[:])
                        ins.then_inc(ht.sem, 1)
                    if tt:
                        out_proj(tt - 1)
                out_proj(TT - 1)

                for lin in range(2):
                    n = KD if lin == 0 else 2
                    src = zn if lin == 0 else av
                    if lin == 0:
                        pe.wait_ge(znr.sem, znr.at(i, 2 * TT))
                    else:
                        pe.wait_ge(ar.sem, ar.at(i, TT))
                    for k in range(n):
                        g = k if lin == 0 else KD + k
                        if g == 0:
                            pe.wait_ge(hl.sem, hl.at(i, 2 * TT))
                        elif g == KD:
                            pe.wait_ge(qc.sem, qc.at(i, 2 * TT))
                        elif g >= 2 and g != KD + 1:
                            pe.wait_ge(t2r.sem, t2r.at(i, g - 1))
                        for tt in range(TT):
                            ins = nc.tensor.transpose(ps[:, g % 2, tt * P:(tt + 1) * P],
                                                      src[:, tt, k * P:(k + 1) * P], ident[:])
                        ins.then_inc(t2.sem, 1)
                    pe.wait_ge(sbr.sem, sbr.at(i, lin + 1))
                    for bank, v in ((2, sm), (3, sr)):
                        for k in range(n):
                            ins = nc.tensor.matmul(ps[:, bank, k * P:(k + 1) * P],
                                                   v[:, k:k + 1].to_broadcast([P, P]), ident[:],
                                                   start=True, stop=True)
                    ins.then_inc(sbp.sem, 1)
                    pe.wait_ge(wsr.sem, wsr.at(i, lin + 1))
                    if lin == 0:
                        pe.wait_ge(x1r.sem, x1r.at(i, TT))
                    else:
                        pe.wait_ge(wsb.sem, wsb.at(i, 1))
                    for k in range(TT):
                        ins = nc.tensor.matmul(ps[:, 5, k * P:(k + 1) * P],
                                               wsc[:, k:k + 1].to_broadcast([P, P]), ident[:],
                                               start=True, stop=True)
                    ins.then_inc(wsp.sem, 1)
                    for g in range(2 * TT):
                        pe.wait_ge(qr.sem, qr.at(i, 2 * TT * lin + g + 1))
                        if g == 0:
                            pe.wait_ge(t2r.sem, t2r.at(i, KD if lin == 0 else KD + 2))
                        if g >= 2:
                            pe.wait_ge(qc.sem, qc.at(i, 2 * TT * lin + g - 1))
                        q = qx if g % 2 == 0 else qw
                        for k in range(n):
                            ins = nc.tensor.transpose(ps[:, g % 2, k * 64:(k + 1) * 64].bitcast(BF16),
                                                      q[:, g // 2, k * P:(k + 1) * P], identb[:])
                        ins.then_inc(qt.sem, 1)
                    pe.wait_ge(qc.sem, qc.at(i, 2 * TT * (lin + 1)))
                    for tt in range(TT):
                        if lin == 0 and tt >= 2:
                            pe.wait_ge(hr.sem, hr.at(i, tt - 1))
                        if lin:
                            if tt < 2:
                                pe.wait_ge(hr.sem, hr.at(i, TT))
                            else:
                                pe.wait_ge(x2r.sem, x2r.at(i, tt - 1))
                        for k in range(n):
                            ins = nc.tensor.matmul(ps[:, 6 + tt % 2, :], qxT[:, k, tt * P:(tt + 1) * P],
                                                   qwT[:, k, :], start=(k == 0), stop=(k == n - 1))
                        ins.then_inc(qm.sem, 1)

                def logits(tt):
                    pe.wait_ge(t3f.sem, t3f.at(i, tt + 1))
                    for k in range(KD):
                        ins = nc.tensor.matmul(ps[:, 2, tt * E:(tt + 1) * E], zTf[:, tt % 2, k, :], rw[:, k, :],
                                               start=(k == 0), stop=(k == KD - 1))
                    ins.then_inc(lgp.sem, 1)

                for tt in range(TT):
                    turn(zn, 2 * TT, t3, tt, t3l)
                    if tt:
                        logits(tt - 1)
                logits(TT - 1)


def expert_pass(nc, gateT, upT, downT, x2_dram, zh_dram, zl_dram, wt_dram, out):
    STEPS = PAIR * B
    with ExitStack() as ctx:
        def sb(name, shape, dt=F32):
            return ctx.enter_context(nc.sbuf_tensor(name, shape, dt))

        def sem(name):
            return ctx.enter_context(nc.semaphore(name))

        counts = []

        def count(name, per):
            counts.append(Count(ctx, nc, name, per))
            return counts[-1]

        pp = ctx.enter_context(nc.psum_tensor("pp", [P, 8, 512], F32))
        acc = sb("acc", [P, NT, D])
        zh = sb("zh", [P, B, KD, L], BF16)
        zl = sb("zl", [P, B, KD, L], BF16)
        wts = sb("wts", [P, B, E, TT])
        wcur = sb("wcur", [P, 2, B, TT])
        guh = sb("guh", [P, PAIR, 2, KD, I], BF16)
        gul = sb("gul", [P, PAIR, 2, KD, I], BF16)
        dnh = sb("dnh", [P, PAIR, IC, D], BF16)
        dnl = sb("dnl", [P, PAIR, IC, D], BF16)
        stage = sb("stage", [P, 2, I])
        sgl = sb("sgl", [P, 2, L])
        hf = sb("hf", [P, 2, L])
        hhi = sb("hhi", [P, IC + 1, L], BF16)
        hlo = sb("hlo", [P, IC + 1, L], BF16)

        s_ld = sem("s_ld")
        s_out = sem("s_out")
        s_pass = sem("s_pass2")
        wl = [count(f"wl{s}", 16 * PAIR * PIECES // 2) for s in range(2)]
        wh = count("wh", PAIR * PIECES)
        wo = count("wo", PAIR * PIECES)
        gu = count("gu", STEPS * IC)
        sgr = count("sg_ready", STEPS * IC)
        hm = count("hm", STEPS * IC)
        hh = count("h_high", STEPS * IC)
        hl = count("h_low", STEPS * IC)
        dn = count("dn", STEPS * TT)
        ad = count("ad", STEPS * TT)
        wc = count("wc", PAIR)

        block = ctx.enter_context(nc.Block())

        def piece(expert, n):
            if n < 2 * KD:
                return (gateT if n < KD else upT)[expert, (n % KD) * P:(n % KD + 1) * P, :]
            k = 2 * (n - 2 * KD)
            return downT[expert, k * P:(k + 2) * P, :].rearrange("(k p) n -> p k n", p=P)

        def place(hi, par, n):
            if n < 2 * KD:
                return (guh if hi else gul)[:, par, n // KD, n % KD, :]
            k = 2 * (n - 2 * KD)
            return (dnh if hi else dnl)[:, par, k:k + 2, :].rearrange("p k n -> p (k n)")

        def staged(n):
            return stage[:, n % 2, :] if n < 2 * KD else stage[:, n % 2, :].rearrange("p (k n) -> p k n", k=2)

        def slot(step, c):
            return (IC if step % 2 else 0) if c == 0 else c

        AFTER = (2, 4, 6)
        FIRST = PIECES

        @block.sync
        def _(sp):
            for n in range(PIECES):
                if n >= 2:
                    sp.wait_ge(wo.sem, wo.per - FIRST + n - 1)
                sp.dma_start(staged(n), piece(0, n)).then_inc(wl[n % 2].sem, 16)
                if n == 1:
                    for b in range(B):
                        sp.dma_start(zh[:, b], zh_dram[b]).then_inc(s_ld, 16)
                        sp.dma_start(zl[:, b], zl_dram[b]).then_inc(s_ld, 16)
                        sp.dma_start(acc[:, b * TT:(b + 1) * TT, :], x2_dram[b]).then_inc(s_ld, 16)
                        sp.dma_start(wts[:, b].rearrange("p e t -> p (e t)"), wt_dram[b]).then_inc(s_ld, 16)
            with sp.Fori(0, E // PAIR) as i:
                for n in range(PAIR * PIECES):
                    sp.wait_ge(wo.sem, wo.at(i, n - 1))
                    sp.sem_inc(s_pass, 1)
                    nxt = i * PAIR + 1 if n < PIECES else (i * PAIR + 2) % E
                    sp.dma_start(staged(n % PIECES), piece(nxt, n % PIECES)).then_inc(wl[n % 2].sem, 16)
            sp.wait_ge(ad.sem, ad.per * (E // PAIR + 1))
            for b in range(B):
                sp.dma_start(out[b], acc[:, b * TT:(b + 1) * TT, :]).then_inc(s_out, 16)
            for s in range(2):
                sp.wait_ge(wl[s].sem, wl[s].per * (E // PAIR + 1))
            sp.wait_ge(s_out, 16 * B)

        @block.gpsimd
        def _(pool):
            for c in counts:
                less = {id(wl[0]): 16 * FIRST // 2, id(wl[1]): 16 * FIRST // 2, id(wh): FIRST, id(wo): FIRST}
                pool.sem_inc(c.sem, c.per - less.get(id(c), 0))

        @block.scalar
        def _(act):
            for n in range(PIECES):
                act.wait_ge(wl[n % 2].sem, wl[n % 2].per - 16 * FIRST // 2 + 16 * (n // 2 + 1))
                nc.scalar.activation(place(True, 0, n), stage[:, n % 2, :], ACT.Copy).then_inc(wh.sem, 1)
            with act.Fori(0, E // PAIR) as i:
                def high(step, c):
                    n = step * IC + c
                    act.wait_ge(hm.sem, hm.at(i, n + 1))
                    if c:
                        act.wait_ge(dn.sem, dn.at(i, TT * step))
                    nc.scalar.activation(hhi[:, slot(step, c), :], hf[:, n % 2, :], ACT.Copy).then_inc(hh.sem, 1)

                for step in range(STEPS):
                    par, tb = divmod(step, B)
                    for c in range(IC):
                        n = step * IC + c
                        act.wait_ge(gu.sem, gu.at(i, n + 1))
                        nc.scalar.activation(sgl[:, n % 2, :], pp[:, n % 2, :], ACT.Silu).then_inc(sgr.sem, 1)
                        if n:
                            high(*divmod(n - 1, IC))
                        if c in AFTER:
                            m = par * PIECES + tb * 3 + AFTER.index(c)
                            act.wait_ge(wl[m % 2].sem, wl[m % 2].at(i, 16 * (m // 2 + 1)))
                            if tb == 0:
                                act.wait_ge(dn.sem, dn.at(i, TT * step))
                            nc.scalar.activation(place(True, 1 - par, m % PIECES), stage[:, m % 2, :],
                                                 ACT.Copy).then_inc(wh.sem, 1)
                high(STEPS - 1, IC - 1)

        @block.vector
        def _(dve):
            for n in range(PIECES):
                dve.wait_ge(wh.sem, wh.per - FIRST + n + 1)
                nc.vector.tensor_tensor(place(False, 0, n), stage[:, n % 2, :], place(True, 0, n),
                                        ALU.subtract).then_inc(wo.sem, 1)
            dve.wait_ge(s_ld, 16 * 4 * B)
            with dve.Fori(0, E // PAIR) as i:
                dve.wait_ge(ad.sem, ad.at(i, 0))
                for par in range(PAIR):
                    nc.vector.tensor_copy(wcur[:, par], wts[:, :, bass.ds(i * PAIR + par, 1), :].rearrange(
                        "p b e t -> p b (e t)")).then_inc(wc.sem, 1)

                def low(step, c):
                    n = step * IC + c
                    dve.wait_ge(hh.sem, hh.at(i, n + 1))
                    nc.vector.tensor_tensor(hlo[:, slot(step, c), :], hf[:, n % 2, :], hhi[:, slot(step, c), :],
                                            ALU.subtract).then_inc(hl.sem, 1)

                def add(step):
                    par, tb = divmod(step, B)
                    for tt in range(TT):
                        dve.wait_ge(dn.sem, dn.at(i, step * TT + tt + 1))
                        a = acc[:, tb * TT + tt, :]
                        nc.vector.scalar_tensor_tensor(out=a, in0=pp[:, 4 + tt, :], scalar=wcur[:, par, tb, tt:tt + 1],
                                                       in1=a, op0=ALU.mult, op1=ALU.add).then_inc(ad.sem, 1)

                dve.wait_ge(wc.sem, wc.at(i, PAIR))
                for step in range(STEPS):
                    par, tb = divmod(step, B)
                    for c in range(IC):
                        n = step * IC + c
                        dve.wait_ge(sgr.sem, sgr.at(i, n + 1))
                        if n >= 2:
                            dve.wait_ge(hl.sem, hl.at(i, n - 1))
                        nc.vector.tensor_tensor(hf[:, n % 2, :], sgl[:, n % 2, :], pp[:, 2 + n % 2, :],
                                                ALU.mult).then_inc(hm.sem, 1)
                        if n:
                            low(*divmod(n - 1, IC))
                        if c == 0 and step:
                            add(step - 1)
                        if c in AFTER:
                            m = par * PIECES + tb * 3 + AFTER.index(c)
                            dve.wait_ge(wh.sem, wh.at(i, m + 1))
                            nc.vector.tensor_tensor(place(False, 1 - par, m % PIECES), stage[:, m % 2, :],
                                                    place(True, 1 - par, m % PIECES),
                                                    ALU.subtract).then_inc(wo.sem, 1)
                low(STEPS - 1, IC - 1)
                add(STEPS - 1)

        @block.tensor
        def _(pe):
            pe.wait_ge(s_ld, 16 * 4 * B)
            with pe.Fori(0, E // PAIR) as i:
                def gate_up(step, c):
                    par, tb = divmod(step, B)
                    n = step * IC + c
                    if c == 0 and tb == 0:
                        pe.wait_ge(wo.sem, wo.at(i, PIECES * par))
                    pe.wait_ge(hm.sem, hm.at(i, n - 1))
                    for j in range(2):
                        for k in range(KD):
                            w = slice(c * P, (c + 1) * P)
                            dst = pp[:, 2 * j + n % 2, :]
                            nc.tensor.matmul(dst, guh[:, par, j, k, w], zh[:, tb, k, :], start=(k == 0), stop=False)
                            nc.tensor.matmul(dst, guh[:, par, j, k, w], zl[:, tb, k, :], start=False, stop=False)
                            ins = nc.tensor.matmul(dst, gul[:, par, j, k, w], zh[:, tb, k, :], start=False,
                                                   stop=(k == KD - 1))
                    ins.then_inc(gu.sem, 1)

                def down(step):
                    par, tb = divmod(step, B)
                    pe.wait_ge(hl.sem, hl.at(i, (step + 1) * IC))
                    for tt in range(TT):
                        pe.wait_ge(ad.sem, ad.at(i, step * TT + tt + 1 - TT))
                        t = slice(tt * P, (tt + 1) * P)
                        for c in range(IC):
                            s = slot(step, c)
                            dst = pp[:, 4 + tt, :]
                            nc.tensor.matmul(dst, hhi[:, s, t], dnh[:, par, c, :], start=(c == 0), stop=False)
                            nc.tensor.matmul(dst, hhi[:, s, t], dnl[:, par, c, :], start=False, stop=False)
                            ins = nc.tensor.matmul(dst, hlo[:, s, t], dnh[:, par, c, :], start=False,
                                                   stop=(c == IC - 1))
                        ins.then_inc(dn.sem, 1)

                gate_up(0, 0)
                for step in range(STEPS):
                    for c in range(1, IC):
                        gate_up(step, c)
                    if step + 1 < STEPS:
                        gate_up(step + 1, 0)
                    down(step)


def kernel(**inputs):
    import numpy as np
    import concourse.bacc as bacc
    from concourse.bass_utils import run_bass_kernel_spmd

    def tiles(a):
        b, r, n = a.shape
        return a.reshape(b, r // P, P, n).transpose(0, 2, 1, 3)

    def rows(v):
        return v.reshape(1, -1)

    f = inputs["fside_BxS2xS2_0"]
    c = inputs["ctx_1024"]
    a = {k.replace("L0_attn_", "").replace("L0_ffn_", ""): np.asarray(v) for k, v in inputs.items()}
    f, c = np.asarray(f), np.asarray(c)
    arrays = {
        "x": tiles(a["x"]),
        "guw": tiles(f),
        "guwT": tiles(f.transpose(0, 2, 1)),
        "dnw": tiles(c),
        "dnwT": tiles(c.transpose(0, 2, 1)),
        "winT": a["in_proj_w"].T,
        "conv_w": a["conv_w"].reshape(NCC, P, KC).transpose(1, 0, 2),
        "conv_b": a["conv_b"].reshape(NCC, P).T,
        "dt_bias": rows(a["dt_bias"]),
        "a_log": rows(a["A_log"]),
        "d_skip": rows(a["D"]),
        "norm_w": a["norm_w"].reshape(NX, P).T,
        "woutT": a["out_proj_w"].T,
        "rwT": a["router_w"].T.reshape(KD, P, E).transpose(1, 0, 2),
        "gateT": a["gate_w"].transpose(0, 2, 1),
        "upT": a["up_w"].transpose(0, 2, 1),
        "downT": a["down_w"].transpose(0, 2, 1),
    }
    arrays = {f"in_{k}": np.ascontiguousarray(v) for k, v in arrays.items()}
    nc = bacc.Bacc("TRN2", target_bir_lowering=False, num_devices=1)
    args = [nc.dram_tensor(k, v.shape, mybir.dt.from_np(v.dtype), kind="ExternalInput").ap()
            for k, v in arrays.items()]
    out = nc.dram_tensor("out", [B, P, TT, D], F32, kind="ExternalOutput").ap()
    decoder_layer(nc, *args, out)
    r = run_bass_kernel_spmd(nc, [arrays], core_ids=[0])
    return r.results[0]["out"].reshape(B, P, TT, D).transpose(0, 2, 1, 3).reshape(B, L, D)
```

```python
from contextlib import ExitStack

import concourse.bass as bass
from concourse import mybir

F32 = mybir.dt.float32
BF16 = mybir.dt.bfloat16
ALU = mybir.AluOpType
ACT = mybir.ActivationFunctionType
AX = mybir.AxisListType

P = 128
B, L, D = 4, 512, 512
TT = L // P
KD = D // P
DIN, HEADS, HD, N, CHUNK, KC = 1024, 64, 16, 128, 64, 4
CONV = DIN + 2 * N
PROJ = DIN + CONV + HEADS
NCC = CONV // P
NX = DIN // P
DTC = DIN + CONV
UH = 8
UPT = HEADS // UH
U = TT * UPT
IQ = 256
E, I = 8, 1024
EPS = 1e-5
QEPS, QMAX, MAGIC = 1e-6, 127.0, 12582912.0
TOP_P = 0.9
NT = B * TT
PAIR = 2
PIECES = 12
IC = I // P
XSTEPS = NCC + 3
QSTEPS = 18
MERGED = sorted([("x", j, (j + 0.5) / XSTEPS) for j in range(XSTEPS)]
                + [("q", j, (j + 0.4) / QSTEPS) for j in range(QSTEPS)], key=lambda v: v[2])
MERGED = [(what, j) for what, j, _ in MERGED]
CONSTS = 22


class Count:

    def __init__(self, ctx, nc, name, per):
        self.sem, self.per = ctx.enter_context(nc.semaphore(name)), per

    def at(self, i, k):
        return i * self.per + (self.per + k)

    def before(self, i, k):
        return i * self.per + k


class Own:

    def __init__(self, count, eng, i):
        self.c, self.eng, self.i, self.n = count, eng, i, 0

    def link(self, ins):
        self.n += 1
        ins.then_inc(self.c.sem, 1)
        self.eng.wait_ge(self.c.sem, self.c.at(self.i, self.n))

    def close(self):
        assert self.n <= self.c.per, self.n
        if self.n < self.c.per:
            self.eng.sem_inc(self.c.sem, self.c.per - self.n)


def decoder_layer(nc, x, guw, guwT, dnw, dnwT, winT, conv_w, conv_b, dt_bias, a_log, d_skip,
                  norm_w, woutT, rwT, gateT, upT, downT, out):
    x2_dram = nc.dram_tensor("x2_dram", [B, P, TT, D], F32, kind="Internal").ap()
    zh_dram = nc.dram_tensor("zh_dram", [B, TT, P, KD, P], BF16, kind="Internal").ap()
    zl_dram = nc.dram_tensor("zl_dram", [B, TT, P, KD, P], BF16, kind="Internal").ap()
    wt_dram = nc.dram_tensor("wt_dram", [B, P, E * TT], F32, kind="Internal").ap()
    first_pass(nc, x, guw, guwT, dnw, dnwT, winT, conv_w, conv_b, dt_bias, a_log, d_skip,
               norm_w, woutT, rwT, x2_dram, zh_dram, zl_dram, wt_dram)
    expert_pass(nc, gateT, upT, downT, x2_dram, zh_dram, zl_dram, wt_dram, out)


def first_pass(nc, x, guw, guwT, dnw, dnwT, winT, conv_w, conv_b, dt_bias, a_log, d_skip,
               norm_w, woutT, rwT, x2_dram, zh_dram, zl_dram, wt_dram):
    with ExitStack() as ctx:
        def sb(name, shape, dt=F32):
            return ctx.enter_context(nc.sbuf_tensor(name, shape, dt))

        def sem(name):
            return ctx.enter_context(nc.semaphore(name))

        counts = []

        def count(name, per):
            counts.append(Count(ctx, nc, name, per))
            return counts[-1]

        ps = ctx.enter_context(nc.psum_tensor("ps", [P, 8, 512], F32))

        win_h = sb("win_h", [P, KD, PROJ], BF16)
        win_l = sb("win_l", [P, KD, PROJ], BF16)
        wout_h = sb("wout_h", [P, NX, D], BF16)
        wout_l = sb("wout_l", [P, NX, D], BF16)
        rw = sb("rw", [P, KD, E])
        cw = sb("cw", [P, NCC, KC])
        cb = sb("cb", [P, NCC])
        dtb_bc = sb("dtb_bc", [P, HEADS])
        alog_bc = sb("alog_bc", [P, HEADS])
        expa_bc = sb("expa_bc", [P, HEADS])
        dcol = sb("dcol", [P, NX])
        nw = sb("nw", [P, NX])
        ident = sb("ident", [P, P])
        identb = sb("identb", [P, P], BF16)
        later = sb("later", [P, P], BF16)
        upto = sb("upto", [P, CHUNK, UH], BF16)
        incl = sb("incl", [P, P])
        in_a = sb("in_a", [P, P])
        in_b = sb("in_b", [P, P])
        gmask = sb("gmask", [P, CHUNK])
        tie = sb("tie", [P, E, E])
        xc = sb("xc", [P, TT, D])
        zn = sb("zn", [P, TT, D])
        st6 = sb("st6", [P, TT, 6])
        mv = sb("mv", [P, TT, 2])
        ve = sb("ve", [P, TT])
        sd = sb("sd", [P, TT])
        r0 = sb("r0", [P, TT])
        r1 = sb("r1", [P, TT])
        rs = sb("rs", [P, TT])
        ssq = sb("ssq", [P, TT])
        xin = sb("xin", [P, TT, D])
        mvx = sb("mvx", [P, TT, 2])
        vex = sb("vex", [P, TT])
        sdx = sb("sdx", [P, TT])
        rsx = sb("rsx", [P, TT])
        xnh = sb("xnh", [P, KD, L], BF16)
        xnl = sb("xnl", [P, KD, L], BF16)
        xraw = sb("xraw", [P, 2, KC - 1 + L])
        cacc = sb("cacc", [P, 2, L])
        bT = sb("bT", [P, L])
        cT = sb("cT", [P, L])
        btok = sb("btok", [P, TT, N])
        big = sb("big", [P, 3 * TT * DIN])
        xall = big[:, 0:NX * L].rearrange("p (k t) -> p k t", k=NX)
        xdt = big[:, TT * DIN:2 * TT * DIN].rearrange("p (t c) -> p t c", t=TT)
        gs = big[:, 2 * TT * DIN:3 * TT * DIN].rearrange("p (t c) -> p t c", t=TT)
        dtv = sb("dtv", [P, TT, HEADS])
        dta = sb("dta", [P, TT, HEADS])
        dte = sb("dte", [P, TT, HEADS])
        dt = sb("dt", [P, TT, HEADS])
        da = sb("da", [P, TT, HEADS])
        dah = sb("dah", [P, TT, HEADS], BF16)
        dal = sb("dal", [P, TT, HEADS], BF16)
        S = sb("S", [P, DIN])
        edec = sb("edec", [P, 2, TT, HEADS])
        cdec = sb("cdec", [P, 2, TT, HEADS])
        gm = sb("gm", [P, TT, CHUNK])
        scr = sb("scr", [P, 6656])
        bh = scr[:, 0:512].bitcast(BF16).rearrange("p (b t h) -> p b t h", b=2, t=CHUNK)
        bl = scr[:, 512:1024].bitcast(BF16).rearrange("p (b t h) -> p b t h", b=2, t=CHUNK)
        mu = scr[:, 2048:4096].bitcast(BF16).rearrange("p (s b c t h) -> p s b c t h", s=2, b=2, c=2, t=CHUNK)
        xdd = scr[:, 4096:5120]
        y = scr[:, 5120:6144]
        junk = scr[:, 6144:6656].bitcast(BF16)
        hth = scr[:, 0:1024].bitcast(BF16).rearrange("p (b k t) -> p b k t", b=2, k=NX)
        htl = scr[:, 1024:2048].bitcast(BF16).rearrange("p (b k t) -> p b k t", b=2, k=NX)
        qxT = scr[:, 0:1024].bitcast(BF16).rearrange("p (k t) -> p k t", k=KD)
        qwT = scr[:, 1024:2048].bitcast(BF16).rearrange("p (k t) -> p k t", k=KD)
        wnat = scr[:, 2048:4096].rearrange("p (t d) -> p t d", t=TT)
        w2nat = scr[:, 2048:3072].rearrange("p (t d) -> p t d", t=TT)
        w2Tr = scr[:, 3072:4096].rearrange("p (t d) -> p t d", t=2)
        wTr = scr[:, 4096:6144].rearrange("p (t d) -> p t d", t=TT)
        qx = scr[:, 4096:5120].bitcast(BF16).rearrange("p (t d) -> p t d", t=TT)
        qw = scr[:, 5120:6144].bitcast(BF16).rearrange("p (t d) -> p t d", t=TT)
        wscb = scr[:, 6144:6656]
        axm = sb("axm", [P, KD])
        awm = sb("awm", [P, KD])
        ra = sb("ra", [P, KD])
        sm = sb("sm", [P, KD])
        sq0 = sb("sq0", [P, KD])
        sr = sb("sr", [P, KD])
        xsc = sb("xsc", [P, TT])
        wsc = sb("wsc", [P, TT])
        rx = sb("rx", [P, TT])
        rw_ = sb("rw_", [P, TT])
        hq = sb("hq", [P, 2, D])
        sg = sb("sg", [P, 2, IQ])
        av = zn[:, :, 0:IQ]
        eu = [v.rearrange("p (t h) -> p t h", t=CHUNK) for v in (scr[:, 1024:1536], scr[:, 1536:2048], hq[:, 0, :])]
        xsp = zn[:].rearrange("p t d -> p (t d)").bitcast(BF16).rearrange("p (b s c) -> p b s c", b=2, s=2)
        zTf = sb("zTf", [P, KD, P])
        z3h = sb("z3h", [P, 2, KD, P], BF16)
        z3l = sb("z3l", [P, 2, KD, P], BF16)
        mx = sb("mx", [P, TT])
        lg = sb("lg", [P, TT, E])
        pe_ = sb("pe_", [P, TT, E])
        pr = sb("pr", [P, TT, E])
        gt = scr[:, 4096:4352].rearrange("p (t a b) -> p t a b", t=TT, a=E)
        eq = scr[:, 4352:4608].rearrange("p (t a b) -> p t a b", t=TT, a=E)
        sums = sb("sums", [P, TT])
        mass = sb("mass", [P, TT, E])
        keep = sb("keep", [P, TT, E])
        wt = sb("wt", [P, E, TT])

        s_win = sem("s_win")
        s_wsplit = sem("s_wsplit")
        s_wout = sem("s_wout")
        s_wsc = sem("s_wsc")
        s_small = sem("s_small")
        s_const = sem("s_const")
        s_wh = sem("s_wh")
        s_wl = sem("s_wl")
        s_expa = sem("s_expa")
        s_pass = sem("s_pass")
        ldx = count("ldx", 16)
        ldc = count("ldc", 16)
        ldq = count("ldq", 32)
        ldq2 = count("ldq2", 32)
        stx = count("stx", 16)
        stz = [count(f"stz{b}", 64) for b in range(2)]
        stw = count("stw", 16)
        own_v = count("own_v", 130)
        own_x = count("own_x", 40)
        own_a = count("own_a", 8)
        var_x = count("var_x", 1)
        std_x = count("std_x", 1)
        zxr = count("zxr", TT)
        var_in = count("var_in", 3)
        std_out = count("std_out", 3)
        znr = count("znr", 2 * TT)
        t1 = count("t1", TT)
        t1h = count("t1h", TT)
        t1l = count("t1l", TT)
        pj = count("pj", NCC)
        raw = count("raw", NCC)
        cv = count("cv", NCC)
        act_x = count("act_x", NCC)
        xt = count("xt", NX + 1)
        xta = count("xta", NX + 1)
        xtd = count("xtd", NX)
        dtp = count("dtp", 1)
        v_in = count("v_in", 1)
        sp_out = count("sp_out", 1)
        dar = count("dar", 1)
        cum = count("cum", 2)
        ecd = count("ecd", 2)
        gp = count("gp", 1)
        gmr = count("gmr", 1)
        gate_p = count("gate_p", 2 * TT)
        gate_e = count("gate_e", 2 * TT)
        gate_s = count("gate_s", TT)
        bhi = count("bhi", U)
        blo = count("blo", U)
        seg = count("seg", U)
        ex = count("ex", U)
        prd = count("prd", U)
        mhr = count("mhr", U)
        mr = count("mr", U)
        xhr = count("xhr", TT)
        xlr = count("xlr", TT)
        yd = count("yd", U)
        xddr = count("xddr", TT)
        yo = count("yo", 2 * TT)
        sn = count("sn", 4 * TT)
        su = count("su", 4 * TT)
        s0 = count("s0", 1)
        ysc = count("ysc", TT)
        yc = count("yc", 2 * TT)
        hgr = count("hgr", TT)
        sqr = count("sqr", TT)
        ht = count("ht", 2 * TT)
        hh = count("hh", 2 * TT)
        hl = count("hl", 2 * TT)
        op = count("op", TT)
        x1r = count("x1r", TT)
        t2 = count("t2", KD + 2)
        t2r = count("t2r", KD + 2)
        rat = count("rat", 2)
        sqt = count("sqt", 2)
        sbr = count("sbr", 2)
        sbp = count("sbp", 2)
        wsr = count("wsr", 2)
        wsp = count("wsp", 2)
        wsb = count("wsb", 2)
        qr = count("qr", 4 * TT)
        qt = count("qt", 4 * TT)
        qc = count("qc", 4 * TT)
        qm = count("qm", 2 * TT)
        hr = count("hr", TT)
        sgr = count("sgr", TT)
        ar = count("ar", TT)
        x2r = count("x2r", TT)
        t3 = count("t3", TT)
        t3f = count("t3f", TT)
        t3h = count("t3h", TT)
        t3l = count("t3l", TT)
        lgp = count("lgp", TT)
        lgi = count("lgi", 1)
        lge = count("lge", 1)
        wtr = count("wtr", 1)

        def rows(eng, take_x, scan, put_out):
            for j in range(XSTEPS):
                take_x(0, j)
            with eng.Fori(0, B - 1) as i:
                scan(i)
                for what, j in MERGED:
                    if what == "x":
                        take_x(i + 1, j)
                    else:
                        put_out(i, j)
            scan(B - 1)
            for j in range(QSTEPS):
                put_out(B - 1, j)

        block = ctx.enter_context(nc.Block())

        @block.sync
        def _(sp):
            sp.dma_start(big[:, 0:KD * PROJ].rearrange("p (k n) -> p k n", k=KD),
                         winT.rearrange("(k p) n -> p k n", p=P)).then_inc(s_win, 16)
            for dst, src in ((rw[:], rwT), (cw[:], conv_w), (cb[:], conv_b), (nw[:], norm_w),
                             (dtb_bc[:], dt_bias.to_broadcast([P, HEADS])),
                             (alog_bc[:], a_log.to_broadcast([P, HEADS])),
                             (dcol[:], d_skip)):
                sp.dma_start(dst, src).then_inc(s_small, 16)
            sp.dma_start(xin[:], x[0]).then_inc(ldx.sem, 16)
            sp.wait_ge(s_wl, 1)
            sp.dma_start(big[:, 0:NX * D].rearrange("p (k n) -> p k n", k=NX),
                         woutT.rearrange("(k p) n -> p k n", p=P)).then_inc(s_wout, 16)

            def row(i, more):
                sp.wait_ge(stx.sem, stx.before(i, 16))
                sp.wait_ge(znr.sem, znr.before(i, 2 * TT))
                sp.sem_inc(s_pass, 1)
                sp.dma_start(xc[:], x[i]).then_inc(ldc.sem, 16)
                if more:
                    sp.wait_ge(t1.sem, t1.at(i, TT))
                    sp.sem_inc(s_pass, 1)
                    sp.dma_start(xin[:], x[i + 1]).then_inc(ldx.sem, 16)
                sp.wait_ge(su.sem, su.at(i, 4 * TT))
                sp.wait_ge(sqr.sem, sqr.at(i, TT))
                sp.sem_inc(s_pass, 1)
                sp.dma_start(wnat, guw[i]).then_inc(ldq.sem, 16)
                sp.dma_start(wTr, guwT[i]).then_inc(ldq.sem, 16)
                sp.wait_ge(qr.sem, qr.at(i, 2 * TT))
                sp.sem_inc(s_pass, 1)
                sp.dma_start(w2nat, dnw[i]).then_inc(ldq2.sem, 16)
                sp.dma_start(w2Tr, dnwT[i]).then_inc(ldq2.sem, 16)
                sp.wait_ge(x2r.sem, x2r.at(i, TT))
                sp.sem_inc(s_pass, 1)
                sp.dma_start(x2_dram[i], xc[:]).then_inc(stx.sem, 16)
                for tt in range(TT):
                    sp.wait_ge(t3l.sem, t3l.at(i, tt + 1))
                    sp.sem_inc(s_pass, 1)
                    sp.dma_start(zh_dram[i, tt], z3h[:, tt % 2]).then_inc(stz[tt % 2].sem, 16)
                    sp.dma_start(zl_dram[i, tt], z3l[:, tt % 2]).then_inc(stz[tt % 2].sem, 16)
                sp.wait_ge(wtr.sem, wtr.at(i, 1))
                sp.sem_inc(s_pass, 1)
                sp.dma_start(wt_dram[i], wt[:].rearrange("p e t -> p (e t)")).then_inc(stw.sem, 16)

            with sp.Fori(0, B - 1) as i:
                row(i, True)
            row(B - 1, False)
            for c in (stx, stz[0], stz[1], stw):
                sp.wait_ge(c.sem, c.per * (B + 1))

        @block.gpsimd
        def _(pool):
            for c in counts:
                pool.sem_inc(c.sem, c.per)
            done = [0]

            def step(ins):
                done[0] += 1
                ins.then_inc(s_const, 1)
                pool.wait_ge(s_const, done[0])

            def select(view, op, fill, pattern, mult):
                step(nc.gpsimd.affine_select(out=view, in_=view, compare_op=op, fill=fill, base=0,
                                             pattern=pattern, channel_multiplier=mult))

            for t, v in ((ident, 0.0), (identb, 0.0), (later, 0.0), (incl, 0.0),
                         (upto, 1.0), (gmask, 1.0), (tie, 1.0), (in_a, 0.0), (in_b, 0.0)):
                step(nc.gpsimd.memset(t[:], v))
            for t in (ident, identb):
                select(t[:], ALU.not_equal, 1.0, [[-1, P]], 1)
            select(tie[:], ALU.is_gt, 0.0, [[1, E], [-1, E]], 0)
            step(nc.gpsimd.memset(in_a[0:CHUNK, :], 1.0))
            step(nc.gpsimd.memset(in_b[CHUNK:P, :], 1.0))
            for h in (0, CHUNK):
                r = slice(h, h + CHUNK)
                select(later[r, r], ALU.is_ge, 1.0, [[1, CHUNK]], -1)
                select(incl[r, r], ALU.is_gt, 1.0, [[-1, CHUNK]], 1)
                select(upto[r], ALU.is_ge, 0.0, [[1, CHUNK], [0, UH]], -1)
                select(gmask[r], ALU.is_ge, 0.0, [[1, CHUNK]], -1)
            assert done[0] == CONSTS
            pool.wait_ge(s_small, 7 * 16)

            def scan(i):
                pool.wait_ge(x2r.sem, x2r.before(i, TT))
                pool.wait_ge(wtr.sem, wtr.before(i, 1))

                def low(u):
                    tt, q = divmod(u, UPT)
                    if u >= 2:
                        pool.wait_ge(seg.sem, seg.at(i, u - 1))
                    nc.gpsimd.tensor_tensor(
                        bl[:, u % 2], dal[:, tt, q * UH:(q + 1) * UH].unsqueeze(1).to_broadcast([P, CHUNK, UH]),
                        upto[:], ALU.mult).then_inc(blo.sem, 1)

                def to_end(tt):
                    if tt:
                        pool.wait_ge(sn.sem, sn.at(i, 4 * tt))
                    nc.gpsimd.tensor_tensor(
                        xdd[:].rearrange("p (h d) -> p h d", h=HEADS),
                        xdt[:, tt, :].rearrange("p (h d) -> p h d", h=HEADS),
                        edec[:, 1, tt, :].unsqueeze(2).to_broadcast([P, HEADS, HD]),
                        ALU.mult).then_inc(xddr.sem, 1)

                def gated(tt):
                    pool.wait_ge(yc.sem, yc.at(i, 2 * tt + 2))
                    pool.wait_ge(gate_s.sem, gate_s.at(i, tt + 1))
                    nc.gpsimd.tensor_tensor(gs[:, tt, :], y[:], gs[:, tt, :], ALU.mult).then_inc(hgr.sem, 1)

                def x_low(tt):
                    pool.wait_ge(xhr.sem, xhr.at(i, tt + 1))
                    nc.gpsimd.tensor_tensor(xsp[:, tt % 2, 1, :], xdt[:, tt, :], xsp[:, tt % 2, 0, :],
                                            ALU.subtract).then_inc(xlr.sem, 1)

                pool.wait_ge(dar.sem, dar.at(i, 1))
                low(0)
                low(1)
                pool.wait_ge(ecd.sem, ecd.at(i, 1))
                pool.wait_ge(xtd.sem, xtd.at(i, NX))
                x_low(0)
                low(2)
                to_end(0)
                for u in range(U):
                    tt, q = divmod(u, UPT)
                    if u + 3 < U:
                        low(u + 3)
                    if q == 3 and tt:
                        gated(tt - 1)
                    if q == 4 and tt + 1 < TT:
                        x_low(tt + 1)
                    if q == 6 and tt + 1 < TT:
                        to_end(tt + 1)
                gated(TT - 1)

            with pool.Fori(0, B) as i:
                scan(i)

        @block.scalar
        def _(act):
            act.wait_ge(s_win, 16)
            nc.scalar.activation(win_h[:].rearrange("p k n -> p (k n)"), big[:, 0:KD * PROJ],
                                 ACT.Copy).then_inc(s_wh, 1)
            act.wait_ge(s_small, 7 * 16)
            nc.scalar.activation(expa_bc[:], alog_bc[:], ACT.Exp).then_inc(s_expa, 1)
            act.wait_ge(s_wsc, NX)
            nc.scalar.activation(wout_h[:].rearrange("p k n -> p (k n)"), big[:, 0:NX * D],
                                 ACT.Copy).then_inc(s_wh, 1)

            def take_x(i, j):
                def conv_in(n):
                    cc = (n + NX) if n < 2 else n - 2
                    act.wait_ge(pj.sem, pj.at(i, n + 1))
                    if n >= 2:
                        act.wait_ge(cv.sem, cv.at(i, n - 1))
                        act.wait_ge(act_x.sem, act_x.at(i, n - 1))
                    nc.scalar.activation(xraw[:, n % 2, KC - 1:], ps[:, 2 + n % 2, :], ACT.Copy)
                    nc.scalar.activation(cacc[:, n % 2, :], ps[:, 2 + n % 2, :], ACT.Identity,
                                         bias=cb[:, cc:cc + 1],
                                         scale=cw[:, cc, KC - 1:KC]).then_inc(raw.sem, 1)

                def conv_out(n):
                    act.wait_ge(cv.sem, cv.at(i, n + 1))
                    dst = (bT[:], cT[:])[n] if n < 2 else xall[:, n - 2, :]
                    nc.scalar.activation(dst, cacc[:, n % 2, :], ACT.Silu).then_inc(act_x.sem, 1)

                def back(j):
                    act.wait_ge(xt.sem, xt.at(i, j + 1))
                    if j == 0:
                        nc.scalar.activation(btok[:], ps[:, 0, :].rearrange("p (t c) -> p t c", t=TT),
                                             ACT.Copy).then_inc(xta.sem, 1)
                    else:
                        nc.scalar.activation(xall[:, j - 1, :], xall[:, j - 1, :], ACT.Identity,
                                             scale=dcol[:, j - 1:j]).then_inc(xta.sem, 1)

                if j == 0:
                    act.wait_ge(su.sem, su.before(i, 4 * TT))
                    act.wait_ge(hgr.sem, hgr.before(i, TT))
                    act.wait_ge(var_x.sem, var_x.at(i, 1))
                    nc.scalar.activation(sdx[:], vex[:], ACT.Sqrt).then_inc(std_x.sem, 1)
                    for tt in range(TT):
                        act.wait_ge(t1.sem, t1.at(i, tt + 1))
                        nc.scalar.activation(xnh[:, :, tt * P:(tt + 1) * P],
                                             ps[:, tt % 2, :].rearrange("p (k t) -> p k t", k=KD),
                                             ACT.Copy).then_inc(t1h.sem, 1)
                elif j <= NCC:
                    n = j - 1
                    conv_in(n)
                    if n == 1:
                        act.wait_ge(v_in.sem, v_in.at(i, 1))
                        own = Own(own_a, act, i)
                        own.link(nc.scalar.activation(dte[:], dta[:], ACT.Exp, scale=-1.0))
                        nc.scalar.activation(dte[:], dte[:], ACT.Ln, bias=1.0).then_inc(sp_out.sem, 1)
                        own.close()
                        act.wait_ge(cum.sem, cum.at(i, 1))
                        nc.scalar.activation(edec[:].rearrange("p c t h -> p (c t h)"), ps[:, 4, :],
                                             ACT.Exp).then_inc(ecd.sem, 1)
                    if n == 2:
                        act.wait_ge(cum.sem, cum.at(i, 2))
                        nc.scalar.activation(cdec[:].rearrange("p c t h -> p (c t h)"), ps[:, 4, :],
                                             ACT.Exp).then_inc(ecd.sem, 1)
                    if n >= 1:
                        conv_out(n - 1)
                    if n == 3:
                        back(0)
                    if n >= 4:
                        back(n - 3)
                elif j == NCC + 1:
                    conv_out(NCC - 1)
                    back(NX - 1)
                elif j == NCC + 2:
                    back(NX)

            def scan(i):
                def square(tt):
                    act.wait_ge(hgr.sem, hgr.at(i, tt + 1))
                    if tt:
                        act.wait_ge(sqr.sem, sqr.at(i, tt))
                    nc.scalar.activation(junk, gs[:, tt, :], ACT.Square,
                                         accum_out=ssq[:, tt:tt + 1]).then_inc(sqr.sem, 1)

                def gate_out(g):
                    act.wait_ge(gate_p.sem, gate_p.at(i, g + 1))
                    nc.scalar.activation(gs[:, g // 2, (g % 2) * 512:(g % 2 + 1) * 512], ps[:, 5, :],
                                         ACT.Copy).then_inc(gate_e.sem, 1)

                def gate_silu(tt):
                    act.wait_ge(gate_e.sem, gate_e.at(i, 2 * tt + 2))
                    nc.scalar.activation(gs[:, tt, :], gs[:, tt, :], ACT.Silu).then_inc(gate_s.sem, 1)

                def decays(u):
                    act.wait_ge(seg.sem, seg.at(i, u + 1))
                    if u >= 3:
                        act.wait_ge(mr.sem, mr.at(i, u - 2))
                    nc.scalar.activation(eu[u % 3].rearrange("p t h -> p (t h)"), ps[:, u % 2, :],
                                         ACT.Exp).then_inc(ex.sem, 1)

                def high(u):
                    act.wait_ge(prd.sem, prd.at(i, u + 1))
                    if u >= 2:
                        act.wait_ge(yd.sem, yd.at(i, u - 1))
                    for c in range(2):
                        r = slice(c * CHUNK, (c + 1) * CHUNK)
                        ins = nc.scalar.activation(mu[r, 0, u % 2, c], eu[u % 3][r], ACT.Copy)
                    ins.then_inc(mhr.sem, 1)

                def x_high(tt):
                    if tt >= 2:
                        act.wait_ge(yd.sem, yd.at(i, (tt - 1) * UPT))
                    nc.scalar.activation(xsp[:, tt % 2, 0, :], xdt[:, tt, :], ACT.Copy).then_inc(xhr.sem, 1)

                act.wait_ge(x2r.sem, x2r.before(i, TT))
                act.wait_ge(t3.sem, t3.before(i, TT))
                act.wait_ge(xtd.sem, xtd.at(i, NX))
                x_high(0)
                decays(0)
                decays(1)
                high(0)
                for u in range(U):
                    tt, q = divmod(u, UPT)
                    if u + 2 < U:
                        decays(u + 2)
                    if u + 1 < U:
                        high(u + 1)
                    if q == 2 and tt + 1 < TT:
                        x_high(tt + 1)
                    if u == 0:
                        act.wait_ge(ht.sem, ht.before(i, 2 * TT))
                    if q % 4 == 3:
                        gate_out(u // 4)
                    if q == 1 and tt:
                        gate_silu(tt - 1)
                    if q == 6 and tt:
                        square(tt - 1)
                gate_silu(TT - 1)
                square(TT - 1)

            def put_out(i, j):
                def root(k):
                    act.wait_ge(var_in.sem, var_in.at(i, k + 1))
                    nc.scalar.activation(sd[:], ve[:], ACT.Sqrt).then_inc(std_out.sem, 1)

                lin = j >= 10
                n = 2 if lin else KD
                if j < TT:
                    if j == 0:
                        act.wait_ge(su.sem, su.at(i, 4 * TT))
                        act.wait_ge(sqr.sem, sqr.at(i, TT))
                    for g in (2 * j, 2 * j + 1):
                        act.wait_ge(ht.sem, ht.at(i, g + 1))
                        if g >= 4:
                            act.wait_ge(op.sem, op.at(i, g // 2 - 1))
                        nc.scalar.activation(hth[:, g // 2 % 2, (g % 2) * 4:(g % 2) * 4 + 4, :],
                                             ps[:, 5 + g % 2, :].rearrange("p (k t) -> p k t", k=4),
                                             ACT.Copy).then_inc(hh.sem, 1)
                    if j == 0:
                        root(0)
                elif j == 4:
                    root(1)
                elif j in (5, 10):
                    act.wait_ge(rat.sem, rat.at(i, lin + 1))
                    nc.scalar.activation(sq0[:, 0:n], ra[:, 0:n], ACT.Sqrt).then_inc(sqt.sem, 1)
                elif j in (7, 12):
                    act.wait_ge(wsp.sem, wsp.at(i, lin + 1))
                    if lin:
                        act.wait_ge(hr.sem, hr.at(i, TT))
                    nc.scalar.activation(wscb, ps[:, 7, :], ACT.Copy).then_inc(wsb.sem, 1)
                elif j in (8, 13):
                    for g in range(2 * TT):
                        act.wait_ge(qt.sem, qt.at(i, 2 * TT * lin + g + 1))
                        if lin and g == 0:
                            act.wait_ge(qm.sem, qm.at(i, TT))
                        dst = (qxT if g % 2 == 0 else qwT)[:, 0:n, (g // 2) * P:(g // 2 + 1) * P]
                        src = ps[:, 5 + g % 2, 0:64 * n].bitcast(BF16).rearrange("p (k t) -> p k t", k=n)
                        nc.scalar.activation(dst, src, ACT.Copy).then_inc(qc.sem, 1)
                elif j == 9:
                    for tt in range(TT):
                        act.wait_ge(hr.sem, hr.at(i, tt + 1))
                        nc.scalar.activation(sg[:, tt % 2, :], hq[:, tt % 2, 0:IQ],
                                             ACT.Silu).then_inc(sgr.sem, 1)
                elif j == 15:
                    root(2)
                elif j == 16:
                    for tt in range(TT):
                        act.wait_ge(t3.sem, t3.at(i, tt + 1))
                        if tt:
                            act.wait_ge(lgp.sem, lgp.at(i, tt))
                        nc.scalar.activation(zTf[:], ps[:, 5 + tt % 2, :].rearrange("p (k t) -> p k t", k=KD),
                                             ACT.Copy).then_inc(t3f.sem, 1)
                        if tt < 2:
                            act.wait_ge(stz[tt].sem, stz[tt].before(i, 64))
                        else:
                            act.wait_ge(stz[tt % 2].sem, stz[tt % 2].at(i, 32))
                        nc.scalar.activation(z3h[:, tt % 2], ps[:, 5 + tt % 2, :].rearrange("p (k t) -> p k t", k=KD),
                                             ACT.Copy).then_inc(t3h.sem, 1)
                elif j == 17:
                    act.wait_ge(lgi.sem, lgi.at(i, 1))
                    nc.scalar.activation(pe_[:], lg[:], ACT.Exp).then_inc(lge.sem, 1)

            rows(act, take_x, scan, put_out)

        @block.vector
        def _(dve):
            nc.vector.memset(xraw[:], 0.0).then_inc(s_wsplit, 1)
            dve.wait_ge(s_wh, 1)
            nc.vector.tensor_tensor(win_l[:].rearrange("p k n -> p (k n)"), big[:, 0:KD * PROJ],
                                    win_h[:].rearrange("p k n -> p (k n)"), ALU.subtract).then_inc(s_wl, 1)
            dve.wait_ge(s_small, 7 * 16)
            dve.wait_ge(s_wout, 16)
            for k in range(NX):
                w = big[:, k * D:(k + 1) * D]
                nc.vector.tensor_scalar(w, w, nw[:, k:k + 1], None, ALU.mult).then_inc(s_wsc, 1)
            dve.wait_ge(s_wh, 2)
            nc.vector.tensor_tensor(wout_l[:].rearrange("p k n -> p (k n)"), big[:, 0:NX * D],
                                    wout_h[:].rearrange("p k n -> p (k n)"), ALU.subtract).then_inc(s_wl, 1)
            dve.wait_ge(s_const, CONSTS)
            dve.wait_ge(s_expa, 1)

            def inv_root(link, var, std, k, v, d, r):
                nc.vector.tensor_copy(r0[:], v[:]).then_inc(var.sem, 1)
                dve.wait_ge(std.sem, k)
                link(nc.vector.reciprocal(r0[:], d[:]))
                link(nc.vector.tensor_tensor(r1[:], r0[:], r0[:], ALU.mult))
                link(nc.vector.tensor_tensor(r1[:], r1[:], v[:], ALU.mult))
                link(nc.vector.tensor_scalar(r1[:], r1[:], -0.5, 1.5, ALU.mult, ALU.add))
                link(nc.vector.tensor_tensor(r[:], r1[:], r0[:], ALU.mult))

            def norm(link, src, dst, m, v, d, r, var, std, k, ready):
                for tt in range(TT):
                    ins = nc.vector.bn_stats(st6[:, tt, :], src[:, tt, :])
                link(ins)
                dve.sem_inc(s_pass, 1)
                for tt in range(TT):
                    ins = nc.vector.bn_aggr(m[:, tt, :], st6[:, tt, :])
                link(ins)
                link(nc.vector.tensor_scalar(v[:], m[:, :, 1], EPS, None, ALU.add))
                inv_root(link, var, std, k, v, d, r)
                for tt in range(TT):
                    nc.vector.tensor_scalar(dst[:, tt, :], src[:, tt, :], m[:, tt, 0:1], r[:, tt:tt + 1],
                                            ALU.subtract, ALU.mult).then_inc(ready.sem, 1)

            owns = {}

            def take_x(i, j):
                if j == 0:
                    owns["x"] = Own(own_x, dve, i)
                link = owns["x"].link

                def conv(n):
                    cc = (n + NX) if n < 2 else n - 2
                    dve.wait_ge(raw.sem, raw.at(i, n + 1))
                    for j in range(KC - 1):
                        ins = nc.vector.scalar_tensor_tensor(
                            out=cacc[:, n % 2, :], in0=xraw[:, n % 2, j:j + L], scalar=cw[:, cc, j:j + 1],
                            in1=cacc[:, n % 2, :], op0=ALU.mult, op1=ALU.add)
                        if j < KC - 2:
                            link(ins)
                    ins.then_inc(cv.sem, 1)

                def back(j):
                    dve.wait_ge(xt.sem, xt.at(i, j + 1))
                    h = P // HD
                    for tt in range(TT):
                        ins = nc.vector.tensor_tensor(
                            xdt[:, tt, (j - 1) * P:j * P].rearrange("p (h d) -> p h d", h=h),
                            ps[:, j % 2, tt * P:(tt + 1) * P].rearrange("p (h d) -> p h d", h=h),
                            dt[:, tt, (j - 1) * h:j * h].unsqueeze(2).to_broadcast([P, h, HD]), ALU.mult)
                    ins.then_inc(xtd.sem, 1)

                if j == 0:
                    dve.wait_ge(hgr.sem, hgr.before(i, TT))
                    dve.wait_ge(su.sem, su.before(i, 4 * TT))
                    dve.wait_ge(ldx.sem, ldx.at(i, 16))
                    norm(link, xin, xin, mvx, vex, sdx, rsx, var_x, std_x, std_x.at(i, 1), zxr)
                    for tt in range(TT):
                        dve.wait_ge(t1h.sem, t1h.at(i, tt + 1))
                        nc.vector.tensor_tensor(xnl[:, :, tt * P:(tt + 1) * P],
                                                ps[:, tt % 2, :].rearrange("p (k t) -> p k t", k=KD),
                                                xnh[:, :, tt * P:(tt + 1) * P], ALU.subtract).then_inc(t1l.sem, 1)
                elif j <= NCC:
                    n = j - 1
                    if n == 1:
                        dve.wait_ge(dtp.sem, dtp.at(i, 1))
                        link(nc.vector.tensor_tensor(dtv[:], ps[:, 4, 0:TT * HEADS].rearrange("p (t h) -> p t h", t=TT),
                                                     dtb_bc[:].unsqueeze(1).to_broadcast([P, TT, HEADS]), ALU.add))
                        nc.vector.scalar_tensor_tensor(out=dta[:], in0=dtv[:], scalar=-1.0, in1=dtv[:],
                                                       op0=ALU.mult, op1=ALU.max).then_inc(v_in.sem, 1)
                        dve.wait_ge(sp_out.sem, sp_out.at(i, 1))
                        link(nc.vector.scalar_tensor_tensor(out=dt[:], in0=dtv[:], scalar=0.0, in1=dte[:],
                                                            op0=ALU.max, op1=ALU.add))
                        link(nc.vector.scalar_tensor_tensor(
                            out=da[:], in0=dt[:], scalar=-1.0,
                            in1=expa_bc[:].unsqueeze(1).to_broadcast([P, TT, HEADS]),
                            op0=ALU.mult, op1=ALU.mult))
                        link(nc.vector.tensor_copy(dah[:], da[:]))
                        nc.vector.tensor_tensor(dal[:], da[:], dah[:], ALU.subtract).then_inc(dar.sem, 1)
                    conv(n)
                    if n == 3:
                        dve.wait_ge(gp.sem, gp.at(i, 1))
                        nc.vector.tensor_tensor(gm[:], ps[:, 4, 0:TT * CHUNK].rearrange("p (t c) -> p t c", t=TT),
                                                gmask[:].unsqueeze(1).to_broadcast([P, TT, CHUNK]),
                                                ALU.mult).then_inc(gmr.sem, 1)
                    if n >= 5:
                        back(n - 4)
                elif j == NCC + 1:
                    back(NX - 2)
                    back(NX - 1)
                elif j == NCC + 2:
                    back(NX)
                    owns["x"].close()

            def scan(i):
                owns["v"] = Own(own_v, dve, i)
                link = owns["v"].link

                def high(u):
                    tt, q = divmod(u, UPT)
                    if u >= 2:
                        dve.wait_ge(seg.sem, seg.at(i, u - 1))
                    nc.vector.tensor_tensor(
                        bh[:, u % 2], dah[:, tt, q * UH:(q + 1) * UH].unsqueeze(1).to_broadcast([P, CHUNK, UH]),
                        upto[:], ALU.mult).then_inc(bhi.sem, 1)

                def product(u):
                    dve.wait_ge(ex.sem, ex.at(i, u + 1))
                    nc.vector.tensor_tensor(eu[u % 3], eu[u % 3],
                                            gm[:, u // UPT, :].unsqueeze(2).to_broadcast([P, CHUNK, UH]),
                                            ALU.mult).then_inc(prd.sem, 1)

                def low(u):
                    dve.wait_ge(mhr.sem, mhr.at(i, u + 1))
                    for c in range(2):
                        r = slice(c * CHUNK, (c + 1) * CHUNK)
                        ins = nc.vector.tensor_tensor(mu[r, 1, u % 2, c], eu[u % 3][r], mu[r, 0, u % 2, c],
                                                      ALU.subtract)
                    ins.then_inc(mr.sem, 1)

                def heads(ap):
                    return ap.rearrange("p (h d) -> p h d", h=HEADS)

                def state(tt, c, a):
                    if a == 0:
                        dve.wait_ge(yo.sem, yo.at(i, 2 * tt + c + 1))
                        link(nc.vector.tensor_tensor(
                            heads(S[:]), heads(S[:]),
                            cdec[:, c, tt, :].unsqueeze(2).to_broadcast([P, HEADS, HD]), ALU.mult))
                    dve.wait_ge(sn.sem, sn.at(i, 4 * tt + 2 * c + a + 1))
                    half = S[:, a * 512:(a + 1) * 512]
                    nc.vector.tensor_tensor(half, half, ps[:, 4, :], ALU.add).then_inc(su.sem, 1)

                def from_state(tt):
                    if tt:
                        dve.wait_ge(hgr.sem, hgr.at(i, tt))
                    nc.vector.tensor_tensor(
                        heads(y), heads(ps[:, 6:8, :].rearrange("p a b -> p (a b)")),
                        edec[:, 0, tt, :].unsqueeze(2).to_broadcast([P, HEADS, HD]), ALU.mult).then_inc(ysc.sem, 1)

                def combine(tt, a):
                    dve.wait_ge(ysc.sem, ysc.at(i, tt + 1))
                    dve.wait_ge(yd.sem, yd.at(i, tt * UPT + (a + 1) * UPT // 2))
                    half = y[:, a * 512:(a + 1) * 512]
                    nc.vector.tensor_tensor(half, half, ps[:, 2 + a, :], ALU.add).then_inc(yc.sem, 1)

                dve.wait_ge(x2r.sem, x2r.before(i, TT))
                nc.vector.memset(S[:], 0.0).then_inc(s0.sem, 1)
                high(0)
                high(1)
                nc.vector.memset(mu[0:CHUNK, :, :, 1].rearrange("p s b t h -> p (s b) (t h)"), 0.0)
                link(nc.vector.memset(mu[CHUNK:P, :, :, 0].rearrange("p s b t h -> p (s b) (t h)"), 0.0))
                product(0)
                high(2)
                for u in range(U):
                    tt, q = divmod(u, UPT)
                    if u + 1 < U:
                        product(u + 1)
                    low(u)
                    if u + 3 < U:
                        high(u + 3)
                    if q == 0 and tt:
                        combine(tt - 1, 1)
                    if q in (1, 2):
                        state(tt, 0, q - 1)
                    if q in (4, 5):
                        state(tt, 1, q - 4)
                    if q == 6:
                        from_state(tt)
                    if q == 7:
                        combine(tt, 0)
                combine(TT - 1, 1)

            def put_out(i, j):
                link = owns["v"].link
                lin = 1 if j >= 10 else 0
                n = 2 if lin else KD
                w = IQ if lin else D
                src, wn, wr = (av, w2nat, w2Tr) if lin else (zn[:], wnat, wTr)

                def add_x1(tt):
                    dve.wait_ge(op.sem, op.at(i, tt + 1))
                    nc.vector.scalar_tensor_tensor(out=xc[:, tt, :], in0=ps[:, 7, :],
                                                   scalar=rs[:, tt:tt + 1], in1=xc[:, tt, :],
                                                   op0=ALU.mult, op1=ALU.add).then_inc(x1r.sem, 1)

                if j < TT:
                    for g in (2 * j, 2 * j + 1):
                        dve.wait_ge(hh.sem, hh.at(i, g + 1))
                        half = slice((g % 2) * 4, (g % 2) * 4 + 4)
                        nc.vector.tensor_tensor(htl[:, g // 2 % 2, half, :],
                                                ps[:, 5 + g % 2, :].rearrange("p (k t) -> p k t", k=4),
                                                hth[:, g // 2 % 2, half, :], ALU.subtract).then_inc(hl.sem, 1)
                    if j == 0:
                        dve.wait_ge(sqr.sem, sqr.at(i, TT))
                        link(nc.vector.tensor_scalar(ve[:], ssq[:], 1.0 / DIN, EPS, ALU.mult, ALU.add))
                        inv_root(link, var_in, std_out, std_out.at(i, 1), ve, sd, rs)
                        dve.wait_ge(ldc.sem, ldc.at(i, 16))
                    else:
                        add_x1(j - 1)
                elif j == 4:
                    add_x1(TT - 1)
                    dve.wait_ge(x1r.sem, x1r.at(i, TT))
                    norm(link, xc, zn, mv, ve, sd, rs, var_in, std_out, std_out.at(i, 2), znr)
                elif j in (5, 10):
                    for k in range(n):
                        g = lin * KD + k
                        dve.wait_ge(t2.sem, t2.at(i, g + 1))
                        nc.vector.tensor_reduce(axm[:, k:k + 1], ps[:, 5 + g % 2, :], AX.X, ALU.max,
                                                apply_absolute_value=True).then_inc(t2r.sem, 1)
                    if lin:
                        dve.wait_ge(ldq2.sem, ldq2.at(i, 32))
                    else:
                        dve.wait_ge(ldq.sem, ldq.at(i, 32))
                    link(nc.vector.tensor_reduce(awm[:, 0:n], wr, AX.X, ALU.max, apply_absolute_value=True))
                    link(nc.vector.tensor_scalar(awm[:, 0:n], awm[:, 0:n], QEPS, None, ALU.max))
                    link(nc.vector.reciprocal(ra[:, 0:n], awm[:, 0:n]))
                    nc.vector.scalar_tensor_tensor(out=ra[:, 0:n], in0=axm[:, 0:n], scalar=QEPS, in1=ra[:, 0:n],
                                                   op0=ALU.max, op1=ALU.mult).then_inc(rat.sem, 1)
                    dve.wait_ge(sqt.sem, sqt.at(i, lin + 1))
                    link(nc.vector.reciprocal(sr[:, 0:n], sq0[:, 0:n]))
                    link(nc.vector.tensor_tensor(sr[:, 0:n], sr[:, 0:n], ra[:, 0:n], ALU.mult))
                    link(nc.vector.tensor_tensor(sm[:, 0:n], sr[:, 0:n], sq0[:, 0:n], ALU.add))
                    link(nc.vector.tensor_scalar(sm[:, 0:n], sm[:, 0:n], 0.5, QEPS, ALU.mult, ALU.max))
                    nc.vector.reciprocal(sr[:, 0:n], sm[:, 0:n]).then_inc(sbr.sem, 1)
                elif j in (6, 11):
                    dve.wait_ge(sbp.sem, sbp.at(i, lin + 1))
                    for t in range(TT):
                        nc.vector.tensor_tensor(src[:, t, :], src[:, t, :], ps[:, 6, 0:w], ALU.mult)
                        ins = nc.vector.tensor_tensor(wn[:, t, :], wn[:, t, :], ps[:, 5, 0:w], ALU.mult)
                    link(ins)
                    nc.vector.tensor_reduce(xsc[:], src, AX.X, ALU.max, apply_absolute_value=True)
                    link(nc.vector.tensor_reduce(wsc[:], wn, AX.X, ALU.max, apply_absolute_value=True))
                    nc.vector.tensor_scalar(xsc[:], xsc[:], QEPS, 1.0 / QMAX, ALU.max, ALU.mult)
                    nc.vector.tensor_scalar(wsc[:], wsc[:], QEPS, 1.0 / QMAX, ALU.max,
                                            ALU.mult).then_inc(wsr.sem, 1)
                elif j in (7, 12):
                    dve.wait_ge(wsr.sem, wsr.at(i, lin + 1))
                    nc.vector.reciprocal(rx[:], xsc[:])
                    link(nc.vector.reciprocal(rw_[:], wsc[:]))
                    if lin:
                        dve.wait_ge(qt.sem, qt.at(i, 2 * TT))
                    both = [(v, r, q, t) for t in range(TT) for v, r, q in ((src, rx, qx), (wn, rw_, qw))]
                    for v, r, q, t in both:
                        ins = nc.vector.tensor_scalar(v[:, t, :], v[:, t, :], r[:, t:t + 1], -QMAX,
                                                      ALU.mult, ALU.max)
                    link(ins)
                    for v, r, q, t in both:
                        ins = nc.vector.tensor_scalar(v[:, t, :], v[:, t, :], QMAX, MAGIC, ALU.min, ALU.add)
                    link(ins)
                    for v, r, q, t in both:
                        nc.vector.tensor_scalar(q[:, t, 0:w], v[:, t, :], MAGIC, None,
                                                ALU.subtract).then_inc(qr.sem, 1)
                elif j in (9, 14):
                    dve.wait_ge(wsb.sem, wsb.at(i, lin + 1))
                    for tt in range(TT):
                        dve.wait_ge(qm.sem, qm.at(i, lin * TT + tt + 1))
                        h = hq[:, tt % 2, :]
                        bank = ps[:, 7 if tt % 2 == 0 else 5, :]
                        if lin == 0:
                            if tt >= 2:
                                dve.wait_ge(ar.sem, ar.at(i, tt - 1))
                            else:
                                dve.wait_ge(qr.sem, qr.at(i, 2 * TT))
                            nc.vector.scalar_tensor_tensor(out=h, in0=bank, scalar=xsc[:, tt:tt + 1],
                                                           in1=wscb, op0=ALU.mult, op1=ALU.mult).then_inc(hr.sem, 1)
                            dve.wait_ge(sgr.sem, sgr.at(i, tt + 1))
                            nc.vector.tensor_tensor(av[:, tt, :], sg[:, tt % 2, :], hq[:, tt % 2, IQ:],
                                                    ALU.mult).then_inc(ar.sem, 1)
                        else:
                            link(nc.vector.scalar_tensor_tensor(out=h, in0=bank,
                                                                scalar=xsc[:, tt:tt + 1], in1=wscb,
                                                                op0=ALU.mult, op1=ALU.mult))
                            nc.vector.tensor_tensor(xc[:, tt, :], xc[:, tt, :], h, ALU.add).then_inc(x2r.sem, 1)
                elif j == 15:
                    dve.wait_ge(x2r.sem, x2r.at(i, TT))
                    norm(link, xc, zn, mv, ve, sd, rs, var_in, std_out, std_out.at(i, 3), znr)
                elif j == 16:
                    for tt in range(TT):
                        dve.wait_ge(t3h.sem, t3h.at(i, tt + 1))
                        nc.vector.tensor_tensor(z3l[:, tt % 2], ps[:, 5 + tt % 2, :].rearrange("p (k t) -> p k t", k=KD),
                                                z3h[:, tt % 2], ALU.subtract).then_inc(t3l.sem, 1)
                elif j == 17:
                    dve.wait_ge(lgp.sem, lgp.at(i, TT))
                    link(nc.vector.tensor_copy(lg[:], ps[:, 7, 0:TT * E].rearrange("p (t e) -> p t e", t=TT)))
                    link(nc.vector.tensor_reduce(mx[:], lg[:], AX.X, ALU.max))
                    ex8 = [P, TT, E]
                    nc.vector.tensor_tensor(lg[:], lg[:], mx[:].unsqueeze(2).to_broadcast(ex8),
                                            ALU.subtract).then_inc(lgi.sem, 1)
                    dve.wait_ge(lge.sem, lge.at(i, 1))
                    link(nc.vector.tensor_reduce(sums[:], pe_[:], AX.X, ALU.add))
                    link(nc.vector.reciprocal(sums[:], sums[:]))
                    link(nc.vector.tensor_tensor(pr[:], pe_[:], sums[:].unsqueeze(2).to_broadcast(ex8), ALU.mult))
                    for tt in range(TT):
                        pj_, pi_ = (pr[:, tt].unsqueeze(1).to_broadcast([P, E, E]),
                                    pr[:, tt].unsqueeze(2).to_broadcast([P, E, E]))
                        nc.vector.tensor_tensor(gt[:, tt], pj_, pi_, ALU.is_gt)
                        ins = nc.vector.tensor_tensor(eq[:, tt], pj_, pi_, ALU.is_equal)
                    link(ins)
                    link(nc.vector.tensor_tensor(eq, eq, tie[:].unsqueeze(1).to_broadcast([P, TT, E, E]), ALU.mult))
                    link(nc.vector.tensor_tensor(gt, gt, eq, ALU.add))
                    link(nc.vector.tensor_tensor(gt, gt, pr[:].unsqueeze(2).to_broadcast([P, TT, E, E]), ALU.mult))
                    link(nc.vector.tensor_reduce(mass[:], gt, AX.X, ALU.add))
                    dve.wait_ge(stw.sem, stw.before(i, 16))
                    link(nc.vector.tensor_scalar(keep[:], mass[:], TOP_P, None, ALU.is_le))
                    nc.vector.tensor_tensor(wt[:].rearrange("p e t -> p t e"), pr[:], keep[:],
                                            ALU.mult).then_inc(wtr.sem, 1)
                    owns["v"].close()

            rows(dve, take_x, scan, put_out)

        @block.tensor
        def _(pe):
            pe.wait_ge(s_const, CONSTS)
            pe.wait_ge(s_small, 7 * 16)
            pe.wait_ge(s_wl, 2)

            def mm3(dst, wh, wl, mh, ml, k, last):
                nc.tensor.matmul(dst, wh, mh, start=(k == 0), stop=False)
                nc.tensor.matmul(dst, wh, ml, start=False, stop=False)
                return nc.tensor.matmul(dst, wl, mh, start=False, stop=last)

            def take_x(i, j):
                def proj(n):
                    c0 = DIN + ((n + NX) if n < 2 else n - 2) * P
                    if n == 0:
                        pe.wait_ge(t1l.sem, t1l.at(i, TT))
                    if n >= 2:
                        pe.wait_ge(raw.sem, raw.at(i, n - 1))
                    for k in range(KD):
                        ins = mm3(ps[:, 2 + n % 2, :], win_h[:, k, c0:c0 + P], win_l[:, k, c0:c0 + P],
                                  xnh[:, k, :], xnl[:, k, :], k, k == KD - 1)
                    ins.then_inc(pj.sem, 1)

                def back(j):
                    n = 0 if j == 0 else j + 1
                    src = bT[:] if j == 0 else xall[:, j - 1, :]
                    pe.wait_ge(act_x.sem, act_x.at(i, n + 1))
                    if j >= 2:
                        if j == 2:
                            pe.wait_ge(xta.sem, xta.at(i, 1))
                        else:
                            pe.wait_ge(xtd.sem, xtd.at(i, j - 2))
                    for tt in range(TT):
                        ins = nc.tensor.transpose(ps[:, j % 2, tt * P:(tt + 1) * P],
                                                  src[:, tt * P:(tt + 1) * P], ident[:])
                    ins.then_inc(xt.sem, 1)

                dflat = da[:].rearrange("p t h -> p (t h)")
                if j == 0:
                    pe.wait_ge(su.sem, su.before(i, 4 * TT))
                    pe.wait_ge(hgr.sem, hgr.before(i, TT))
                    for tt in range(TT):
                        pe.wait_ge(zxr.sem, zxr.at(i, tt + 1))
                        if tt >= 2:
                            pe.wait_ge(t1l.sem, t1l.at(i, tt - 1))
                        for k in range(KD):
                            ins = nc.tensor.transpose(ps[:, tt % 2, k * P:(k + 1) * P],
                                                      xin[:, tt, k * P:(k + 1) * P], ident[:])
                        ins.then_inc(t1.sem, 1)
                elif j <= NCC:
                    n = j - 1
                    proj(n)
                    if n == 0:
                        for tt in range(TT):
                            for k in range(KD):
                                t = slice(tt * P, (tt + 1) * P)
                                ins = mm3(ps[:, 4, tt * HEADS:(tt + 1) * HEADS], xnh[:, k, t], xnl[:, k, t],
                                          win_h[:, k, DTC:], win_l[:, k, DTC:], k, k == KD - 1)
                        ins.then_inc(dtp.sem, 1)
                    if n == 1:
                        pe.wait_ge(dar.sem, dar.at(i, 1))
                        nc.tensor.matmul(ps[:, 4, 0:TT * HEADS], incl[:], dflat, start=True, stop=True)
                        nc.tensor.matmul(ps[:, 4, TT * HEADS:], later[:], dah[:].rearrange("p t h -> p (t h)"),
                                         start=True, stop=False)
                        nc.tensor.matmul(ps[:, 4, TT * HEADS:], later[:], dal[:].rearrange("p t h -> p (t h)"),
                                         start=False, stop=True).then_inc(cum.sem, 1)
                    if n == 2:
                        pe.wait_ge(ecd.sem, ecd.at(i, 1))
                        nc.tensor.matmul(ps[:, 4, 0:TT * HEADS], in_a[:], dflat, start=True, stop=True)
                        nc.tensor.matmul(ps[:, 4, TT * HEADS:], in_b[:], dflat, start=True,
                                         stop=True).then_inc(cum.sem, 1)
                        back(0)
                    if n == 3:
                        pe.wait_ge(act_x.sem, act_x.at(i, 2))
                        pe.wait_ge(ecd.sem, ecd.at(i, 2))
                        for tt in range(TT):
                            for c in range(2):
                                t = slice(tt * P + c * CHUNK, tt * P + (c + 1) * CHUNK)
                                ins = nc.tensor.matmul(ps[c * CHUNK:(c + 1) * CHUNK, 4, tt * CHUNK:(tt + 1) * CHUNK],
                                                       bT[:, t], cT[:, t], start=True, stop=True)
                        ins.then_inc(gp.sem, 1)
                    if n >= 4:
                        back(n - 3)
                elif j == NCC + 1:
                    back(NX - 1)
                elif j == NCC + 2:
                    back(NX)

            def scan(i):
                def decay(u):
                    pe.wait_ge(bhi.sem, bhi.at(i, u + 1))
                    pe.wait_ge(blo.sem, blo.at(i, u + 1))
                    if u >= 2:
                        pe.wait_ge(ex.sem, ex.at(i, u - 1))
                    nc.tensor.matmul(ps[:, u % 2, :], later[:], bh[:, u % 2].rearrange("p t h -> p (t h)"),
                                     start=True, stop=False)
                    nc.tensor.matmul(ps[:, u % 2, :], later[:], bl[:, u % 2].rearrange("p t h -> p (t h)"),
                                     start=False, stop=True).then_inc(seg.sem, 1)

                def within(u):
                    tt, q = divmod(u, UPT)
                    bank, c0 = 2 + q // 4, q % 4 * P
                    if q % 4 == 0 and tt:
                        pe.wait_ge(yc.sem, yc.at(i, 2 * tt - 1 + q // 4))
                    nc.tensor.matmul(ps[:, bank, c0:c0 + P], xall[:, q, tt * P:(tt + 1) * P], ident[:],
                                     start=True, stop=False)
                    if q == 0:
                        pe.wait_ge(xlr.sem, xlr.at(i, tt + 1))
                    pe.wait_ge(mr.sem, mr.at(i, u + 1))
                    mh, ml = (mu[:, s, u % 2].rearrange("p c t h -> p (c t) h") for s in range(2))
                    for h in range(UH):
                        dst = ps[:, bank, c0 + h * HD:c0 + (h + 1) * HD]
                        xh, xl = (xsp[:, tt % 2, s, (q * UH + h) * HD:(q * UH + h + 1) * HD] for s in range(2))
                        nc.tensor.matmul(dst, mh[:, :, h], xh, start=False, stop=False)
                        nc.tensor.matmul(dst, mh[:, :, h], xl, start=False, stop=False)
                        ins = nc.tensor.matmul(dst, ml[:, :, h], xh, start=False, stop=(h == UH - 1))
                    ins.then_inc(yd.sem, 1)

                def gate(g, k):
                    t = slice(g // 2 * P, (g // 2 + 1) * P)
                    c = slice((g % 2) * 512, (g % 2 + 1) * 512)
                    if g and k == 0:
                        pe.wait_ge(gate_e.sem, gate_e.at(i, g))
                    ins = mm3(ps[:, 5, :], xnh[:, k, t], xnl[:, k, t], win_h[:, k, c], win_l[:, k, c],
                              k, k == KD - 1)
                    if k == KD - 1:
                        ins.then_inc(gate_p.sem, 1)

                def from_state(tt, c):
                    r = slice(c * CHUNK, (c + 1) * CHUNK)
                    t = slice(tt * P + c * CHUNK, tt * P + (c + 1) * CHUNK)
                    if tt == 0 and c == 0:
                        pe.wait_ge(s0.sem, s0.at(i, 1))
                    else:
                        pe.wait_ge(su.sem, su.at(i, 4 * tt + 2 * c))
                    if tt and c == 0:
                        pe.wait_ge(ysc.sem, ysc.at(i, tt))
                    for a in range(2):
                        ins = nc.tensor.matmul(ps[r, 6 + a, :], cT[:, t], S[:, a * 512:(a + 1) * 512],
                                               start=True, stop=True)
                    ins.then_inc(yo.sem, 1)

                def to_state(tt, c, a):
                    r = slice(c * CHUNK, (c + 1) * CHUNK)
                    n = 4 * tt + 2 * c + a
                    pe.wait_ge(xddr.sem, xddr.at(i, tt + 1))
                    if n:
                        pe.wait_ge(su.sem, su.at(i, n))
                    nc.tensor.matmul(ps[:, 4, :], btok[r, tt, :], xdd[r, a * 512:(a + 1) * 512],
                                     start=True, stop=True).then_inc(sn.sem, 1)

                pe.wait_ge(xtd.sem, xtd.at(i, NX))
                pe.wait_ge(xta.sem, xta.at(i, NX + 1))
                pe.wait_ge(raw.sem, raw.at(i, NCC))
                pe.wait_ge(gmr.sem, gmr.at(i, 1))
                pe.wait_ge(t3l.sem, t3l.before(i, TT))
                pe.wait_ge(lgi.sem, lgi.before(i, 1))
                decay(0)
                decay(1)
                for u in range(U):
                    if u + 2 < U:
                        decay(u + 2)
                    tt, q = divmod(u, UPT)
                    gate(u // 4, u % 4)
                    within(u)
                    if q in (0, 3):
                        from_state(tt, q // 3)
                    if q in (0, 1, 3, 4):
                        to_state(tt, q // 3, q % 3)

            def put_out(i, j):
                lin = 1 if j >= 10 else 0
                n = 2 if lin else KD

                def out_proj(tt):
                    pe.wait_ge(hl.sem, hl.at(i, 2 * tt + 2))
                    if tt:
                        pe.wait_ge(x1r.sem, x1r.at(i, tt))
                    for k in range(NX):
                        ins = mm3(ps[:, 7, :], hth[:, tt % 2, k, :], htl[:, tt % 2, k, :],
                                  wout_h[:, k, :], wout_l[:, k, :], k, k == NX - 1)
                    ins.then_inc(op.sem, 1)

                def spread(bank, v, m):
                    for k in range(m):
                        ins = nc.tensor.matmul(ps[:, bank, k * P:(k + 1) * P],
                                               v[:, k:k + 1].to_broadcast([P, P]), ident[:],
                                               start=True, stop=True)
                    return ins

                def logits(tt):
                    pe.wait_ge(t3f.sem, t3f.at(i, tt + 1))
                    for k in range(KD):
                        ins = nc.tensor.matmul(ps[:, 7, tt * E:(tt + 1) * E], zTf[:, k, :], rw[:, k, :],
                                               start=(k == 0), stop=(k == KD - 1))
                    ins.then_inc(lgp.sem, 1)

                if j < TT:
                    if j == 0:
                        pe.wait_ge(su.sem, su.at(i, 4 * TT))
                        pe.wait_ge(hgr.sem, hgr.at(i, TT))
                    for a in range(2):
                        g = 2 * j + a
                        if g >= 2:
                            pe.wait_ge(hl.sem, hl.at(i, g - 1))
                        for k in range(4):
                            c = (a * 4 + k) * P
                            ins = nc.tensor.transpose(ps[:, 5 + a, k * P:(k + 1) * P], gs[:, j, c:c + P], ident[:])
                        ins.then_inc(ht.sem, 1)
                    if j:
                        out_proj(j - 1)
                elif j == 4:
                    out_proj(TT - 1)
                elif j in (5, 10):
                    if lin:
                        pe.wait_ge(ar.sem, ar.at(i, TT))
                    else:
                        pe.wait_ge(znr.sem, znr.at(i, TT))
                    src = av if lin else zn
                    for k in range(n):
                        g = lin * KD + k
                        if k >= 2:
                            pe.wait_ge(t2r.sem, t2r.at(i, g - 1))
                        for tt in range(TT):
                            ins = nc.tensor.transpose(ps[:, 5 + g % 2, tt * P:(tt + 1) * P],
                                                      src[:, tt, k * P:(k + 1) * P], ident[:])
                        ins.then_inc(t2.sem, 1)
                elif j in (6, 11):
                    pe.wait_ge(sbr.sem, sbr.at(i, lin + 1))
                    spread(5, sm, n)
                    spread(6, sr, n).then_inc(sbp.sem, 1)
                elif j in (7, 12):
                    pe.wait_ge(wsr.sem, wsr.at(i, lin + 1))
                    spread(7, wsc, TT).then_inc(wsp.sem, 1)
                elif j in (8, 13):
                    for g in range(2 * TT):
                        pe.wait_ge(qr.sem, qr.at(i, 2 * TT * lin + g + 1))
                        if g >= 2:
                            pe.wait_ge(qc.sem, qc.at(i, 2 * TT * lin + g - 1))
                        q = qx if g % 2 == 0 else qw
                        for k in range(n):
                            ins = nc.tensor.transpose(ps[:, 5 + g % 2, k * 64:(k + 1) * 64].bitcast(BF16),
                                                      q[:, g // 2, k * P:(k + 1) * P], identb[:])
                        ins.then_inc(qt.sem, 1)
                elif j in (9, 14):
                    pe.wait_ge(qc.sem, qc.at(i, 2 * TT * (lin + 1)))
                    pe.wait_ge(wsb.sem, wsb.at(i, lin + 1))
                    for tt in range(TT):
                        if tt >= 2:
                            if lin:
                                pe.wait_ge(x2r.sem, x2r.at(i, tt - 1))
                            else:
                                pe.wait_ge(hr.sem, hr.at(i, tt - 1))
                        for k in range(n):
                            ins = nc.tensor.matmul(ps[:, 7 if tt % 2 == 0 else 5, :], qxT[:, k, tt * P:(tt + 1) * P],
                                                   qwT[:, k, :], start=(k == 0), stop=(k == n - 1))
                        ins.then_inc(qm.sem, 1)
                elif j == 16:
                    for tt in range(TT):
                        pe.wait_ge(znr.sem, znr.at(i, TT + tt + 1))
                        if tt >= 2:
                            pe.wait_ge(t3l.sem, t3l.at(i, tt - 1))
                        for k in range(KD):
                            ins = nc.tensor.transpose(ps[:, 5 + tt % 2, k * P:(k + 1) * P],
                                                      zn[:, tt, k * P:(k + 1) * P], ident[:])
                        ins.then_inc(t3.sem, 1)
                        if tt:
                            logits(tt - 1)
                    logits(TT - 1)

            rows(pe, take_x, scan, put_out)


def expert_pass(nc, gateT, upT, downT, x2_dram, zh_dram, zl_dram, wt_dram, out):
    STEPS = PAIR * B
    with ExitStack() as ctx:
        def sb(name, shape, dt=F32):
            return ctx.enter_context(nc.sbuf_tensor(name, shape, dt))

        def sem(name):
            return ctx.enter_context(nc.semaphore(name))

        counts = []

        def count(name, per):
            counts.append(Count(ctx, nc, name, per))
            return counts[-1]

        pp = ctx.enter_context(nc.psum_tensor("pp", [P, 8, 512], F32))
        acc = sb("acc", [P, NT, D])
        zh = sb("zh", [P, B, TT, KD, P], BF16)
        zl = sb("zl", [P, B, TT, KD, P], BF16)
        wts = sb("wts", [P, B, E, TT])
        wcur = sb("wcur", [P, 2, B, TT])
        guh = sb("guh", [P, PAIR, 2, KD, I], BF16)
        gul = sb("gul", [P, PAIR, 2, KD, I], BF16)
        dnh = sb("dnh", [P, PAIR, IC, D], BF16)
        dnl = sb("dnl", [P, PAIR, IC, D], BF16)
        stage = sb("stage", [P, 2, I])
        sgl = sb("sgl", [P, 2, L])
        hf = sb("hf", [P, 2, L])
        hhi = sb("hhi", [P, IC + 1, L], BF16)
        hlo = sb("hlo", [P, IC + 1, L], BF16)

        s_ld = sem("s_ld")
        s_out = sem("s_out")
        s_pass = sem("s_pass2")
        wl = [count(f"wl{s}", 16 * PAIR * PIECES // 2) for s in range(2)]
        wh = count("wh", PAIR * PIECES)
        wo = count("wo", PAIR * PIECES)
        gu = count("gu", STEPS * IC)
        sgr = count("sg_ready", STEPS * IC)
        hm = count("hm", STEPS * IC)
        hh = count("h_high", STEPS * IC)
        hl = count("h_low", STEPS * IC)
        dn = count("dn", STEPS * TT)
        ad = count("ad", STEPS * TT)
        wc = count("wc", PAIR)

        block = ctx.enter_context(nc.Block())

        def piece(expert, n):
            if n < 2 * KD:
                return (gateT if n < KD else upT)[expert, (n % KD) * P:(n % KD + 1) * P, :]
            k = 2 * (n - 2 * KD)
            return downT[expert, k * P:(k + 2) * P, :].rearrange("(k p) n -> p k n", p=P)

        def place(hi, par, n):
            if n < 2 * KD:
                return (guh if hi else gul)[:, par, n // KD, n % KD, :]
            k = 2 * (n - 2 * KD)
            return (dnh if hi else dnl)[:, par, k:k + 2, :].rearrange("p k n -> p (k n)")

        def staged(n):
            return stage[:, n % 2, :] if n < 2 * KD else stage[:, n % 2, :].rearrange("p (k n) -> p k n", k=2)

        def slot(step, c):
            return (IC if step % 2 else 0) if c == 0 else c

        AFTER = (2, 4, 6)
        FIRST = PIECES

        @block.sync
        def _(sp):
            for n in range(PIECES):
                if n >= 2:
                    sp.wait_ge(wo.sem, wo.per - FIRST + n - 1)
                sp.dma_start(staged(n), piece(0, n)).then_inc(wl[n % 2].sem, 16)
                if n == 1:
                    for b in range(B):
                        sp.dma_start(zh[:, b], zh_dram[b].rearrange("t p k c -> p t k c")).then_inc(s_ld, 16)
                        sp.dma_start(zl[:, b], zl_dram[b].rearrange("t p k c -> p t k c")).then_inc(s_ld, 16)
                        sp.dma_start(acc[:, b * TT:(b + 1) * TT, :], x2_dram[b]).then_inc(s_ld, 16)
                        sp.dma_start(wts[:, b].rearrange("p e t -> p (e t)"), wt_dram[b]).then_inc(s_ld, 16)
            with sp.Fori(0, E // PAIR) as i:
                for n in range(PAIR * PIECES):
                    sp.wait_ge(wo.sem, wo.at(i, n - 1))
                    sp.sem_inc(s_pass, 1)
                    nxt = i * PAIR + 1 if n < PIECES else (i * PAIR + 2) % E
                    sp.dma_start(staged(n % PIECES), piece(nxt, n % PIECES)).then_inc(wl[n % 2].sem, 16)
            sp.wait_ge(ad.sem, ad.per * (E // PAIR + 1))
            for b in range(B):
                sp.dma_start(out[b], acc[:, b * TT:(b + 1) * TT, :]).then_inc(s_out, 16)
            for s in range(2):
                sp.wait_ge(wl[s].sem, wl[s].per * (E // PAIR + 1))
            sp.wait_ge(s_out, 16 * B)

        @block.gpsimd
        def _(pool):
            for c in counts:
                less = {id(wl[0]): 16 * FIRST // 2, id(wl[1]): 16 * FIRST // 2, id(wh): FIRST, id(wo): FIRST}
                pool.sem_inc(c.sem, c.per - less.get(id(c), 0))

        @block.scalar
        def _(act):
            for n in range(PIECES):
                act.wait_ge(wl[n % 2].sem, wl[n % 2].per - 16 * FIRST // 2 + 16 * (n // 2 + 1))
                nc.scalar.activation(place(True, 0, n), stage[:, n % 2, :], ACT.Copy).then_inc(wh.sem, 1)
            with act.Fori(0, E // PAIR) as i:
                def high(step, c):
                    n = step * IC + c
                    act.wait_ge(hm.sem, hm.at(i, n + 1))
                    if c:
                        act.wait_ge(dn.sem, dn.at(i, TT * step))
                    nc.scalar.activation(hhi[:, slot(step, c), :], hf[:, n % 2, :], ACT.Copy).then_inc(hh.sem, 1)

                for step in range(STEPS):
                    par, tb = divmod(step, B)
                    for c in range(IC):
                        n = step * IC + c
                        act.wait_ge(gu.sem, gu.at(i, n + 1))
                        nc.scalar.activation(sgl[:, n % 2, :], pp[:, n % 2, :], ACT.Silu).then_inc(sgr.sem, 1)
                        if n and c:
                            high(step, c - 1)
                        if c == IC - 1:
                            high(step, c)
                        if c in AFTER:
                            m = par * PIECES + tb * 3 + AFTER.index(c)
                            act.wait_ge(wl[m % 2].sem, wl[m % 2].at(i, 16 * (m // 2 + 1)))
                            if tb == 0:
                                act.wait_ge(dn.sem, dn.at(i, TT * step))
                            nc.scalar.activation(place(True, 1 - par, m % PIECES), stage[:, m % 2, :],
                                                 ACT.Copy).then_inc(wh.sem, 1)

        @block.vector
        def _(dve):
            for n in range(PIECES):
                dve.wait_ge(wh.sem, wh.per - FIRST + n + 1)
                nc.vector.tensor_tensor(place(False, 0, n), stage[:, n % 2, :], place(True, 0, n),
                                        ALU.subtract).then_inc(wo.sem, 1)
            dve.wait_ge(s_ld, 16 * 4 * B)
            with dve.Fori(0, E // PAIR) as i:
                dve.wait_ge(ad.sem, ad.at(i, 0))
                for par in range(PAIR):
                    nc.vector.tensor_copy(wcur[:, par], wts[:, :, bass.ds(i * PAIR + par, 1), :].rearrange(
                        "p b e t -> p b (e t)")).then_inc(wc.sem, 1)

                def low(step, c):
                    n = step * IC + c
                    dve.wait_ge(hh.sem, hh.at(i, n + 1))
                    nc.vector.tensor_tensor(hlo[:, slot(step, c), :], hf[:, n % 2, :], hhi[:, slot(step, c), :],
                                            ALU.subtract).then_inc(hl.sem, 1)

                def add(step):
                    par, tb = divmod(step, B)
                    for tt in range(TT):
                        dve.wait_ge(dn.sem, dn.at(i, step * TT + tt + 1))
                        a = acc[:, tb * TT + tt, :]
                        nc.vector.scalar_tensor_tensor(out=a, in0=pp[:, 4 + tt, :], scalar=wcur[:, par, tb, tt:tt + 1],
                                                       in1=a, op0=ALU.mult, op1=ALU.add).then_inc(ad.sem, 1)

                dve.wait_ge(wc.sem, wc.at(i, PAIR))
                for step in range(STEPS):
                    par, tb = divmod(step, B)
                    for c in range(IC):
                        n = step * IC + c
                        dve.wait_ge(sgr.sem, sgr.at(i, n + 1))
                        if n >= 2:
                            dve.wait_ge(hl.sem, hl.at(i, n - 1))
                        nc.vector.tensor_tensor(hf[:, n % 2, :], sgl[:, n % 2, :], pp[:, 2 + n % 2, :],
                                                ALU.mult).then_inc(hm.sem, 1)
                        if n and c:
                            low(step, c - 1)
                        if c == IC - 1:
                            low(step, c)
                        if c == 0 and step:
                            add(step - 1)
                        if c in AFTER:
                            m = par * PIECES + tb * 3 + AFTER.index(c)
                            dve.wait_ge(wh.sem, wh.at(i, m + 1))
                            nc.vector.tensor_tensor(place(False, 1 - par, m % PIECES), stage[:, m % 2, :],
                                                    place(True, 1 - par, m % PIECES),
                                                    ALU.subtract).then_inc(wo.sem, 1)
                add(STEPS - 1)

        @block.tensor
        def _(pe):
            pe.wait_ge(s_ld, 16 * 4 * B)
            with pe.Fori(0, E // PAIR) as i:
                def gate_up(step, c):
                    par, tb = divmod(step, B)
                    n = step * IC + c
                    if c == 0 and tb == 0:
                        pe.wait_ge(wo.sem, wo.at(i, PIECES * par))
                    pe.wait_ge(hm.sem, hm.at(i, n - 1))
                    for j in range(2):
                        for k in range(KD):
                            w = slice(c * P, (c + 1) * P)
                            dst = pp[:, 2 * j + n % 2, :]
                            nc.tensor.matmul(dst, guh[:, par, j, k, w], zh[:, tb, :, k, :], start=(k == 0), stop=False)
                            nc.tensor.matmul(dst, guh[:, par, j, k, w], zl[:, tb, :, k, :], start=False, stop=False)
                            ins = nc.tensor.matmul(dst, gul[:, par, j, k, w], zh[:, tb, :, k, :], start=False,
                                                   stop=(k == KD - 1))
                    ins.then_inc(gu.sem, 1)

                def down(step):
                    par, tb = divmod(step, B)
                    pe.wait_ge(hl.sem, hl.at(i, (step + 1) * IC))
                    for tt in range(TT):
                        pe.wait_ge(ad.sem, ad.at(i, step * TT + tt + 1 - TT))
                        t = slice(tt * P, (tt + 1) * P)
                        for c in range(IC):
                            s = slot(step, c)
                            dst = pp[:, 4 + tt, :]
                            nc.tensor.matmul(dst, hhi[:, s, t], dnh[:, par, c, :], start=(c == 0), stop=False)
                            nc.tensor.matmul(dst, hhi[:, s, t], dnl[:, par, c, :], start=False, stop=False)
                            ins = nc.tensor.matmul(dst, hlo[:, s, t], dnh[:, par, c, :], start=False,
                                                   stop=(c == IC - 1))
                        ins.then_inc(dn.sem, 1)

                gate_up(0, 0)
                for step in range(STEPS):
                    for c in range(1, IC):
                        gate_up(step, c)
                    if step + 1 < STEPS:
                        gate_up(step + 1, 0)
                    down(step)


def kernel(**inputs):
    import numpy as np
    import concourse.bacc as bacc
    from concourse.bass_utils import run_bass_kernel_spmd

    def tiles(a):
        b, r, n = a.shape
        return a.reshape(b, r // P, P, n).transpose(0, 2, 1, 3)

    def rows(v):
        return v.reshape(1, -1)

    f = inputs["fside_BxS2xS2_0"]
    c = inputs["ctx_1024"]
    a = {k.replace("L0_attn_", "").replace("L0_ffn_", ""): np.asarray(v) for k, v in inputs.items()}
    f, c = np.asarray(f), np.asarray(c)
    arrays = {
        "x": tiles(a["x"]),
        "guw": tiles(f),
        "guwT": tiles(f.transpose(0, 2, 1)),
        "dnw": tiles(c),
        "dnwT": tiles(c.transpose(0, 2, 1)),
        "winT": a["in_proj_w"].T,
        "conv_w": a["conv_w"].reshape(NCC, P, KC).transpose(1, 0, 2),
        "conv_b": a["conv_b"].reshape(NCC, P).T,
        "dt_bias": rows(a["dt_bias"]),
        "a_log": rows(a["A_log"]),
        "d_skip": np.repeat(a["D"], HD).reshape(NX, P).T,
        "norm_w": a["norm_w"].reshape(NX, P).T,
        "woutT": a["out_proj_w"].T,
        "rwT": a["router_w"].T.reshape(KD, P, E).transpose(1, 0, 2),
        "gateT": a["gate_w"].transpose(0, 2, 1),
        "upT": a["up_w"].transpose(0, 2, 1),
        "downT": a["down_w"].transpose(0, 2, 1),
    }
    arrays = {f"in_{k}": np.ascontiguousarray(v) for k, v in arrays.items()}
    nc = bacc.Bacc("TRN2", target_bir_lowering=False, num_devices=1)
    args = [nc.dram_tensor(k, v.shape, mybir.dt.from_np(v.dtype), kind="ExternalInput").ap()
            for k, v in arrays.items()]
    out = nc.dram_tensor("out", [B, P, TT, D], F32, kind="ExternalOutput").ap()
    decoder_layer(nc, *args, out)
    r = run_bass_kernel_spmd(nc, [arrays], core_ids=[0])
    return r.results[0]["out"].reshape(B, P, TT, D).transpose(0, 2, 1, 3).reshape(B, L, D)
```

```python
from contextlib import ExitStack

import concourse.bass as bass
from concourse import mybir

F32 = mybir.dt.float32
BF16 = mybir.dt.bfloat16
ALU = mybir.AluOpType
ACT = mybir.ActivationFunctionType
AX = mybir.AxisListType

P = 128
B, L, D = 4, 512, 512
TT = L // P
KD = D // P
DIN, HEADS, HD, N, CHUNK, KC = 1024, 64, 16, 128, 64, 4
CONV = DIN + 2 * N
PROJ = DIN + CONV + HEADS
NCC = CONV // P
NX = DIN // P
DTC = DIN + CONV
UH = 8
UPT = HEADS // UH
U = TT * UPT
IQ = 256
E, I = 8, 1024
EPS = 1e-5
QEPS, QMAX, MAGIC = 1e-6, 127.0, 12582912.0
TOP_P = 0.9
NT = B * TT
PAIR = 2
PIECES = 12
IC = I // P
LEAD = 5
XSTEPS = LEAD + NCC + 5
PUT = [0, 0.5, 1, 2, 3, 4, 4.5, 5, 5.5, 6, 7, 8, 9, 10, 10.5, 11, 12, 13, 14, 15, 15.5, 16, 17, 17.5]
MERGED = sorted([("x", j, (j + 0.1) / XSTEPS) for j in range(XSTEPS)]
                + [("q", j, (n + 0.4) / len(PUT)) for n, j in enumerate(PUT)], key=lambda v: v[2])
MERGED = [(what, j) for what, j, _ in MERGED]
CONSTS = 22


class Count:

    def __init__(self, ctx, nc, name, per):
        self.sem, self.per = ctx.enter_context(nc.semaphore(name)), per

    def at(self, i, k):
        return i * self.per + (self.per + k)

    def before(self, i, k):
        return i * self.per + k


class Own:

    def __init__(self, count, eng, i):
        self.c, self.eng, self.i, self.n = count, eng, i, 0

    def link(self, ins):
        self.n += 1
        ins.then_inc(self.c.sem, 1)
        self.eng.wait_ge(self.c.sem, self.c.at(self.i, self.n))

    def close(self):
        assert self.n <= self.c.per, self.n
        if self.n < self.c.per:
            self.eng.sem_inc(self.c.sem, self.c.per - self.n)


def decoder_layer(nc, x, guw, guwT, dnw, dnwT, winT, conv_w, conv_b, dt_bias, a_log, d_skip,
                  norm_w, woutT, rwT, gateT, upT, downT, out):
    x2_dram = nc.dram_tensor("x2_dram", [B, P, TT, D], F32, kind="Internal").ap()
    zh_dram = nc.dram_tensor("zh_dram", [B, TT, P, KD, P], BF16, kind="Internal").ap()
    zl_dram = nc.dram_tensor("zl_dram", [B, TT, P, KD, P], BF16, kind="Internal").ap()
    wt_dram = nc.dram_tensor("wt_dram", [B, P, E * TT], F32, kind="Internal").ap()
    first_pass(nc, x, guw, guwT, dnw, dnwT, winT, conv_w, conv_b, dt_bias, a_log, d_skip,
               norm_w, woutT, rwT, x2_dram, zh_dram, zl_dram, wt_dram)
    expert_pass(nc, gateT, upT, downT, x2_dram, zh_dram, zl_dram, wt_dram, out)


def first_pass(nc, x, guw, guwT, dnw, dnwT, winT, conv_w, conv_b, dt_bias, a_log, d_skip,
               norm_w, woutT, rwT, x2_dram, zh_dram, zl_dram, wt_dram):
    with ExitStack() as ctx:
        def sb(name, shape, dt=F32):
            return ctx.enter_context(nc.sbuf_tensor(name, shape, dt))

        def sem(name):
            return ctx.enter_context(nc.semaphore(name))

        counts = []

        def count(name, per):
            counts.append(Count(ctx, nc, name, per))
            return counts[-1]

        ps = ctx.enter_context(nc.psum_tensor("ps", [P, 8, 512], F32))

        win_h = sb("win_h", [P, KD, PROJ], BF16)
        win_l = sb("win_l", [P, KD, PROJ], BF16)
        wout_h = sb("wout_h", [P, NX, D], BF16)
        wout_l = sb("wout_l", [P, NX, D], BF16)
        rw = sb("rw", [P, KD, E])
        cw = sb("cw", [P, NCC, KC])
        cb = sb("cb", [P, NCC])
        dtb_bc = sb("dtb_bc", [P, HEADS])
        alog_bc = sb("alog_bc", [P, HEADS])
        expa_bc = sb("expa_bc", [P, HEADS])
        dcol = sb("dcol", [P, NX])
        nw = sb("nw", [P, NX])
        ident = sb("ident", [P, P])
        identb = sb("identb", [P, P], BF16)
        later = sb("later", [P, P], BF16)
        upto = sb("upto", [P, CHUNK, UH], BF16)
        incl = sb("incl", [P, P])
        in_a = sb("in_a", [P, P])
        in_b = sb("in_b", [P, P])
        gmask = sb("gmask", [P, CHUNK])
        tie = sb("tie", [P, E, E])
        xc = sb("xc", [P, TT, D])
        zn = sb("zn", [P, TT, D])
        st6 = sb("st6", [P, TT, 6])
        mv = sb("mv", [P, TT, 2])
        ve = sb("ve", [P, TT])
        sd = sb("sd", [P, TT])
        r0 = sb("r0", [P, TT])
        r1 = sb("r1", [P, TT])
        rs = sb("rs", [P, TT])
        ssq = sb("ssq", [P, TT])
        xin = sb("xin", [P, TT, D])
        mvx = sb("mvx", [P, TT, 2])
        vex = sb("vex", [P, TT])
        sdx = sb("sdx", [P, TT])
        rsx = sb("rsx", [P, TT])
        xnh = sb("xnh", [P, KD, L], BF16)
        xnl = sb("xnl", [P, KD, L], BF16)
        xraw = sb("xraw", [P, 2, KC - 1 + L])
        cacc = sb("cacc", [P, 2, L])
        bT = sb("bT", [P, L])
        cT = sb("cT", [P, L])
        btok = sb("btok", [P, TT, N])
        big = sb("big", [P, 3 * TT * DIN])
        xall = big[:, 0:NX * L].rearrange("p (k t) -> p k t", k=NX)
        xdt = big[:, TT * DIN:2 * TT * DIN].rearrange("p (t c) -> p t c", t=TT)
        gs = big[:, 2 * TT * DIN:3 * TT * DIN].rearrange("p (t c) -> p t c", t=TT)
        dtv = sb("dtv", [P, TT, HEADS])
        dta = sb("dta", [P, TT, HEADS])
        dte = sb("dte", [P, TT, HEADS])
        dt = sb("dt", [P, TT, HEADS])
        da = sb("da", [P, TT, HEADS])
        dah = sb("dah", [P, TT, HEADS], BF16)
        dal = sb("dal", [P, TT, HEADS], BF16)
        S = sb("S", [P, DIN])
        edec = sb("edec", [P, 2, TT, HEADS])
        cdec = sb("cdec", [P, 2, TT, HEADS])
        gm = sb("gm", [P, TT, CHUNK])
        scr = sb("scr", [P, 6656])
        bh = scr[:, 0:512].bitcast(BF16).rearrange("p (b t h) -> p b t h", b=2, t=CHUNK)
        bl = scr[:, 512:1024].bitcast(BF16).rearrange("p (b t h) -> p b t h", b=2, t=CHUNK)
        mu = scr[:, 2048:4096].bitcast(BF16).rearrange("p (s b c t h) -> p s b c t h", s=2, b=2, c=2, t=CHUNK)
        xdd = scr[:, 4096:5120]
        y = scr[:, 5120:6144]
        junk = scr[:, 6144:6656].bitcast(BF16)
        hth = scr[:, 0:1024].bitcast(BF16).rearrange("p (b k t) -> p b k t", b=2, k=NX)
        htl = scr[:, 1024:2048].bitcast(BF16).rearrange("p (b k t) -> p b k t", b=2, k=NX)
        qxT = scr[:, 0:1024].bitcast(BF16).rearrange("p (k t) -> p k t", k=KD)
        qwT = scr[:, 1024:2048].bitcast(BF16).rearrange("p (k t) -> p k t", k=KD)
        wnat = scr[:, 2048:4096].rearrange("p (t d) -> p t d", t=TT)
        w2nat = scr[:, 2048:3072].rearrange("p (t d) -> p t d", t=TT)
        w2Tr = scr[:, 3072:4096].rearrange("p (t d) -> p t d", t=2)
        wTr = scr[:, 4096:6144].rearrange("p (t d) -> p t d", t=TT)
        qx = scr[:, 4096:5120].bitcast(BF16).rearrange("p (t d) -> p t d", t=TT)
        qw = scr[:, 5120:6144].bitcast(BF16).rearrange("p (t d) -> p t d", t=TT)
        wscb = scr[:, 6144:6656]
        axm = sb("axm", [P, KD])
        awm = sb("awm", [P, KD])
        ra = sb("ra", [P, KD])
        sm = sb("sm", [P, KD])
        sq0 = sb("sq0", [P, KD])
        sr = sb("sr", [P, KD])
        xsc = sb("xsc", [P, TT])
        wsc = sb("wsc", [P, TT])
        rx = sb("rx", [P, TT])
        rw_ = sb("rw_", [P, TT])
        hq = sb("hq", [P, 2, D])
        sg = sb("sg", [P, 2, IQ])
        av = zn[:, :, 0:IQ]
        eu = [v.rearrange("p (t h) -> p t h", t=CHUNK) for v in (scr[:, 1024:1536], scr[:, 1536:2048], hq[:, 0, :])]
        xsp = zn[:].rearrange("p t d -> p (t d)").bitcast(BF16).rearrange("p (b s c) -> p b s c", b=2, s=2)
        zTf = sb("zTf", [P, KD, P])
        z3h = sb("z3h", [P, 2, KD, P], BF16)
        z3l = sb("z3l", [P, 2, KD, P], BF16)
        mx = sb("mx", [P, TT])
        lg = sb("lg", [P, TT, E])
        pe_ = sb("pe_", [P, TT, E])
        pr = sb("pr", [P, TT, E])
        gt = scr[:, 4096:4352].rearrange("p (t a b) -> p t a b", t=TT, a=E)
        eq = scr[:, 4352:4608].rearrange("p (t a b) -> p t a b", t=TT, a=E)
        sums = sb("sums", [P, TT])
        mass = sb("mass", [P, TT, E])
        keep = sb("keep", [P, TT, E])
        wt = sb("wt", [P, E, TT])

        s_win = [sem(f"s_win{k}") for k in range(KD)]
        s_wsplit = sem("s_wsplit")
        s_wout = sem("s_wout")
        s_small = sem("s_small")
        s_const = sem("s_const")
        s_wh = sem("s_wh")
        s_wl = sem("s_wl")
        s_expa = sem("s_expa")
        s_pass = sem("s_pass")
        ldx = count("ldx", 16)
        ldc = count("ldc", 16)
        ldq = count("ldq", 32)
        ldq2 = count("ldq2", 32)
        stx = count("stx", 16)
        stz = [count(f"stz{b}", 64) for b in range(2)]
        stw = count("stw", 16)
        own_v = count("own_v", 130)
        own_x = count("own_x", 40)
        own_a = count("own_a", 8)
        var_x = count("var_x", 1)
        std_x = count("std_x", 1)
        zxr = count("zxr", TT)
        var_in = count("var_in", 3)
        std_out = count("std_out", 3)
        znr = count("znr", 2 * TT)
        t1 = count("t1", TT)
        t1h = count("t1h", TT)
        t1l = count("t1l", TT)
        pj = count("pj", NCC)
        raw = count("raw", NCC)
        cv = count("cv", NCC)
        act_x = count("act_x", NCC)
        xt = count("xt", NX + 1)
        xta = count("xta", NX + 1)
        xtd = count("xtd", NX)
        dtp = count("dtp", 1)
        v_in = count("v_in", 1)
        sp_out = count("sp_out", 1)
        dar = count("dar", 1)
        cum = count("cum", 2)
        ecd = count("ecd", 2)
        gp = count("gp", 1)
        gmr = count("gmr", 1)
        gate_p = count("gate_p", 2 * TT)
        gate_e = count("gate_e", 2 * TT)
        gate_s = count("gate_s", TT)
        bhi = count("bhi", U)
        blo = count("blo", U)
        seg = count("seg", U)
        ex = count("ex", U)
        prd = count("prd", U)
        mhr = count("mhr", U)
        mr = count("mr", U)
        xhr = count("xhr", TT)
        xlr = count("xlr", TT)
        yd = count("yd", U)
        xddr = count("xddr", TT)
        yo = count("yo", 2 * TT)
        sn = count("sn", 4 * TT)
        su = count("su", 4 * TT)
        sdr = count("sdr", 2 * TT)
        s0 = count("s0", 1)
        ysc = count("ysc", TT)
        yc = count("yc", 2 * TT)
        hgr = count("hgr", TT)
        sqr = count("sqr", TT)
        ht = count("ht", 2 * TT)
        hh = count("hh", 2 * TT)
        hl = count("hl", 2 * TT)
        op = count("op", TT)
        x1r = count("x1r", TT)
        t2 = count("t2", KD + 2)
        t2r = count("t2r", KD + 2)
        rat = count("rat", 2)
        sqt = count("sqt", 2)
        sbr = count("sbr", 2)
        sbp = count("sbp", 2)
        wsr = count("wsr", 2)
        wsp = count("wsp", 2)
        wsb = count("wsb", 2)
        qi = count("qi", 4 * TT)
        qr = count("qr", 4 * TT)
        qt = count("qt", 4 * TT)
        qc = count("qc", 4 * TT)
        qm = count("qm", 2 * TT)
        hr = count("hr", TT)
        sgr = count("sgr", TT)
        ar = count("ar", TT)
        x2r = count("x2r", TT)
        t3 = count("t3", TT)
        t3f = count("t3f", TT)
        t3h = count("t3h", TT)
        t3l = count("t3l", TT)
        lgp = count("lgp", TT)
        lgi = count("lgi", 1)
        lge = count("lge", 1)
        wtr = count("wtr", 1)

        def rows(eng, take_x, scan, put_out, split_in, split_out):
            for j in range(XSTEPS):
                take_x(0, j)
                if j == LEAD - 1:
                    split_in()
            split_out()
            with eng.Fori(0, B - 1) as i:
                scan(i)
                for what, j in MERGED:
                    if what == "x":
                        take_x(i + 1, j)
                    else:
                        put_out(i, j)
            scan(B - 1)
            for j in PUT:
                put_out(B - 1, j)

        block = ctx.enter_context(nc.Block())

        @block.sync
        def _(sp):
            sp.dma_start(xin[:], x[0]).then_inc(ldx.sem, 16)
            for k in range(KD):
                sp.dma_start(big[:, k * PROJ:(k + 1) * PROJ], winT[k * P:(k + 1) * P, :]).then_inc(s_win[k], 16)
            for dst, src in ((rw[:], rwT), (cw[:], conv_w), (cb[:], conv_b), (nw[:], norm_w),
                             (dtb_bc[:], dt_bias.to_broadcast([P, HEADS])),
                             (alog_bc[:], a_log.to_broadcast([P, HEADS])),
                             (dcol[:], d_skip)):
                sp.dma_start(dst, src).then_inc(s_small, 16)
            sp.dma_start(scr[:, 0:NX * D].rearrange("p (k n) -> p k n", k=NX),
                         woutT.rearrange("(k p) n -> p k n", p=P)).then_inc(s_wout, 16)

            def row(i, more):
                sp.wait_ge(stx.sem, stx.before(i, 16))
                sp.wait_ge(znr.sem, znr.before(i, 2 * TT))
                sp.sem_inc(s_pass, 1)
                sp.dma_start(xc[:], x[i]).then_inc(ldc.sem, 16)
                if more:
                    sp.wait_ge(t1.sem, t1.at(i, TT))
                    sp.sem_inc(s_pass, 1)
                    sp.dma_start(xin[:], x[i + 1]).then_inc(ldx.sem, 16)
                sp.wait_ge(su.sem, su.at(i, 4 * TT))
                sp.wait_ge(sqr.sem, sqr.at(i, TT))
                sp.sem_inc(s_pass, 1)
                sp.dma_start(wnat, guw[i]).then_inc(ldq.sem, 16)
                sp.dma_start(wTr, guwT[i]).then_inc(ldq.sem, 16)
                sp.wait_ge(qr.sem, qr.at(i, 2 * TT))
                sp.sem_inc(s_pass, 1)
                sp.dma_start(w2nat, dnw[i]).then_inc(ldq2.sem, 16)
                sp.dma_start(w2Tr, dnwT[i]).then_inc(ldq2.sem, 16)
                sp.wait_ge(x2r.sem, x2r.at(i, TT))
                sp.sem_inc(s_pass, 1)
                sp.dma_start(x2_dram[i], xc[:]).then_inc(stx.sem, 16)
                for tt in range(TT):
                    sp.wait_ge(t3l.sem, t3l.at(i, tt + 1))
                    sp.sem_inc(s_pass, 1)
                    sp.dma_start(zh_dram[i, tt], z3h[:, tt % 2]).then_inc(stz[tt % 2].sem, 16)
                    sp.dma_start(zl_dram[i, tt], z3l[:, tt % 2]).then_inc(stz[tt % 2].sem, 16)
                sp.wait_ge(wtr.sem, wtr.at(i, 1))
                sp.sem_inc(s_pass, 1)
                sp.dma_start(wt_dram[i], wt[:].rearrange("p e t -> p (e t)")).then_inc(stw.sem, 16)

            with sp.Fori(0, B - 1) as i:
                row(i, True)
            row(B - 1, False)
            for c in (stx, stz[0], stz[1], stw):
                sp.wait_ge(c.sem, c.per * (B + 1))

        @block.gpsimd
        def _(pool):
            for c in counts:
                pool.sem_inc(c.sem, c.per)
            done = [0]

            def step(ins):
                done[0] += 1
                ins.then_inc(s_const, 1)
                pool.wait_ge(s_const, done[0])

            def select(view, op, fill, pattern, mult):
                step(nc.gpsimd.affine_select(out=view, in_=view, compare_op=op, fill=fill, base=0,
                                             pattern=pattern, channel_multiplier=mult))

            for t, v in ((ident, 0.0), (identb, 0.0), (later, 0.0), (incl, 0.0),
                         (upto, 1.0), (gmask, 1.0), (tie, 1.0), (in_a, 0.0), (in_b, 0.0)):
                step(nc.gpsimd.memset(t[:], v))
            for t in (ident, identb):
                select(t[:], ALU.not_equal, 1.0, [[-1, P]], 1)
            select(tie[:], ALU.is_gt, 0.0, [[1, E], [-1, E]], 0)
            step(nc.gpsimd.memset(in_a[0:CHUNK, :], 1.0))
            step(nc.gpsimd.memset(in_b[CHUNK:P, :], 1.0))
            for h in (0, CHUNK):
                r = slice(h, h + CHUNK)
                select(later[r, r], ALU.is_ge, 1.0, [[1, CHUNK]], -1)
                select(incl[r, r], ALU.is_gt, 1.0, [[-1, CHUNK]], 1)
                select(upto[r], ALU.is_ge, 0.0, [[1, CHUNK], [0, UH]], -1)
                select(gmask[r], ALU.is_ge, 0.0, [[1, CHUNK]], -1)
            assert done[0] == CONSTS
            pool.wait_ge(s_small, 7 * 16)

            def scan(i):
                pool.wait_ge(x2r.sem, x2r.before(i, TT))
                pool.wait_ge(wtr.sem, wtr.before(i, 1))

                def low(u):
                    tt, q = divmod(u, UPT)
                    if u >= 2:
                        pool.wait_ge(seg.sem, seg.at(i, u - 1))
                    nc.gpsimd.tensor_tensor(
                        bl[:, u % 2], dal[:, tt, q * UH:(q + 1) * UH].unsqueeze(1).to_broadcast([P, CHUNK, UH]),
                        upto[:], ALU.mult).then_inc(blo.sem, 1)

                def to_end(tt):
                    if tt:
                        pool.wait_ge(sn.sem, sn.at(i, 4 * tt))
                    nc.gpsimd.tensor_tensor(
                        xdd[:].rearrange("p (h d) -> p h d", h=HEADS),
                        xdt[:, tt, :].rearrange("p (h d) -> p h d", h=HEADS),
                        edec[:, 1, tt, :].unsqueeze(2).to_broadcast([P, HEADS, HD]),
                        ALU.mult).then_inc(xddr.sem, 1)

                def gated(tt):
                    pool.wait_ge(yc.sem, yc.at(i, 2 * tt + 2))
                    pool.wait_ge(gate_s.sem, gate_s.at(i, tt + 1))
                    nc.gpsimd.tensor_tensor(gs[:, tt, :], y[:], gs[:, tt, :], ALU.mult).then_inc(hgr.sem, 1)

                def state_decay(tt, c):
                    pool.wait_ge(yo.sem, yo.at(i, 2 * tt + c + 1))
                    v = S[:].rearrange("p (h d) -> p h d", h=HEADS)
                    nc.gpsimd.tensor_tensor(v, v, cdec[:, c, tt, :].unsqueeze(2).to_broadcast([P, HEADS, HD]),
                                            ALU.mult).then_inc(sdr.sem, 1)

                def x_low(tt):
                    pool.wait_ge(xhr.sem, xhr.at(i, tt + 1))
                    nc.gpsimd.tensor_tensor(xsp[:, tt % 2, 1, :], xdt[:, tt, :], xsp[:, tt % 2, 0, :],
                                            ALU.subtract).then_inc(xlr.sem, 1)

                pool.wait_ge(s_wl, KD + NX)
                pool.wait_ge(dar.sem, dar.at(i, 1))
                low(0)
                low(1)
                pool.wait_ge(ecd.sem, ecd.at(i, 2))
                pool.wait_ge(xtd.sem, xtd.at(i, NX))
                x_low(0)
                low(2)
                to_end(0)
                for u in range(U):
                    tt, q = divmod(u, UPT)
                    if u + 3 < U:
                        low(u + 3)
                    if q in (0, 3):
                        state_decay(tt, q // 3)
                    if q == 2 and tt:
                        gated(tt - 1)
                    if q == 5 and tt + 1 < TT:
                        x_low(tt + 1)
                    if q == 6 and tt + 1 < TT:
                        to_end(tt + 1)
                gated(TT - 1)

            with pool.Fori(0, B) as i:
                scan(i)

        @block.scalar
        def _(act):
            def split_in():
                act.wait_ge(s_small, 7 * 16)
                nc.scalar.activation(expa_bc[:], alog_bc[:], ACT.Exp).then_inc(s_expa, 1)
                for k in range(KD):
                    act.wait_ge(s_win[k], 16)
                    nc.scalar.activation(win_h[:, k, :], big[:, k * PROJ:(k + 1) * PROJ],
                                         ACT.Copy).then_inc(s_wh, 1)

            def split_out():
                act.wait_ge(s_wout, 16)
                for k in range(NX):
                    nc.scalar.activation(wout_h[:, k, :], scr[:, k * D:(k + 1) * D], ACT.Identity,
                                         scale=nw[:, k:k + 1]).then_inc(s_wh, 1)

            def take_x(i, j):
                def conv_in(n):
                    cc = (n + NX) if n < 2 else n - 2
                    act.wait_ge(pj.sem, pj.at(i, n + 1))
                    if n >= 2:
                        act.wait_ge(cv.sem, cv.at(i, n - 1))
                        act.wait_ge(act_x.sem, act_x.at(i, n - 1))
                    nc.scalar.activation(xraw[:, n % 2, KC - 1:], ps[:, 2 + n % 2, :], ACT.Copy)
                    nc.scalar.activation(cacc[:, n % 2, :], ps[:, 2 + n % 2, :], ACT.Identity,
                                         bias=cb[:, cc:cc + 1],
                                         scale=cw[:, cc, KC - 1:KC]).then_inc(raw.sem, 1)

                def conv_out(n):
                    act.wait_ge(cv.sem, cv.at(i, n + 1))
                    dst = (bT[:], cT[:])[n] if n < 2 else xall[:, n - 2, :]
                    nc.scalar.activation(dst, cacc[:, n % 2, :], ACT.Silu).then_inc(act_x.sem, 1)

                def back(j):
                    act.wait_ge(xt.sem, xt.at(i, j + 1))
                    if j == 0:
                        nc.scalar.activation(btok[:], ps[:, 0, :].rearrange("p (t c) -> p t c", t=TT),
                                             ACT.Copy).then_inc(xta.sem, 1)
                    else:
                        nc.scalar.activation(xall[:, j - 1, :], xall[:, j - 1, :], ACT.Identity,
                                             scale=dcol[:, j - 1:j]).then_inc(xta.sem, 1)

                n = j - LEAD
                if j == 0:
                    act.wait_ge(var_x.sem, var_x.at(i, 1))
                    nc.scalar.activation(sdx[:], vex[:], ACT.Sqrt).then_inc(std_x.sem, 1)
                if j == 3:
                    act.wait_ge(su.sem, su.before(i, 4 * TT))
                    act.wait_ge(hgr.sem, hgr.before(i, TT))
                    for tt in range(TT):
                        act.wait_ge(t1.sem, t1.at(i, tt + 1))
                        nc.scalar.activation(xnh[:, :, tt * P:(tt + 1) * P],
                                             ps[:, tt, :].rearrange("p (k t) -> p k t", k=KD),
                                             ACT.Copy).then_inc(t1h.sem, 1)
                if n == 2:
                    act.wait_ge(v_in.sem, v_in.at(i, 1))
                    own = Own(own_a, act, i)
                    own.link(nc.scalar.activation(dte[:], dta[:], ACT.Exp, scale=-1.0))
                    nc.scalar.activation(dte[:], dte[:], ACT.Ln, bias=1.0).then_inc(sp_out.sem, 1)
                    own.close()
                if n == 5:
                    act.wait_ge(cum.sem, cum.at(i, 1))
                    nc.scalar.activation(edec[:].rearrange("p c t h -> p (c t h)"), ps[:, 4, :],
                                         ACT.Exp).then_inc(ecd.sem, 1)
                if n == 7:
                    act.wait_ge(cum.sem, cum.at(i, 2))
                    nc.scalar.activation(cdec[:].rearrange("p c t h -> p (c t h)"), ps[:, 4, :],
                                         ACT.Exp).then_inc(ecd.sem, 1)
                if 3 <= n <= NCC + 2:
                    conv_out(n - 3)
                if 1 <= n <= NCC:
                    conv_in(n - 1)
                if n == 5:
                    back(0)
                if n >= 7:
                    back(n - 6)

            def scan(i):
                def square(tt):
                    act.wait_ge(hgr.sem, hgr.at(i, tt + 1))
                    if tt:
                        act.wait_ge(sqr.sem, sqr.at(i, tt))
                    nc.scalar.activation(junk, gs[:, tt, :], ACT.Square,
                                         accum_out=ssq[:, tt:tt + 1]).then_inc(sqr.sem, 1)

                def gate_out(g):
                    act.wait_ge(gate_p.sem, gate_p.at(i, g + 1))
                    nc.scalar.activation(gs[:, g // 2, (g % 2) * 512:(g % 2 + 1) * 512], ps[:, 5, :],
                                         ACT.Copy).then_inc(gate_e.sem, 1)

                def gate_silu(tt):
                    act.wait_ge(gate_e.sem, gate_e.at(i, 2 * tt + 2))
                    nc.scalar.activation(gs[:, tt, :], gs[:, tt, :], ACT.Silu).then_inc(gate_s.sem, 1)

                def decays(u):
                    act.wait_ge(seg.sem, seg.at(i, u + 1))
                    if u >= 3:
                        act.wait_ge(mr.sem, mr.at(i, u - 2))
                    nc.scalar.activation(eu[u % 3].rearrange("p t h -> p (t h)"), ps[:, u % 2, :],
                                         ACT.Exp).then_inc(ex.sem, 1)

                def high(u):
                    act.wait_ge(prd.sem, prd.at(i, u + 1))
                    if u >= 2:
                        act.wait_ge(yd.sem, yd.at(i, u - 1))
                    for c in range(2):
                        r = slice(c * CHUNK, (c + 1) * CHUNK)
                        ins = nc.scalar.activation(mu[r, 0, u % 2, c], eu[u % 3][r], ACT.Copy)
                    ins.then_inc(mhr.sem, 1)

                def x_high(tt):
                    if tt >= 2:
                        act.wait_ge(yd.sem, yd.at(i, (tt - 1) * UPT))
                    nc.scalar.activation(xsp[:, tt % 2, 0, :], xdt[:, tt, :], ACT.Copy).then_inc(xhr.sem, 1)

                act.wait_ge(x2r.sem, x2r.before(i, TT))
                act.wait_ge(t3.sem, t3.before(i, TT))
                act.wait_ge(xtd.sem, xtd.at(i, NX))
                x_high(0)
                decays(0)
                decays(1)
                high(0)
                for u in range(U):
                    tt, q = divmod(u, UPT)
                    if u == 4:
                        act.wait_ge(ht.sem, ht.before(i, 2 * TT))
                    if u and q % 4 == 0:
                        gate_out(u // 4 - 1)
                    if u + 2 < U:
                        decays(u + 2)
                    if u + 1 < U:
                        high(u + 1)
                    if q == 0 and tt:
                        gate_silu(tt - 1)
                    if q == 3 and tt + 1 < TT:
                        x_high(tt + 1)
                    if q == 6 and tt:
                        square(tt - 1)
                gate_out(2 * TT - 1)
                gate_silu(TT - 1)
                square(TT - 1)

            def put_out(i, j):
                if j % 1:
                    return

                def root(k):
                    act.wait_ge(var_in.sem, var_in.at(i, k + 1))
                    nc.scalar.activation(sd[:], ve[:], ACT.Sqrt).then_inc(std_out.sem, 1)

                lin = j >= 10
                n = 2 if lin else KD
                if j < TT:
                    if j == 0:
                        act.wait_ge(su.sem, su.at(i, 4 * TT))
                        act.wait_ge(sqr.sem, sqr.at(i, TT))
                    for g in (2 * j, 2 * j + 1):
                        act.wait_ge(ht.sem, ht.at(i, g + 1))
                        if g >= 4:
                            act.wait_ge(op.sem, op.at(i, g // 2 - 1))
                        nc.scalar.activation(hth[:, g // 2 % 2, (g % 2) * 4:(g % 2) * 4 + 4, :],
                                             ps[:, 5 + g % 2, :].rearrange("p (k t) -> p k t", k=4),
                                             ACT.Copy).then_inc(hh.sem, 1)
                    if j == 0:
                        root(0)
                elif j == 4:
                    root(1)
                elif j in (5, 10):
                    act.wait_ge(rat.sem, rat.at(i, lin + 1))
                    nc.scalar.activation(sq0[:, 0:n], ra[:, 0:n], ACT.Sqrt).then_inc(sqt.sem, 1)
                elif j in (7, 12):
                    act.wait_ge(wsp.sem, wsp.at(i, lin + 1))
                    if lin:
                        act.wait_ge(hr.sem, hr.at(i, TT))
                    nc.scalar.activation(wscb, ps[:, 7, :], ACT.Copy).then_inc(wsb.sem, 1)
                    if lin:
                        act.wait_ge(qt.sem, qt.at(i, 2 * TT))
                    w = IQ if lin else D
                    src, wn = (av, w2nat) if lin else (zn[:], wnat)
                    for g in range(2 * TT):
                        act.wait_ge(qi.sem, qi.at(i, 2 * TT * lin + g + 1))
                        v, q = (src, qx) if g % 2 == 0 else (wn, qw)
                        nc.scalar.activation(q[:, g // 2, 0:w], v[:, g // 2, :], ACT.Copy,
                                             bias=-MAGIC).then_inc(qr.sem, 1)
                elif j in (8, 13):
                    for g in range(2 * TT):
                        act.wait_ge(qt.sem, qt.at(i, 2 * TT * lin + g + 1))
                        if lin and g == 0:
                            act.wait_ge(qm.sem, qm.at(i, TT))
                        dst = (qxT if g % 2 == 0 else qwT)[:, 0:n, (g // 2) * P:(g // 2 + 1) * P]
                        src = ps[:, 5 + g % 2, 0:64 * n].bitcast(BF16).rearrange("p (k t) -> p k t", k=n)
                        nc.scalar.activation(dst, src, ACT.Copy).then_inc(qc.sem, 1)
                elif j == 9:
                    for tt in range(TT):
                        act.wait_ge(hr.sem, hr.at(i, tt + 1))
                        nc.scalar.activation(sg[:, tt % 2, :], hq[:, tt % 2, 0:IQ],
                                             ACT.Silu).then_inc(sgr.sem, 1)
                elif j == 15:
                    root(2)
                elif j == 16:
                    for tt in range(TT):
                        act.wait_ge(t3.sem, t3.at(i, tt + 1))
                        if tt:
                            act.wait_ge(lgp.sem, lgp.at(i, tt))
                        nc.scalar.activation(zTf[:], ps[:, 5 + tt % 2, :].rearrange("p (k t) -> p k t", k=KD),
                                             ACT.Copy).then_inc(t3f.sem, 1)
                        if tt < 2:
                            act.wait_ge(stz[tt].sem, stz[tt].before(i, 64))
                        else:
                            act.wait_ge(stz[tt % 2].sem, stz[tt % 2].at(i, 32))
                        nc.scalar.activation(z3h[:, tt % 2], ps[:, 5 + tt % 2, :].rearrange("p (k t) -> p k t", k=KD),
                                             ACT.Copy).then_inc(t3h.sem, 1)
                elif j == 17:
                    act.wait_ge(lgi.sem, lgi.at(i, 1))
                    nc.scalar.activation(pe_[:], lg[:], ACT.Exp).then_inc(lge.sem, 1)

            rows(act, take_x, scan, put_out, split_in, split_out)

        @block.vector
        def _(dve):
            nc.vector.memset(xraw[:], 0.0).then_inc(s_wsplit, 1)

            def split_in():
                for k in range(KD):
                    dve.wait_ge(s_wh, k + 1)
                    nc.vector.tensor_tensor(win_l[:, k, :], big[:, k * PROJ:(k + 1) * PROJ], win_h[:, k, :],
                                            ALU.subtract).then_inc(s_wl, 1)
                dve.wait_ge(s_const, CONSTS)
                dve.wait_ge(s_small, 7 * 16)
                dve.wait_ge(s_expa, 1)

            def split_out():
                for k in range(NX):
                    dve.wait_ge(s_wh, KD + k + 1)
                    nc.vector.scalar_tensor_tensor(out=wout_l[:, k, :], in0=scr[:, k * D:(k + 1) * D],
                                                   scalar=nw[:, k:k + 1], in1=wout_h[:, k, :], op0=ALU.mult,
                                                   op1=ALU.subtract).then_inc(s_wl, 1)
                dve.wait_ge(s_wl, KD + NX)

            def inv_root(link, std, k, v, d, r):
                dve.wait_ge(std.sem, k)
                link(nc.vector.reciprocal(r0[:], d[:]))
                link(nc.vector.tensor_tensor(r1[:], r0[:], r0[:], ALU.mult))
                link(nc.vector.tensor_tensor(r1[:], r1[:], v[:], ALU.mult))
                link(nc.vector.tensor_scalar(r1[:], r1[:], -0.5, 1.5, ALU.mult, ALU.add))
                link(nc.vector.tensor_tensor(r[:], r1[:], r0[:], ALU.mult))

            def moments(link, src, m, v, var):
                for tt in range(TT):
                    ins = nc.vector.bn_stats(st6[:, tt, :], src[:, tt, :])
                link(ins)
                dve.sem_inc(s_pass, 1)
                for tt in range(TT):
                    ins = nc.vector.bn_aggr(m[:, tt, :], st6[:, tt, :])
                link(ins)
                nc.vector.tensor_scalar(v[:], m[:, :, 1], EPS, None, ALU.add).then_inc(var.sem, 1)

            def norm(link, src, dst, m, v, d, r, std, k, ready):
                inv_root(link, std, k, v, d, r)
                for tt in range(TT):
                    nc.vector.tensor_scalar(dst[:, tt, :], src[:, tt, :], m[:, tt, 0:1], r[:, tt:tt + 1],
                                            ALU.subtract, ALU.mult).then_inc(ready.sem, 1)

            owns = {}

            def take_x(i, j):
                if j == 0:
                    owns["x"] = Own(own_x, dve, i)
                link = owns["x"].link

                def conv(n):
                    cc = (n + NX) if n < 2 else n - 2
                    dve.wait_ge(raw.sem, raw.at(i, n + 1))
                    for j in range(KC - 1):
                        ins = nc.vector.scalar_tensor_tensor(
                            out=cacc[:, n % 2, :], in0=xraw[:, n % 2, j:j + L], scalar=cw[:, cc, j:j + 1],
                            in1=cacc[:, n % 2, :], op0=ALU.mult, op1=ALU.add)
                        if j < KC - 2:
                            link(ins)
                    ins.then_inc(cv.sem, 1)

                def back(j):
                    dve.wait_ge(xt.sem, xt.at(i, j + 1))
                    h = P // HD
                    for tt in range(TT):
                        ins = nc.vector.tensor_tensor(
                            xdt[:, tt, (j - 1) * P:j * P].rearrange("p (h d) -> p h d", h=h),
                            ps[:, j % 2, tt * P:(tt + 1) * P].rearrange("p (h d) -> p h d", h=h),
                            dt[:, tt, (j - 1) * h:j * h].unsqueeze(2).to_broadcast([P, h, HD]), ALU.mult)
                    ins.then_inc(xtd.sem, 1)

                n = j - LEAD
                if j == 0:
                    dve.wait_ge(ldx.sem, ldx.at(i, 16))
                    moments(link, xin, mvx, vex, var_x)
                if j == 1:
                    norm(link, xin, xin, mvx, vex, sdx, rsx, std_x, std_x.at(i, 1), zxr)
                if j == 4:
                    dve.wait_ge(hgr.sem, hgr.before(i, TT))
                    dve.wait_ge(su.sem, su.before(i, 4 * TT))
                    for tt in range(TT):
                        dve.wait_ge(t1h.sem, t1h.at(i, tt + 1))
                        nc.vector.tensor_tensor(xnl[:, :, tt * P:(tt + 1) * P],
                                                ps[:, tt, :].rearrange("p (k t) -> p k t", k=KD),
                                                xnh[:, :, tt * P:(tt + 1) * P], ALU.subtract).then_inc(t1l.sem, 1)
                if n == 1:
                    dve.wait_ge(dtp.sem, dtp.at(i, 1))
                    link(nc.vector.tensor_tensor(dtv[:], ps[:, 4, 0:TT * HEADS].rearrange("p (t h) -> p t h", t=TT),
                                                 dtb_bc[:].unsqueeze(1).to_broadcast([P, TT, HEADS]), ALU.add))
                    nc.vector.scalar_tensor_tensor(out=dta[:], in0=dtv[:], scalar=-1.0, in1=dtv[:],
                                                   op0=ALU.mult, op1=ALU.max).then_inc(v_in.sem, 1)
                if n == 3:
                    dve.wait_ge(sp_out.sem, sp_out.at(i, 1))
                    link(nc.vector.scalar_tensor_tensor(out=dt[:], in0=dtv[:], scalar=0.0, in1=dte[:],
                                                        op0=ALU.max, op1=ALU.add))
                    link(nc.vector.scalar_tensor_tensor(
                        out=da[:], in0=dt[:], scalar=-1.0,
                        in1=expa_bc[:].unsqueeze(1).to_broadcast([P, TT, HEADS]),
                        op0=ALU.mult, op1=ALU.mult))
                    link(nc.vector.tensor_copy(dah[:], da[:]))
                    nc.vector.tensor_tensor(dal[:], da[:], dah[:], ALU.subtract).then_inc(dar.sem, 1)
                if 2 <= n <= NCC + 1:
                    conv(n - 2)
                if n == 9:
                    dve.wait_ge(gp.sem, gp.at(i, 1))
                    nc.vector.tensor_tensor(gm[:], ps[:, 4, 0:TT * CHUNK].rearrange("p (t c) -> p t c", t=TT),
                                            gmask[:].unsqueeze(1).to_broadcast([P, TT, CHUNK]),
                                            ALU.mult).then_inc(gmr.sem, 1)
                if n >= 7:
                    back(n - 6)
                if j == XSTEPS - 1:
                    owns["x"].close()

            def scan(i):
                owns["v"] = Own(own_v, dve, i)
                link = owns["v"].link

                def high(u):
                    tt, q = divmod(u, UPT)
                    if u >= 2:
                        dve.wait_ge(seg.sem, seg.at(i, u - 1))
                    nc.vector.tensor_tensor(
                        bh[:, u % 2], dah[:, tt, q * UH:(q + 1) * UH].unsqueeze(1).to_broadcast([P, CHUNK, UH]),
                        upto[:], ALU.mult).then_inc(bhi.sem, 1)

                def product(u):
                    dve.wait_ge(ex.sem, ex.at(i, u + 1))
                    nc.vector.tensor_tensor(eu[u % 3], eu[u % 3],
                                            gm[:, u // UPT, :].unsqueeze(2).to_broadcast([P, CHUNK, UH]),
                                            ALU.mult).then_inc(prd.sem, 1)

                def low(u):
                    dve.wait_ge(mhr.sem, mhr.at(i, u + 1))
                    for c in range(2):
                        r = slice(c * CHUNK, (c + 1) * CHUNK)
                        ins = nc.vector.tensor_tensor(mu[r, 1, u % 2, c], eu[u % 3][r], mu[r, 0, u % 2, c],
                                                      ALU.subtract)
                    ins.then_inc(mr.sem, 1)

                def heads(ap):
                    return ap.rearrange("p (h d) -> p h d", h=HEADS)

                def state(tt, c, a):
                    if a == 0:
                        dve.wait_ge(sdr.sem, sdr.at(i, 2 * tt + c + 1))
                    dve.wait_ge(sn.sem, sn.at(i, 4 * tt + 2 * c + a + 1))
                    half = S[:, a * 512:(a + 1) * 512]
                    nc.vector.tensor_tensor(half, half, ps[:, 4, :], ALU.add).then_inc(su.sem, 1)

                def from_state(tt):
                    if tt:
                        dve.wait_ge(hgr.sem, hgr.at(i, tt))
                    nc.vector.tensor_tensor(
                        heads(y), heads(ps[:, 6:8, :].rearrange("p a b -> p (a b)")),
                        edec[:, 0, tt, :].unsqueeze(2).to_broadcast([P, HEADS, HD]), ALU.mult).then_inc(ysc.sem, 1)

                def combine(tt, a):
                    dve.wait_ge(ysc.sem, ysc.at(i, tt + 1))
                    dve.wait_ge(yd.sem, yd.at(i, tt * UPT + (a + 1) * UPT // 2))
                    half = y[:, a * 512:(a + 1) * 512]
                    nc.vector.tensor_tensor(half, half, ps[:, 2 + a, :], ALU.add).then_inc(yc.sem, 1)

                dve.wait_ge(x2r.sem, x2r.before(i, TT))
                nc.vector.memset(S[:], 0.0).then_inc(s0.sem, 1)
                high(0)
                high(1)
                nc.vector.memset(mu[0:CHUNK, :, :, 1].rearrange("p s b t h -> p (s b) (t h)"), 0.0)
                link(nc.vector.memset(mu[CHUNK:P, :, :, 0].rearrange("p s b t h -> p (s b) (t h)"), 0.0))
                product(0)
                high(2)
                for u in range(U):
                    tt, q = divmod(u, UPT)
                    if u + 1 < U:
                        product(u + 1)
                    low(u)
                    if u + 3 < U:
                        high(u + 3)
                    if q == 0 and tt:
                        combine(tt - 1, 1)
                    if q in (1, 2):
                        state(tt, 0, q - 1)
                    if q in (4, 5):
                        state(tt, 1, q - 4)
                    if q == 6:
                        from_state(tt)
                    if q == 7:
                        combine(tt, 0)
                combine(TT - 1, 1)

            def put_out(i, j):
                link = owns["v"].link
                lin = 1 if j >= 10 else 0
                n = 2 if lin else KD
                ex8 = [P, TT, E]
                w = IQ if lin else D
                src, wn = (av, w2nat) if lin else (zn[:], wnat)

                def add_x1(tt):
                    dve.wait_ge(op.sem, op.at(i, tt + 1))
                    nc.vector.scalar_tensor_tensor(out=xc[:, tt, :], in0=ps[:, 7, :],
                                                   scalar=rs[:, tt:tt + 1], in1=xc[:, tt, :],
                                                   op0=ALU.mult, op1=ALU.add).then_inc(x1r.sem, 1)

                def weight_max(load, wr, n):
                    dve.wait_ge(load.sem, load.at(i, 32))
                    link(nc.vector.tensor_reduce(awm[:, 0:n], wr, AX.X, ALU.max, apply_absolute_value=True))
                    link(nc.vector.tensor_scalar(awm[:, 0:n], awm[:, 0:n], QEPS, None, ALU.max))
                    link(nc.vector.reciprocal(awm[:, 0:n], awm[:, 0:n]))

                if j == 0.5:
                    inv_root(link, std_out, std_out.at(i, 1), ve, sd, rs)
                    dve.wait_ge(ldc.sem, ldc.at(i, 16))
                elif j == 4.5:
                    norm(link, xc, zn, mv, ve, sd, rs, std_out, std_out.at(i, 2), znr)
                elif j == 15.5:
                    norm(link, xc, zn, mv, ve, sd, rs, std_out, std_out.at(i, 3), znr)
                elif j < TT:
                    for g in (2 * j, 2 * j + 1):
                        dve.wait_ge(hh.sem, hh.at(i, g + 1))
                        half = slice((g % 2) * 4, (g % 2) * 4 + 4)
                        nc.vector.tensor_tensor(htl[:, g // 2 % 2, half, :],
                                                ps[:, 5 + g % 2, :].rearrange("p (k t) -> p k t", k=4),
                                                hth[:, g // 2 % 2, half, :], ALU.subtract).then_inc(hl.sem, 1)
                    if j == 0:
                        dve.wait_ge(sqr.sem, sqr.at(i, TT))
                        nc.vector.tensor_scalar(ve[:], ssq[:], 1.0 / DIN, EPS, ALU.mult, ALU.add).then_inc(var_in.sem, 1)
                    else:
                        add_x1(j - 1)
                    if j == TT - 1:
                        weight_max(ldq, wTr, KD)
                elif j == 4:
                    add_x1(TT - 1)
                    dve.wait_ge(x1r.sem, x1r.at(i, TT))
                    moments(link, xc, mv, ve, var_in)
                elif j in (5, 10):
                    for k in range(n):
                        g = lin * KD + k
                        dve.wait_ge(t2.sem, t2.at(i, g + 1))
                        ins = nc.vector.tensor_reduce(axm[:, k:k + 1], ps[:, 5 + g % 2, :], AX.X, ALU.max,
                                                      apply_absolute_value=True)
                        if k < n - 1:
                            ins.then_inc(t2r.sem, 1)
                    ins.then_inc(t2r.sem, 1)
                    dve.wait_ge(t2r.sem, t2r.at(i, lin * KD + n))
                    nc.vector.scalar_tensor_tensor(out=ra[:, 0:n], in0=axm[:, 0:n], scalar=QEPS, in1=awm[:, 0:n],
                                                   op0=ALU.max, op1=ALU.mult).then_inc(rat.sem, 1)
                elif j in (5.5, 10.5):
                    dve.wait_ge(sqt.sem, sqt.at(i, lin + 1))
                    link(nc.vector.reciprocal(sr[:, 0:n], sq0[:, 0:n]))
                    link(nc.vector.tensor_tensor(sr[:, 0:n], sr[:, 0:n], ra[:, 0:n], ALU.mult))
                    link(nc.vector.tensor_tensor(sm[:, 0:n], sr[:, 0:n], sq0[:, 0:n], ALU.add))
                    link(nc.vector.tensor_scalar(sm[:, 0:n], sm[:, 0:n], 0.5, QEPS, ALU.mult, ALU.max))
                    nc.vector.reciprocal(sr[:, 0:n], sm[:, 0:n]).then_inc(sbr.sem, 1)
                elif j in (6, 11):
                    dve.wait_ge(sbp.sem, sbp.at(i, lin + 1))
                    for t in range(TT):
                        nc.vector.tensor_tensor(src[:, t, :], src[:, t, :], ps[:, 6, 0:w], ALU.mult)
                        ins = nc.vector.tensor_tensor(wn[:, t, :], wn[:, t, :], ps[:, 5, 0:w], ALU.mult)
                    link(ins)
                    nc.vector.tensor_reduce(xsc[:], src, AX.X, ALU.max, apply_absolute_value=True)
                    link(nc.vector.tensor_reduce(wsc[:], wn, AX.X, ALU.max, apply_absolute_value=True))
                    nc.vector.tensor_scalar(xsc[:], xsc[:], QEPS, 1.0 / QMAX, ALU.max, ALU.mult)
                    nc.vector.tensor_scalar(wsc[:], wsc[:], QEPS, 1.0 / QMAX, ALU.max,
                                            ALU.mult).then_inc(wsr.sem, 1)
                elif j in (7, 12):
                    dve.wait_ge(wsr.sem, wsr.at(i, lin + 1))
                    nc.vector.reciprocal(rx[:], xsc[:])
                    link(nc.vector.reciprocal(rw_[:], wsc[:]))
                    both = [(v, r, q, t) for t in range(TT) for v, r, q in ((src, rx, qx), (wn, rw_, qw))]
                    for v, r, q, t in both:
                        ins = nc.vector.tensor_scalar(v[:, t, :], v[:, t, :], r[:, t:t + 1], -QMAX,
                                                      ALU.mult, ALU.max)
                    link(ins)
                    for v, r, q, t in both:
                        nc.vector.tensor_scalar(v[:, t, :], v[:, t, :], QMAX, MAGIC, ALU.min,
                                                ALU.add).then_inc(qi.sem, 1)
                elif j in (9, 14):
                    if lin == 0:
                        weight_max(ldq2, w2Tr, 2)
                    dve.wait_ge(wsb.sem, wsb.at(i, lin + 1))
                    for tt in range(TT):
                        dve.wait_ge(qm.sem, qm.at(i, lin * TT + tt + 1))
                        h = hq[:, tt % 2, :]
                        bank = ps[:, 7 if tt % 2 == 0 else 5, :]
                        if lin == 0:
                            if tt >= 2:
                                dve.wait_ge(ar.sem, ar.at(i, tt - 1))
                            else:
                                dve.wait_ge(qr.sem, qr.at(i, 2 * TT))
                            nc.vector.scalar_tensor_tensor(out=h, in0=bank, scalar=xsc[:, tt:tt + 1],
                                                           in1=wscb, op0=ALU.mult, op1=ALU.mult).then_inc(hr.sem, 1)
                            dve.wait_ge(sgr.sem, sgr.at(i, tt + 1))
                            nc.vector.tensor_tensor(av[:, tt, :], sg[:, tt % 2, :], hq[:, tt % 2, IQ:],
                                                    ALU.mult).then_inc(ar.sem, 1)
                        else:
                            link(nc.vector.scalar_tensor_tensor(out=h, in0=bank,
                                                                scalar=xsc[:, tt:tt + 1], in1=wscb,
                                                                op0=ALU.mult, op1=ALU.mult))
                            nc.vector.tensor_tensor(xc[:, tt, :], xc[:, tt, :], h, ALU.add).then_inc(x2r.sem, 1)
                elif j == 15:
                    dve.wait_ge(x2r.sem, x2r.at(i, TT))
                    moments(link, xc, mv, ve, var_in)
                elif j == 16:
                    for tt in range(TT):
                        dve.wait_ge(t3h.sem, t3h.at(i, tt + 1))
                        nc.vector.tensor_tensor(z3l[:, tt % 2], ps[:, 5 + tt % 2, :].rearrange("p (k t) -> p k t", k=KD),
                                                z3h[:, tt % 2], ALU.subtract).then_inc(t3l.sem, 1)
                elif j == 17:
                    dve.wait_ge(lgp.sem, lgp.at(i, TT))
                    link(nc.vector.tensor_copy(lg[:], ps[:, 7, 0:TT * E].rearrange("p (t e) -> p t e", t=TT)))
                    link(nc.vector.tensor_reduce(mx[:], lg[:], AX.X, ALU.max))
                    nc.vector.tensor_tensor(lg[:], lg[:], mx[:].unsqueeze(2).to_broadcast(ex8),
                                            ALU.subtract).then_inc(lgi.sem, 1)
                elif j == 17.5:
                    dve.wait_ge(lge.sem, lge.at(i, 1))
                    link(nc.vector.tensor_reduce(sums[:], pe_[:], AX.X, ALU.add))
                    link(nc.vector.reciprocal(sums[:], sums[:]))
                    link(nc.vector.tensor_tensor(pr[:], pe_[:], sums[:].unsqueeze(2).to_broadcast(ex8), ALU.mult))
                    for tt in range(TT):
                        pj_, pi_ = (pr[:, tt].unsqueeze(1).to_broadcast([P, E, E]),
                                    pr[:, tt].unsqueeze(2).to_broadcast([P, E, E]))
                        nc.vector.tensor_tensor(gt[:, tt], pj_, pi_, ALU.is_gt)
                        ins = nc.vector.tensor_tensor(eq[:, tt], pj_, pi_, ALU.is_equal)
                    link(ins)
                    link(nc.vector.tensor_tensor(eq, eq, tie[:].unsqueeze(1).to_broadcast([P, TT, E, E]), ALU.mult))
                    link(nc.vector.tensor_tensor(gt, gt, eq, ALU.add))
                    link(nc.vector.tensor_tensor(gt, gt, pr[:].unsqueeze(2).to_broadcast([P, TT, E, E]), ALU.mult))
                    link(nc.vector.tensor_reduce(mass[:], gt, AX.X, ALU.add))
                    dve.wait_ge(stw.sem, stw.before(i, 16))
                    link(nc.vector.tensor_scalar(keep[:], mass[:], TOP_P, None, ALU.is_le))
                    nc.vector.tensor_tensor(wt[:].rearrange("p e t -> p t e"), pr[:], keep[:],
                                            ALU.mult).then_inc(wtr.sem, 1)
                    owns["v"].close()

            rows(dve, take_x, scan, put_out, split_in, split_out)

        @block.tensor
        def _(pe):
            pe.wait_ge(s_const, CONSTS)

            def split_in():
                pe.wait_ge(s_small, 7 * 16)
                pe.wait_ge(s_wl, KD)

            def split_out():
                pe.wait_ge(s_wl, KD + NX)

            def mm3(dst, wh, wl, mh, ml, k, last):
                nc.tensor.matmul(dst, wh, mh, start=(k == 0), stop=False)
                nc.tensor.matmul(dst, wh, ml, start=False, stop=False)
                return nc.tensor.matmul(dst, wl, mh, start=False, stop=last)

            def take_x(i, j):
                def proj(n):
                    c0 = DIN + ((n + NX) if n < 2 else n - 2) * P
                    if n == 0:
                        pe.wait_ge(t1l.sem, t1l.at(i, TT))
                    if n >= 2:
                        pe.wait_ge(raw.sem, raw.at(i, n - 1))
                    for k in range(KD):
                        ins = mm3(ps[:, 2 + n % 2, :], win_h[:, k, c0:c0 + P], win_l[:, k, c0:c0 + P],
                                  xnh[:, k, :], xnl[:, k, :], k, k == KD - 1)
                    ins.then_inc(pj.sem, 1)

                def back(j):
                    n = 0 if j == 0 else j + 1
                    src = bT[:] if j == 0 else xall[:, j - 1, :]
                    pe.wait_ge(act_x.sem, act_x.at(i, n + 1))
                    if j >= 2:
                        if j == 2:
                            pe.wait_ge(xta.sem, xta.at(i, 1))
                        else:
                            pe.wait_ge(xtd.sem, xtd.at(i, j - 2))
                    for tt in range(TT):
                        ins = nc.tensor.transpose(ps[:, j % 2, tt * P:(tt + 1) * P],
                                                  src[:, tt * P:(tt + 1) * P], ident[:])
                    ins.then_inc(xt.sem, 1)

                dflat = da[:].rearrange("p t h -> p (t h)")
                n = j - LEAD
                if j == 2:
                    pe.wait_ge(su.sem, su.before(i, 4 * TT))
                    pe.wait_ge(hgr.sem, hgr.before(i, TT))
                    for tt in range(TT):
                        pe.wait_ge(zxr.sem, zxr.at(i, tt + 1))
                        for k in range(KD):
                            ins = nc.tensor.transpose(ps[:, tt, k * P:(k + 1) * P],
                                                      xin[:, tt, k * P:(k + 1) * P], ident[:])
                        ins.then_inc(t1.sem, 1)
                if 0 <= n < NCC:
                    proj(n)
                if n == 0:
                    for tt in range(TT):
                        for k in range(KD):
                            t = slice(tt * P, (tt + 1) * P)
                            ins = mm3(ps[:, 4, tt * HEADS:(tt + 1) * HEADS], xnh[:, k, t], xnl[:, k, t],
                                      win_h[:, k, DTC:], win_l[:, k, DTC:], k, k == KD - 1)
                    ins.then_inc(dtp.sem, 1)
                if n == 4:
                    back(0)
                if n == 4:
                    pe.wait_ge(dar.sem, dar.at(i, 1))
                    nc.tensor.matmul(ps[:, 4, 0:TT * HEADS], incl[:], dflat, start=True, stop=True)
                    nc.tensor.matmul(ps[:, 4, TT * HEADS:], later[:], dah[:].rearrange("p t h -> p (t h)"),
                                     start=True, stop=False)
                    nc.tensor.matmul(ps[:, 4, TT * HEADS:], later[:], dal[:].rearrange("p t h -> p (t h)"),
                                     start=False, stop=True).then_inc(cum.sem, 1)
                if n == 6:
                    pe.wait_ge(ecd.sem, ecd.at(i, 1))
                    nc.tensor.matmul(ps[:, 4, 0:TT * HEADS], in_a[:], dflat, start=True, stop=True)
                    nc.tensor.matmul(ps[:, 4, TT * HEADS:], in_b[:], dflat, start=True,
                                     stop=True).then_inc(cum.sem, 1)
                if n == 8:
                    pe.wait_ge(act_x.sem, act_x.at(i, 2))
                    pe.wait_ge(ecd.sem, ecd.at(i, 2))
                    for tt in range(TT):
                        for c in range(2):
                            t = slice(tt * P + c * CHUNK, tt * P + (c + 1) * CHUNK)
                            ins = nc.tensor.matmul(ps[c * CHUNK:(c + 1) * CHUNK, 4, tt * CHUNK:(tt + 1) * CHUNK],
                                                   bT[:, t], cT[:, t], start=True, stop=True)
                    ins.then_inc(gp.sem, 1)
                if 6 <= n <= NX + 5:
                    back(n - 5)

            def scan(i):
                def decay(u):
                    pe.wait_ge(bhi.sem, bhi.at(i, u + 1))
                    pe.wait_ge(blo.sem, blo.at(i, u + 1))
                    if u >= 2:
                        pe.wait_ge(ex.sem, ex.at(i, u - 1))
                    nc.tensor.matmul(ps[:, u % 2, :], later[:], bh[:, u % 2].rearrange("p t h -> p (t h)"),
                                     start=True, stop=False)
                    nc.tensor.matmul(ps[:, u % 2, :], later[:], bl[:, u % 2].rearrange("p t h -> p (t h)"),
                                     start=False, stop=True).then_inc(seg.sem, 1)

                def within(u):
                    tt, q = divmod(u, UPT)
                    bank, c0 = 2 + q // 4, q % 4 * P
                    if q % 4 == 0 and tt:
                        pe.wait_ge(yc.sem, yc.at(i, 2 * tt - 1 + q // 4))
                    nc.tensor.matmul(ps[:, bank, c0:c0 + P], xall[:, q, tt * P:(tt + 1) * P], ident[:],
                                     start=True, stop=False)
                    if q == 0:
                        pe.wait_ge(xlr.sem, xlr.at(i, tt + 1))
                    pe.wait_ge(mr.sem, mr.at(i, u + 1))
                    mh, ml = (mu[:, s, u % 2].rearrange("p c t h -> p (c t) h") for s in range(2))
                    for h in range(UH):
                        dst = ps[:, bank, c0 + h * HD:c0 + (h + 1) * HD]
                        xh, xl = (xsp[:, tt % 2, s, (q * UH + h) * HD:(q * UH + h + 1) * HD] for s in range(2))
                        nc.tensor.matmul(dst, mh[:, :, h], xh, start=False, stop=False)
                        nc.tensor.matmul(dst, mh[:, :, h], xl, start=False, stop=False)
                        ins = nc.tensor.matmul(dst, ml[:, :, h], xh, start=False, stop=(h == UH - 1))
                    ins.then_inc(yd.sem, 1)

                def gate(g, k):
                    t = slice(g // 2 * P, (g // 2 + 1) * P)
                    c = slice((g % 2) * 512, (g % 2 + 1) * 512)
                    if g and k == 0:
                        pe.wait_ge(gate_e.sem, gate_e.at(i, g))
                    ins = mm3(ps[:, 5, :], xnh[:, k, t], xnl[:, k, t], win_h[:, k, c], win_l[:, k, c],
                              k, k == KD - 1)
                    if k == KD - 1:
                        ins.then_inc(gate_p.sem, 1)

                def from_state(tt, c):
                    r = slice(c * CHUNK, (c + 1) * CHUNK)
                    t = slice(tt * P + c * CHUNK, tt * P + (c + 1) * CHUNK)
                    if tt == 0 and c == 0:
                        pe.wait_ge(s0.sem, s0.at(i, 1))
                    else:
                        pe.wait_ge(su.sem, su.at(i, 4 * tt + 2 * c))
                    if tt and c == 0:
                        pe.wait_ge(ysc.sem, ysc.at(i, tt))
                    for a in range(2):
                        ins = nc.tensor.matmul(ps[r, 6 + a, :], cT[:, t], S[:, a * 512:(a + 1) * 512],
                                               start=True, stop=True)
                    ins.then_inc(yo.sem, 1)

                def to_state(tt, c, a):
                    r = slice(c * CHUNK, (c + 1) * CHUNK)
                    n = 4 * tt + 2 * c + a
                    pe.wait_ge(xddr.sem, xddr.at(i, tt + 1))
                    if n:
                        pe.wait_ge(su.sem, su.at(i, n))
                    nc.tensor.matmul(ps[:, 4, :], btok[r, tt, :], xdd[r, a * 512:(a + 1) * 512],
                                     start=True, stop=True).then_inc(sn.sem, 1)

                pe.wait_ge(xtd.sem, xtd.at(i, NX))
                pe.wait_ge(xta.sem, xta.at(i, NX + 1))
                pe.wait_ge(raw.sem, raw.at(i, NCC))
                pe.wait_ge(gmr.sem, gmr.at(i, 1))
                pe.wait_ge(t3l.sem, t3l.before(i, TT))
                pe.wait_ge(lgi.sem, lgi.before(i, 1))
                for u in range(3):
                    decay(u)
                for u in range(U):
                    tt, q = divmod(u, UPT)
                    if q in (0, 3):
                        from_state(tt, q // 3)
                    within(u)
                    if u + 3 < U:
                        decay(u + 3)
                    if q in (0, 1, 3, 4):
                        to_state(tt, q // 3, q % 3)
                    gate(u // 4, u % 4)

            def put_out(i, j):
                if j % 1:
                    return
                lin = 1 if j >= 10 else 0
                n = 2 if lin else KD

                def out_proj(tt):
                    pe.wait_ge(hl.sem, hl.at(i, 2 * tt + 2))
                    if tt:
                        pe.wait_ge(x1r.sem, x1r.at(i, tt))
                    for k in range(NX):
                        ins = mm3(ps[:, 7, :], hth[:, tt % 2, k, :], htl[:, tt % 2, k, :],
                                  wout_h[:, k, :], wout_l[:, k, :], k, k == NX - 1)
                    ins.then_inc(op.sem, 1)

                def spread(bank, v, m):
                    for k in range(m):
                        ins = nc.tensor.matmul(ps[:, bank, k * P:(k + 1) * P],
                                               v[:, k:k + 1].to_broadcast([P, P]), ident[:],
                                               start=True, stop=True)
                    return ins

                def logits(tt):
                    pe.wait_ge(t3f.sem, t3f.at(i, tt + 1))
                    for k in range(KD):
                        ins = nc.tensor.matmul(ps[:, 7, tt * E:(tt + 1) * E], zTf[:, k, :], rw[:, k, :],
                                               start=(k == 0), stop=(k == KD - 1))
                    ins.then_inc(lgp.sem, 1)

                if j < TT:
                    if j == 0:
                        pe.wait_ge(su.sem, su.at(i, 4 * TT))
                        pe.wait_ge(hgr.sem, hgr.at(i, TT))
                    for a in range(2):
                        g = 2 * j + a
                        if g >= 2:
                            pe.wait_ge(hl.sem, hl.at(i, g - 1))
                        for k in range(4):
                            c = (a * 4 + k) * P
                            ins = nc.tensor.transpose(ps[:, 5 + a, k * P:(k + 1) * P], gs[:, j, c:c + P], ident[:])
                        ins.then_inc(ht.sem, 1)
                    if j:
                        out_proj(j - 1)
                elif j == 4:
                    out_proj(TT - 1)
                elif j in (5, 10):
                    if lin:
                        pe.wait_ge(ar.sem, ar.at(i, TT))
                    else:
                        pe.wait_ge(znr.sem, znr.at(i, TT))
                    src = av if lin else zn
                    for k in range(n):
                        g = lin * KD + k
                        if k >= 2:
                            pe.wait_ge(t2r.sem, t2r.at(i, g - 1))
                        for tt in range(TT):
                            ins = nc.tensor.transpose(ps[:, 5 + g % 2, tt * P:(tt + 1) * P],
                                                      src[:, tt, k * P:(k + 1) * P], ident[:])
                        ins.then_inc(t2.sem, 1)
                elif j in (6, 11):
                    pe.wait_ge(sbr.sem, sbr.at(i, lin + 1))
                    spread(5, sm, n)
                    spread(6, sr, n).then_inc(sbp.sem, 1)
                elif j in (7, 12):
                    pe.wait_ge(wsr.sem, wsr.at(i, lin + 1))
                    spread(7, wsc, TT).then_inc(wsp.sem, 1)
                elif j in (8, 13):
                    for g in range(2 * TT):
                        pe.wait_ge(qr.sem, qr.at(i, 2 * TT * lin + g + 1))
                        if g >= 2:
                            pe.wait_ge(qc.sem, qc.at(i, 2 * TT * lin + g - 1))
                        q = qx if g % 2 == 0 else qw
                        for k in range(n):
                            ins = nc.tensor.transpose(ps[:, 5 + g % 2, k * 64:(k + 1) * 64].bitcast(BF16),
                                                      q[:, g // 2, k * P:(k + 1) * P], identb[:])
                        ins.then_inc(qt.sem, 1)
                elif j in (9, 14):
                    pe.wait_ge(qc.sem, qc.at(i, 2 * TT * (lin + 1)))
                    pe.wait_ge(wsb.sem, wsb.at(i, lin + 1))
                    for tt in range(TT):
                        if tt >= 2:
                            if lin:
                                pe.wait_ge(x2r.sem, x2r.at(i, tt - 1))
                            else:
                                pe.wait_ge(hr.sem, hr.at(i, tt - 1))
                        for k in range(n):
                            ins = nc.tensor.matmul(ps[:, 7 if tt % 2 == 0 else 5, :], qxT[:, k, tt * P:(tt + 1) * P],
                                                   qwT[:, k, :], start=(k == 0), stop=(k == n - 1))
                        ins.then_inc(qm.sem, 1)
                elif j == 16:
                    for tt in range(TT):
                        pe.wait_ge(znr.sem, znr.at(i, TT + tt + 1))
                        if tt >= 2:
                            pe.wait_ge(t3l.sem, t3l.at(i, tt - 1))
                        for k in range(KD):
                            ins = nc.tensor.transpose(ps[:, 5 + tt % 2, k * P:(k + 1) * P],
                                                      zn[:, tt, k * P:(k + 1) * P], ident[:])
                        ins.then_inc(t3.sem, 1)
                        if tt:
                            logits(tt - 1)
                    logits(TT - 1)

            rows(pe, take_x, scan, put_out, split_in, split_out)


def expert_pass(nc, gateT, upT, downT, x2_dram, zh_dram, zl_dram, wt_dram, out):
    STEPS = PAIR * B
    with ExitStack() as ctx:
        def sb(name, shape, dt=F32):
            return ctx.enter_context(nc.sbuf_tensor(name, shape, dt))

        def sem(name):
            return ctx.enter_context(nc.semaphore(name))

        counts = []

        def count(name, per):
            counts.append(Count(ctx, nc, name, per))
            return counts[-1]

        pp = ctx.enter_context(nc.psum_tensor("pp", [P, 8, 512], F32))
        acc = sb("acc", [P, NT, D])
        zh = sb("zh", [P, B, TT, KD, P], BF16)
        zl = sb("zl", [P, B, TT, KD, P], BF16)
        wts = sb("wts", [P, B, E, TT])
        wcur = sb("wcur", [P, 2, B, TT])
        guh = sb("guh", [P, PAIR, 2, KD, I], BF16)
        gul = sb("gul", [P, PAIR, 2, KD, I], BF16)
        dnh = sb("dnh", [P, PAIR, IC, D], BF16)
        dnl = sb("dnl", [P, PAIR, IC, D], BF16)
        stage = sb("stage", [P, 2, I])
        sgl = sb("sgl", [P, 2, L])
        hf = sb("hf", [P, 2, L])
        hhi = sb("hhi", [P, IC + 1, L], BF16)
        hlo = sb("hlo", [P, IC + 1, L], BF16)

        s_first = [sem(f"s_first{n}") for n in range(PIECES)]
        s_z = [sem(f"s_z{b}") for b in range(B)]
        s_x2 = [sem(f"s_x2_{b}") for b in range(B)]
        s_wt = sem("s_wt")
        s_out = sem("s_out")
        s_pass = sem("s_pass2")
        wl = [count(f"wl{s}", 16 * PAIR * PIECES // 2) for s in range(2)]
        wh = count("wh", PAIR * PIECES)
        wo = count("wo", PAIR * PIECES)
        gu = count("gu", STEPS * IC)
        sgr = count("sg_ready", STEPS * IC)
        hm = count("hm", STEPS * IC)
        hh = count("h_high", STEPS * IC)
        hl = count("h_low", STEPS * IC)
        dn = count("dn", STEPS * TT)
        ad = count("ad", STEPS * TT)
        wc = count("wc", PAIR)

        block = ctx.enter_context(nc.Block())

        def piece(expert, n):
            if n < 2 * KD:
                return (gateT if n < KD else upT)[expert, (n % KD) * P:(n % KD + 1) * P, :]
            k = 2 * (n - 2 * KD)
            return downT[expert, k * P:(k + 2) * P, :].rearrange("(k p) n -> p k n", p=P)

        def place(hi, par, n):
            if n < 2 * KD:
                return (guh if hi else gul)[:, par, n // KD, n % KD, :]
            k = 2 * (n - 2 * KD)
            return (dnh if hi else dnl)[:, par, k:k + 2, :].rearrange("p k n -> p (k n)")

        def staged(n):
            return stage[:, n % 2, :] if n < 2 * KD else stage[:, n % 2, :].rearrange("p (k n) -> p k n", k=2)

        def first(n):
            if n < 6:
                return acc[:, TT + 2 * n:TT + 2 * n + 2, :].rearrange("p a d -> p (a d)")
            if n < 8:
                return stage[:, n - 6, :]
            half = (hhi if n < 10 else hlo)[:, 4 * (n % 2):4 * (n % 2) + 4, :]
            return half.rearrange("p c t -> p (c t)").bitcast(F32)

        def slot(step, c):
            return (IC if step % 2 else 0) if c == 0 else c

        AFTER = (2, 4, 6)
        FIRST = PIECES

        @block.sync
        def _(sp):
            def load_z(b):
                sp.dma_start(zh[:, b], zh_dram[b].rearrange("t p k c -> p t k c")).then_inc(s_z[b], 16)
                sp.dma_start(zl[:, b], zl_dram[b].rearrange("t p k c -> p t k c")).then_inc(s_z[b], 16)

            def load_x2(b):
                sp.dma_start(acc[:, b * TT:(b + 1) * TT, :], x2_dram[b]).then_inc(s_x2[b], 16)

            for n in range(PIECES):
                sp.dma_start(first(n) if n < 2 * KD else first(n).rearrange("p (k n) -> p k n", k=2),
                             piece(0, n)).then_inc(s_first[n], 16)
                if n == 2 * KD - 1:
                    load_z(0)
            for b in range(B):
                sp.dma_start(wts[:, b].rearrange("p e t -> p (e t)"), wt_dram[b]).then_inc(s_wt, 16)
            load_z(1)
            load_x2(0)
            load_z(2)
            load_z(3)
            sp.wait_ge(wo.sem, wo.per)
            for b in range(1, B):
                load_x2(b)
            with sp.Fori(0, E // PAIR) as i:
                for n in range(PAIR * PIECES):
                    sp.wait_ge(wo.sem, wo.at(i, n - 1))
                    sp.sem_inc(s_pass, 1)
                    nxt = i * PAIR + 1 if n < PIECES else (i * PAIR + 2) % E
                    sp.dma_start(staged(n % PIECES), piece(nxt, n % PIECES)).then_inc(wl[n % 2].sem, 16)
            for b in range(B):
                for tt in range(TT):
                    if tt == 0 or b == B - 1:
                        last = tt if b == B - 1 else TT - 1
                        sp.wait_ge(ad.sem, ad.per * (E // PAIR + 1) - NT + b * TT + last + 1)
                        t = slice(tt, tt + 1) if b == B - 1 else slice(0, TT)
                        sp.dma_start(out[b, :, t, :], acc[:, b * TT + t.start:b * TT + t.stop, :]).then_inc(s_out, 16)
            for s in range(2):
                sp.wait_ge(wl[s].sem, wl[s].per * (E // PAIR + 1))
            sp.wait_ge(s_out, 16 * (B - 1 + TT))

        @block.gpsimd
        def _(pool):
            for c in counts:
                less = {id(wh): FIRST, id(wo): FIRST}
                pool.sem_inc(c.sem, c.per - less.get(id(c), 0))

        @block.scalar
        def _(act):
            for n in range(PIECES):
                act.wait_ge(s_first[n], 16)
                nc.scalar.activation(place(True, 0, n), first(n), ACT.Copy).then_inc(wh.sem, 1)
            with act.Fori(0, E // PAIR) as i:
                def high(step, c):
                    n = step * IC + c
                    act.wait_ge(hm.sem, hm.at(i, n + 1))
                    if c:
                        act.wait_ge(dn.sem, dn.at(i, TT * step))
                    nc.scalar.activation(hhi[:, slot(step, c), :], hf[:, n % 2, :], ACT.Copy).then_inc(hh.sem, 1)

                for step in range(STEPS):
                    par, tb = divmod(step, B)
                    for c in range(IC):
                        n = step * IC + c
                        act.wait_ge(gu.sem, gu.at(i, n + 1))
                        nc.scalar.activation(sgl[:, n % 2, :], pp[:, n % 2, :], ACT.Silu).then_inc(sgr.sem, 1)
                        if n and c:
                            high(step, c - 1)
                        if c == IC - 1:
                            high(step, c)
                        if c in AFTER:
                            m = par * PIECES + tb * 3 + AFTER.index(c)
                            act.wait_ge(wl[m % 2].sem, wl[m % 2].at(i, 16 * (m // 2 + 1)))
                            if tb == 0:
                                act.wait_ge(dn.sem, dn.at(i, TT * step))
                            nc.scalar.activation(place(True, 1 - par, m % PIECES), stage[:, m % 2, :],
                                                 ACT.Copy).then_inc(wh.sem, 1)

        @block.vector
        def _(dve):
            for n in range(PIECES):
                dve.wait_ge(wh.sem, wh.per - FIRST + n + 1)
                nc.vector.tensor_tensor(place(False, 0, n), first(n), place(True, 0, n),
                                        ALU.subtract).then_inc(wo.sem, 1)
            dve.wait_ge(s_wt, 16 * B)
            with dve.Fori(0, E // PAIR) as i:
                dve.wait_ge(ad.sem, ad.at(i, 0))
                for par in range(PAIR):
                    nc.vector.tensor_copy(wcur[:, par], wts[:, :, bass.ds(i * PAIR + par, 1), :].rearrange(
                        "p b e t -> p b (e t)")).then_inc(wc.sem, 1)

                def low(step, c):
                    n = step * IC + c
                    dve.wait_ge(hh.sem, hh.at(i, n + 1))
                    nc.vector.tensor_tensor(hlo[:, slot(step, c), :], hf[:, n % 2, :], hhi[:, slot(step, c), :],
                                            ALU.subtract).then_inc(hl.sem, 1)

                def add(step):
                    par, tb = divmod(step, B)
                    dve.wait_ge(s_x2[tb], 16)
                    for tt in range(TT):
                        dve.wait_ge(dn.sem, dn.at(i, step * TT + tt + 1))
                        a = acc[:, tb * TT + tt, :]
                        nc.vector.scalar_tensor_tensor(out=a, in0=pp[:, 4 + tt, :], scalar=wcur[:, par, tb, tt:tt + 1],
                                                       in1=a, op0=ALU.mult, op1=ALU.add).then_inc(ad.sem, 1)

                dve.wait_ge(wc.sem, wc.at(i, PAIR))
                for step in range(STEPS):
                    par, tb = divmod(step, B)
                    for c in range(IC):
                        n = step * IC + c
                        dve.wait_ge(sgr.sem, sgr.at(i, n + 1))
                        if n >= 2:
                            dve.wait_ge(hl.sem, hl.at(i, n - 1))
                        nc.vector.tensor_tensor(hf[:, n % 2, :], sgl[:, n % 2, :], pp[:, 2 + n % 2, :],
                                                ALU.mult).then_inc(hm.sem, 1)
                        if n and c:
                            low(step, c - 1)
                        if c == IC - 1:
                            low(step, c)
                        if c == 0 and step:
                            add(step - 1)
                        if c in AFTER:
                            m = par * PIECES + tb * 3 + AFTER.index(c)
                            dve.wait_ge(wh.sem, wh.at(i, m + 1))
                            nc.vector.tensor_tensor(place(False, 1 - par, m % PIECES), stage[:, m % 2, :],
                                                    place(True, 1 - par, m % PIECES),
                                                    ALU.subtract).then_inc(wo.sem, 1)
                add(STEPS - 1)

        @block.tensor
        def _(pe):
            with pe.Fori(0, E // PAIR) as i:
                def gate_up(step, c):
                    par, tb = divmod(step, B)
                    n = step * IC + c
                    if c == 0:
                        pe.wait_ge(s_z[tb], 32)
                    if c == 0 and tb == 0:
                        pe.wait_ge(wo.sem, wo.at(i, PIECES * par - (PIECES - 2 * KD)))
                    pe.wait_ge(hm.sem, hm.at(i, n - 1))
                    for j in range(2):
                        for k in range(KD):
                            w = slice(c * P, (c + 1) * P)
                            dst = pp[:, 2 * j + n % 2, :]
                            nc.tensor.matmul(dst, guh[:, par, j, k, w], zh[:, tb, :, k, :], start=(k == 0), stop=False)
                            nc.tensor.matmul(dst, guh[:, par, j, k, w], zl[:, tb, :, k, :], start=False, stop=False)
                            ins = nc.tensor.matmul(dst, gul[:, par, j, k, w], zh[:, tb, :, k, :], start=False,
                                                   stop=(k == KD - 1))
                    ins.then_inc(gu.sem, 1)

                def down(step):
                    par, tb = divmod(step, B)
                    pe.wait_ge(hl.sem, hl.at(i, (step + 1) * IC))
                    if tb == 0:
                        pe.wait_ge(wo.sem, wo.at(i, PIECES * par))
                    for tt in range(TT):
                        pe.wait_ge(ad.sem, ad.at(i, step * TT + tt + 1 - TT))
                        t = slice(tt * P, (tt + 1) * P)
                        for c in range(IC):
                            s = slot(step, c)
                            dst = pp[:, 4 + tt, :]
                            nc.tensor.matmul(dst, hhi[:, s, t], dnh[:, par, c, :], start=(c == 0), stop=False)
                            nc.tensor.matmul(dst, hhi[:, s, t], dnl[:, par, c, :], start=False, stop=False)
                            ins = nc.tensor.matmul(dst, hlo[:, s, t], dnh[:, par, c, :], start=False,
                                                   stop=(c == IC - 1))
                        ins.then_inc(dn.sem, 1)

                gate_up(0, 0)
                for step in range(STEPS):
                    for c in range(1, IC):
                        gate_up(step, c)
                    if step + 1 < STEPS:
                        gate_up(step + 1, 0)
                    down(step)


def kernel(**inputs):
    import numpy as np
    import concourse.bacc as bacc
    from concourse.bass_utils import run_bass_kernel_spmd

    def tiles(a):
        b, r, n = a.shape
        return a.reshape(b, r // P, P, n).transpose(0, 2, 1, 3)

    def rows(v):
        return v.reshape(1, -1)

    f = inputs["fside_BxS2xS2_0"]
    c = inputs["ctx_1024"]
    a = {k.replace("L0_attn_", "").replace("L0_ffn_", ""): np.asarray(v) for k, v in inputs.items()}
    f, c = np.asarray(f), np.asarray(c)
    arrays = {
        "x": tiles(a["x"]),
        "guw": tiles(f),
        "guwT": tiles(f.transpose(0, 2, 1)),
        "dnw": tiles(c),
        "dnwT": tiles(c.transpose(0, 2, 1)),
        "winT": a["in_proj_w"].T,
        "conv_w": a["conv_w"].reshape(NCC, P, KC).transpose(1, 0, 2),
        "conv_b": a["conv_b"].reshape(NCC, P).T,
        "dt_bias": rows(a["dt_bias"]),
        "a_log": rows(a["A_log"]),
        "d_skip": np.repeat(a["D"], HD).reshape(NX, P).T,
        "norm_w": a["norm_w"].reshape(NX, P).T,
        "woutT": a["out_proj_w"].T,
        "rwT": a["router_w"].T.reshape(KD, P, E).transpose(1, 0, 2),
        "gateT": a["gate_w"].transpose(0, 2, 1),
        "upT": a["up_w"].transpose(0, 2, 1),
        "downT": a["down_w"].transpose(0, 2, 1),
    }
    arrays = {f"in_{k}": np.ascontiguousarray(v) for k, v in arrays.items()}
    nc = bacc.Bacc("TRN2", target_bir_lowering=False, num_devices=1)
    args = [nc.dram_tensor(k, v.shape, mybir.dt.from_np(v.dtype), kind="ExternalInput").ap()
            for k, v in arrays.items()]
    out = nc.dram_tensor("out", [B, P, TT, D], F32, kind="ExternalOutput").ap()
    decoder_layer(nc, *args, out)
    r = run_bass_kernel_spmd(nc, [arrays], core_ids=[0])
    return r.results[0]["out"].reshape(B, P, TT, D).transpose(0, 2, 1, 3).reshape(B, L, D)
```
